# Optimizing a Trainium2 kernel written in Bass

```python
import numpy as np
import jax
import jax.numpy as jnp

def _softmax(x, axis=-1):
    return jax.nn.softmax(x, axis=axis)

def _gelu(x):
    return jax.nn.gelu(x, approximate=True)

def _silu(x):
    return jax.nn.silu(x)

def _sigmoid(x):
    return jax.nn.sigmoid(x)

def _layernorm(x, axis=-1, eps=1e-05):
    m = jnp.mean(x, axis=axis, keepdims=True)
    v = jnp.var(x, axis=axis, keepdims=True)
    return (x - m) / jnp.sqrt(v + eps)

def _scatter_add(tgt, idx, src, axis=0):
    return tgt.at[idx].add(src)

def _segment_sum(src, seg, n):
    return jax.ops.segment_sum(src, seg, n)
kernel_name = 'mk_recurrent_d2_jaxref_r8_87fb24'

def setup_inputs(seed: int=0):
    np.random.seed(seed)
    _w = jnp.asarray

    def _L0_attn_setup():
        import jax, jax.numpy as jnp
        import numpy as np
        import math
        D = 256
        H = 16
        KV = 4
        DH = D // H
        REP = H // KV
        LAMBDA_INIT = 0.8 - 0.6 * math.exp(-0.3 * 0)
        ROPE_BASE = 10000.0
        EPS = 1e-05

        def _rope(x, cos, sin):
            x1, x2 = (x[..., ::2], x[..., 1::2])
            c = cos[None, None]
            s = sin[None, None]
            o1 = x1 * c - x2 * s
            o2 = x1 * s + x2 * c
            return jnp.stack([o1, o2], axis=-1).reshape(x.shape)

        def _forward(x, Wq, Wk, Wv, Wo, lambda_q1, lambda_k1, lambda_q2, lambda_k2, gn_w, gn_b):
            B, T, _ = x.shape
            q = (x @ Wq).reshape(B, T, H, 2 * DH).transpose(0, 2, 1, 3)
            k = (x @ Wk).reshape(B, T, KV, 2 * DH).transpose(0, 2, 1, 3)
            v = (x @ Wv).reshape(B, T, KV, 2 * DH).transpose(0, 2, 1, 3)
            q1, q2 = (q[..., :DH], q[..., DH:])
            k1, k2 = (k[..., :DH], k[..., DH:])
            inv = 1.0 / ROPE_BASE ** (jnp.arange(0, DH, 2, dtype=jnp.float32) / DH)
            freqs = jnp.arange(T, dtype=jnp.float32)[:, None] * inv[None, :]
            cos, sin = (jnp.cos(freqs), jnp.sin(freqs))
            q1, q2 = (_rope(q1, cos, sin), _rope(q2, cos, sin))
            k1, k2 = (_rope(k1, cos, sin), _rope(k2, cos, sin))
            k1 = jnp.repeat(k1, REP, axis=1)
            k2 = jnp.repeat(k2, REP, axis=1)
            v = jnp.repeat(v, REP, axis=1)
            mask = jnp.triu(jnp.full((T, T), -jnp.inf, dtype=x.dtype), k=1)[None, None]
            scale = 1.0 / math.sqrt(DH)
            s1 = jnp.einsum('bhtd,bhsd->bhts', q1, k1) * scale + mask
            s2 = jnp.einsum('bhtd,bhsd->bhts', q2, k2) * scale + mask
            a1 = jax.nn.softmax(s1, axis=-1)
            a2 = jax.nn.softmax(s2, axis=-1)
            lam = jnp.exp(jnp.sum(lambda_q1 * lambda_k1)) - jnp.exp(jnp.sum(lambda_q2 * lambda_k2)) + LAMBDA_INIT
            diff = a1 - lam * a2
            out = jnp.einsum('bhts,bhsd->bhtd', diff, v)
            out = out.transpose(0, 2, 1, 3)
            mean = jnp.mean(out, axis=(1, 3), keepdims=True)
            var = jnp.var(out, axis=(1, 3), keepdims=True)
            out = (out - mean) * jax.lax.rsqrt(var + EPS)
            out = out * gn_w.reshape(1, 1, H, 2 * DH) + gn_b.reshape(1, 1, H, 2 * DH)
            out = out.reshape(B, T, 2 * H * DH) * (1.0 - LAMBDA_INIT)
            return out @ Wo
        key = jax.random.key(seed)
        ks = jax.random.split(key, 12)
        B, T = (1, 256)
        s = 0.02
        return {'x': jax.random.normal(ks[0], (B, T, D), jnp.float32), 'Wq': jax.random.normal(ks[1], (D, 2 * H * DH), jnp.float32) * s, 'Wk': jax.random.normal(ks[2], (D, 2 * KV * DH), jnp.float32) * s, 'Wv': jax.random.normal(ks[3], (D, 2 * KV * DH), jnp.float32) * s, 'Wo': jax.random.normal(ks[4], (2 * H * DH, D), jnp.float32) * s, 'lambda_q1': jax.random.normal(ks[5], (DH,), jnp.float32) * 0.1, 'lambda_k1': jax.random.normal(ks[6], (DH,), jnp.float32) * 0.1, 'lambda_q2': jax.random.normal(ks[7], (DH,), jnp.float32) * 0.1, 'lambda_k2': jax.random.normal(ks[8], (DH,), jnp.float32) * 0.1, 'gn_w': jnp.ones((2 * H * DH,), jnp.float32), 'gn_b': jnp.zeros((2 * H * DH,), jnp.float32)}
    _L0_attn_in = _L0_attn_setup()

    def _L0_ffn_setup():
        import jax, jax.numpy as jnp
        import numpy as np
        DIM = 256
        INTER = 176
        N_EXPERTS = 16
        TOP_K = 2
        N_SHARED = 2
        SHARED_INTER = N_SHARED * INTER

        def _swiglu(t, wa, wb, wo):
            h = jax.nn.silu(t @ wa.T) * (t @ wb.T)
            return h @ wo.T
        key = jax.random.key(seed)
        ks = jax.random.split(key, 9)
        s = 0.02
        return {'x': jax.random.normal(ks[0], (4, 256, DIM), dtype=jnp.float32), 'gate_w': jax.random.normal(ks[1], (N_EXPERTS, DIM), dtype=jnp.float32) * s, 'w1': jax.random.normal(ks[2], (N_EXPERTS, INTER, DIM), dtype=jnp.float32) * s, 'w2': jax.random.normal(ks[3], (N_EXPERTS, DIM, INTER), dtype=jnp.float32) * s, 'w3': jax.random.normal(ks[4], (N_EXPERTS, INTER, DIM), dtype=jnp.float32) * s, 'sw1': jax.random.normal(ks[5], (SHARED_INTER, DIM), dtype=jnp.float32) * s, 'sw2': jax.random.normal(ks[6], (DIM, SHARED_INTER), dtype=jnp.float32) * s, 'sw3': jax.random.normal(ks[7], (SHARED_INTER, DIM), dtype=jnp.float32) * s}
    _L0_ffn_in = _L0_ffn_setup()

    def _L1_attn_setup():
        import jax, jax.numpy as jnp
        import numpy as np
        B, T, C, H = (2, 256, 256, 16)
        HD = C // H
        BASE = 10000.0

        def _rope_tables(seq_len, d):
            p = jnp.arange(d // 2, dtype=jnp.float32)
            theta = jnp.power(BASE, -2.0 ** p / d)
            pos = jnp.arange(1, seq_len + 1, dtype=jnp.float32)[:, None]
            c = pos * theta
            ang = jnp.concatenate([c, c], axis=-1)
            return (jnp.cos(ang), jnp.sin(ang))

        def _rope(x):
            d = x.shape[-1]
            cos, sin = _rope_tables(x.shape[-2], d)
            half = d // 2
            x_rot = jnp.concatenate([-x[..., half:], x[..., :half]], axis=-1)
            return x * cos + x_rot * sin
        key = jax.random.key(seed)
        k1, k2, k3 = jax.random.split(key, 3)
        x = jax.random.normal(k1, (B, T, C), dtype=jnp.float32)
        Wqkv = jax.random.normal(k2, (3 * C, C), dtype=jnp.float32) * 0.02
        bqkv = jnp.zeros((3 * C,), dtype=jnp.float32)
        Wo = jax.random.normal(k3, (C, C), dtype=jnp.float32) * 0.02
        bo = jnp.zeros((C,), dtype=jnp.float32)
        return {'x': x, 'Wqkv': Wqkv, 'bqkv': bqkv, 'Wo': Wo, 'bo': bo}
    _L1_attn_in = _L1_attn_setup()

    def _L1_ffn_setup():
        import math
        import jax, jax.numpy as jnp
        import numpy as np
        CAPACITY_FACTOR = 1.25
        MIN_CAPACITY = 4

        def _capacity(num_tokens: int, num_experts: int) -> int:
            cap = math.floor(CAPACITY_FACTOR * num_tokens / num_experts)
            cap += cap % 2
            return max(cap, MIN_CAPACITY)
        key = jax.random.key(seed)
        k1, k2, k3, k4 = jax.random.split(key, 4)
        B, S, H, I, E = (2, 512, 256, 256, 8)
        inputs = jax.random.normal(k1, (B, S, H), dtype=jnp.float32)
        gate_weight = jax.random.normal(k2, (E, H), dtype=jnp.float32) * math.sqrt(0.1 / H)
        w1 = jax.random.normal(k3, (E, H, I), dtype=jnp.float32) * 0.02
        w2 = jax.random.normal(k4, (E, I, H), dtype=jnp.float32) * 0.02
        return {'inputs': inputs, 'gate_weight': gate_weight, 'w1': w1, 'w2': w2}
    _L1_ffn_in = _L1_ffn_setup()
    _d = {'L0_attn_x': _L0_attn_in['x'], 'L0_attn_Wq': _L0_attn_in['Wq'], 'L0_attn_Wk': _L0_attn_in['Wk'], 'L0_attn_Wv': _L0_attn_in['Wv'], 'L0_attn_Wo': _L0_attn_in['Wo'], 'L0_attn_lambda_q1': _L0_attn_in['lambda_q1'], 'L0_attn_lambda_k1': _L0_attn_in['lambda_k1'], 'L0_attn_lambda_q2': _L0_attn_in['lambda_q2'], 'L0_attn_lambda_k2': _L0_attn_in['lambda_k2'], 'L0_attn_gn_w': _L0_attn_in['gn_w'], 'L0_attn_gn_b': _L0_attn_in['gn_b'], 'L0_ffn_gate_w': _L0_ffn_in['gate_w'], 'L0_ffn_w1': _L0_ffn_in['w1'], 'L0_ffn_w2': _L0_ffn_in['w2'], 'L0_ffn_w3': _L0_ffn_in['w3'], 'L0_ffn_sw1': _L0_ffn_in['sw1'], 'L0_ffn_sw2': _L0_ffn_in['sw2'], 'L0_ffn_sw3': _L0_ffn_in['sw3'], 'L1_attn_Wqkv': _L1_attn_in['Wqkv'], 'L1_attn_bqkv': _L1_attn_in['bqkv'], 'L1_attn_Wo': _L1_attn_in['Wo'], 'L1_attn_bo': _L1_attn_in['bo'], 'L1_ffn_gate_weight': _L1_ffn_in['gate_weight'], 'L1_ffn_w1': _L1_ffn_in['w1'], 'L1_ffn_w2': _L1_ffn_in['w2']}
    _x0 = _d['L0_attn_x']
    _d['L0_attn_x'] = jax.random.normal(jax.random.fold_in(jax.random.key(seed), 1), (4, 256, 256), dtype=_x0.dtype)
    del _x0
    return _d

def reference(L0_attn_x, L0_attn_Wq, L0_attn_Wk, L0_attn_Wv, L0_attn_Wo, L0_attn_lambda_q1, L0_attn_lambda_k1, L0_attn_lambda_q2, L0_attn_lambda_k2, L0_attn_gn_w, L0_attn_gn_b, L0_ffn_gate_w, L0_ffn_w1, L0_ffn_w2, L0_ffn_w3, L0_ffn_sw1, L0_ffn_sw2, L0_ffn_sw3, L1_attn_Wqkv, L1_attn_bqkv, L1_attn_Wo, L1_attn_bo, L1_ffn_gate_weight, L1_ffn_w1, L1_ffn_w2):

    def _L0_attn_ref(x, Wq, Wk, Wv, Wo, lambda_q1, lambda_k1, lambda_q2, lambda_k2, gn_w, gn_b):
        import jax, jax.numpy as jnp
        import numpy as np
        import math
        D = 256
        H = 16
        KV = 4
        DH = D // H
        REP = H // KV
        LAMBDA_INIT = 0.8 - 0.6 * math.exp(-0.3 * 0)
        ROPE_BASE = 10000.0
        EPS = 1e-05

        def _rope(x, cos, sin):
            x1, x2 = (x[..., ::2], x[..., 1::2])
            c = cos[None, None]
            s = sin[None, None]
            o1 = x1 * c - x2 * s
            o2 = x1 * s + x2 * c
            return jnp.stack([o1, o2], axis=-1).reshape(x.shape)

        def _forward(x, Wq, Wk, Wv, Wo, lambda_q1, lambda_k1, lambda_q2, lambda_k2, gn_w, gn_b):
            B, T, _ = x.shape
            q = (x @ Wq).reshape(B, T, H, 2 * DH).transpose(0, 2, 1, 3)
            k = (x @ Wk).reshape(B, T, KV, 2 * DH).transpose(0, 2, 1, 3)
            v = (x @ Wv).reshape(B, T, KV, 2 * DH).transpose(0, 2, 1, 3)
            q1, q2 = (q[..., :DH], q[..., DH:])
            k1, k2 = (k[..., :DH], k[..., DH:])
            inv = 1.0 / ROPE_BASE ** (jnp.arange(0, DH, 2, dtype=jnp.float32) / DH)
            freqs = jnp.arange(T, dtype=jnp.float32)[:, None] * inv[None, :]
            cos, sin = (jnp.cos(freqs), jnp.sin(freqs))
            q1, q2 = (_rope(q1, cos, sin), _rope(q2, cos, sin))
            k1, k2 = (_rope(k1, cos, sin), _rope(k2, cos, sin))
            k1 = jnp.repeat(k1, REP, axis=1)
            k2 = jnp.repeat(k2, REP, axis=1)
            v = jnp.repeat(v, REP, axis=1)
            mask = jnp.triu(jnp.full((T, T), -jnp.inf, dtype=x.dtype), k=1)[None, None]
            scale = 1.0 / math.sqrt(DH)
            s1 = jnp.einsum('bhtd,bhsd->bhts', q1, k1) * scale + mask
            s2 = jnp.einsum('bhtd,bhsd->bhts', q2, k2) * scale + mask
            a1 = jax.nn.softmax(s1, axis=-1)
            a2 = jax.nn.softmax(s2, axis=-1)
            lam = jnp.exp(jnp.sum(lambda_q1 * lambda_k1)) - jnp.exp(jnp.sum(lambda_q2 * lambda_k2)) + LAMBDA_INIT
            diff = a1 - lam * a2
            out = jnp.einsum('bhts,bhsd->bhtd', diff, v)
            out = out.transpose(0, 2, 1, 3)
            mean = jnp.mean(out, axis=(1, 3), keepdims=True)
            var = jnp.var(out, axis=(1, 3), keepdims=True)
            out = (out - mean) * jax.lax.rsqrt(var + EPS)
            out = out * gn_w.reshape(1, 1, H, 2 * DH) + gn_b.reshape(1, 1, H, 2 * DH)
            out = out.reshape(B, T, 2 * H * DH) * (1.0 - LAMBDA_INIT)
            return out @ Wo
        return _forward(x, Wq, Wk, Wv, Wo, lambda_q1, lambda_k1, lambda_q2, lambda_k2, gn_w, gn_b)

    def _L0_ffn_ref(x, gate_w, w1, w2, w3, sw1, sw2, sw3):
        import jax, jax.numpy as jnp
        import numpy as np
        DIM = 256
        INTER = 176
        N_EXPERTS = 16
        TOP_K = 2
        N_SHARED = 2
        SHARED_INTER = N_SHARED * INTER

        def _swiglu(t, wa, wb, wo):
            h = jax.nn.silu(t @ wa.T) * (t @ wb.T)
            return h @ wo.T
        shape = x.shape
        t = x.reshape(-1, DIM)
        scores = jax.nn.softmax(t @ gate_w.T, axis=-1)
        weights, indices = jax.lax.top_k(scores, TOP_K)
        y = jnp.zeros_like(t)
        for e in range(N_EXPERTS):
            w_e = jnp.sum(jnp.where(indices == e, weights, 0.0), axis=-1)
            y = y + _swiglu(t, w1[e], w3[e], w2[e]) * w_e[:, None]
        z = _swiglu(t, sw1, sw3, sw2)
        return (y + z).reshape(shape)

    def _L1_attn_ref(x, Wqkv, bqkv, Wo, bo):
        import jax, jax.numpy as jnp
        import numpy as np
        B, T, C, H = (2, 256, 256, 16)
        HD = C // H
        BASE = 10000.0

        def _rope_tables(seq_len, d):
            p = jnp.arange(d // 2, dtype=jnp.float32)
            theta = jnp.power(BASE, -2.0 ** p / d)
            pos = jnp.arange(1, seq_len + 1, dtype=jnp.float32)[:, None]
            c = pos * theta
            ang = jnp.concatenate([c, c], axis=-1)
            return (jnp.cos(ang), jnp.sin(ang))

        def _rope(x):
            d = x.shape[-1]
            cos, sin = _rope_tables(x.shape[-2], d)
            half = d // 2
            x_rot = jnp.concatenate([-x[..., half:], x[..., :half]], axis=-1)
            return x * cos + x_rot * sin
        b, t, c = x.shape
        qkv = x @ Wqkv.T + bqkv
        q, k, v = jnp.split(qkv, 3, axis=-1)

        def to_heads(z):
            return z.reshape(b, t, H, HD).transpose(0, 2, 1, 3)
        q, k, v = (to_heads(q), to_heads(k), to_heads(v))
        q = _rope(q)
        k = _rope(k)
        scale = 1.0 / jnp.sqrt(jnp.float32(HD))
        att = jnp.einsum('bhqd,bhkd->bhqk', q, k) * scale
        causal = jnp.tril(jnp.ones((t, t), dtype=bool))
        att = jnp.where(causal, att, -jnp.inf)
        att = jax.nn.softmax(att, axis=-1)
        y = jnp.einsum('bhqk,bhkd->bhqd', att, v)
        y = y.transpose(0, 2, 1, 3).reshape(b, t, c)
        y = y @ Wo.T + bo
        return y

    def _L1_ffn_ref(inputs, gate_weight, w1, w2):
        import math
        import jax, jax.numpy as jnp
        import numpy as np
        CAPACITY_FACTOR = 1.25
        MIN_CAPACITY = 4

        def _capacity(num_tokens: int, num_experts: int) -> int:
            cap = math.floor(CAPACITY_FACTOR * num_tokens / num_experts)
            cap += cap % 2
            return max(cap, MIN_CAPACITY)
        B, S, H = inputs.shape
        E = gate_weight.shape[0]
        tokens = inputs.reshape(-1, H)
        T = tokens.shape[0]
        C = _capacity(T, E)
        logits = tokens.astype(jnp.float32) @ gate_weight.astype(jnp.float32).T
        probs = jax.nn.softmax(logits, axis=-1)
        top1 = jnp.argmax(logits, axis=-1)
        mask = jax.nn.one_hot(top1, E, dtype=jnp.int32)
        ranks = jnp.cumsum(mask, axis=0) - 1
        mask = mask * (ranks < C).astype(jnp.int32)
        rank1 = jnp.sum(mask * ranks, axis=-1)
        weight = mask.astype(probs.dtype) * probs
        rank_oh = jax.nn.one_hot(rank1, C, dtype=probs.dtype)
        combine_weights = weight[:, :, None] * rank_oh[:, None, :]
        sec_mask = (combine_weights != 0).astype(inputs.dtype)
        dispatch = jnp.einsum('tec,th->ech', sec_mask, tokens)
        hmid = jax.nn.gelu(jnp.einsum('ech,ehi->eci', dispatch, w1), approximate=False)
        expert_out = jnp.einsum('eci,eih->ech', hmid, w2)
        out = jnp.einsum('tec,ech->th', combine_weights.astype(inputs.dtype), expert_out)
        return out.reshape(B, S, H)
    x = L0_attn_x
    xn = _layernorm(x, axis=-1)
    s = _L0_attn_ref(xn, L0_attn_Wq, L0_attn_Wk, L0_attn_Wv, L0_attn_Wo, L0_attn_lambda_q1, L0_attn_lambda_k1, L0_attn_lambda_q2, L0_attn_lambda_k2, L0_attn_gn_w, L0_attn_gn_b)
    g = _silu(_L0_ffn_ref(xn, L0_ffn_gate_w, L0_ffn_w1, L0_ffn_w2, L0_ffn_w3, L0_ffn_sw1, L0_ffn_sw2, L0_ffn_sw3))
    x = x + s * g
    xn = _layernorm(x, axis=-1)
    s = _L1_attn_ref(xn, L1_attn_Wqkv, L1_attn_bqkv, L1_attn_Wo, L1_attn_bo)
    g = _silu(_L1_ffn_ref(xn, L1_ffn_gate_weight, L1_ffn_w1, L1_ffn_w2))
    x = x + s * g
    return x

_drawn_inputs = setup_inputs


def setup_inputs(seed=0):
    import zlib

    import numpy as np

    out = dict(_drawn_inputs(seed))
    spreads = {'L0_attn_gn_w': (1.0, 0.6),
     'L0_attn_gn_b': (0.0, 0.8),
     'L1_attn_bqkv': (0.0, 0.8),
     'L1_attn_bo': (0.0, 2.0)}
    factors = {'L0_attn_Wq': 8.0,
     'L0_attn_Wk': 8.0,
     'L0_attn_Wv': 8.0,
     'L0_attn_Wo': 8.0,
     'L0_attn_lambda_q1': 8.0,
     'L0_attn_lambda_k1': 8.0,
     'L0_attn_lambda_q2': 8.0,
     'L0_attn_lambda_k2': 8.0,
     'L0_ffn_gate_w': 8.0,
     'L0_ffn_w1': 8.0,
     'L0_ffn_w2': 8.0,
     'L0_ffn_w3': 8.0,
     'L0_ffn_sw1': 8.0,
     'L0_ffn_sw2': 8.0,
     'L0_ffn_sw3': 8.0,
     'L1_attn_Wqkv': 8.0,
     'L1_attn_Wo': 8.0,
     'L1_ffn_gate_weight': 8.0,
     'L1_ffn_w1': 8.0,
     'L1_ffn_w2': 8.0}
    for name, (base, spread) in spreads.items():
        noise = np.random.default_rng([zlib.crc32(name.encode()), seed]).standard_normal(out[name].shape)
        drawn = base * np.exp(spread * noise) if base else spread * noise
        out[name] = jnp.asarray(drawn.astype(out[name].dtype))
    for name, factor in factors.items():
        out[name] = (out[name] * factor).astype(out[name].dtype)
    return out
```

```python
from contextlib import ExitStack

import concourse.bass as bass
from concourse import mybir
import numpy as np

P = 128
ALU = mybir.AluOpType
ACT = mybir.ActivationFunctionType
F32 = mybir.dt.float32
BF16 = mybir.dt.bfloat16
AX_X = mybir.AxisListType.X

BATCH, SEQ, D = 4, 256, 256
TILES = BATCH * SEQ // P
HALVES = SEQ // P
KD = D // P
DH = 16
EPS = 1e-5
LAMBDA_INIT = 0.2
MASKED = -1e30
PARTS = 3
STACK = 6 * DH
DEEP = STACK + PARTS
SCALE = DH ** -0.5

E0, SHARED, F0 = 16, 2, 176
EXPERTS0 = E0 + SHARED
FH = F0 // 2
E1, F1 = 8, 256
CAPACITY = 160

ROPE_COLS = HALVES * 2 * DH
C_IDENT, C_ROPE = 0, P
C_IOTA = C_ROPE + 2 * ROPE_COLS
C_NEG1 = C_KEPT = C_IOTA + E0
C_NEG2, C_TRIU = C_NEG1 + P, C_NEG1 + 2 * P
C_COLS = C_TRIU + P


def constants():
    c = np.zeros((P, C_COLS), np.float32)
    r = np.arange(P)
    c[:, C_IDENT:C_IDENT + P] = np.eye(P)
    c[:, C_NEG1:C_NEG1 + P] = np.where(r[None, :] > r[:, None], MASKED, 0.0)
    c[:, C_NEG2:C_NEG2 + P] = np.where(r[:, None] > r[None, :], MASKED, 0.0)
    c[:, C_TRIU:C_TRIU + P] = r[:, None] <= r[None, :]
    pos = np.arange(SEQ, dtype=np.float32)
    inv = (np.float32(1.0) / np.power(np.float32(10000.0), np.arange(0, DH, 2, dtype=np.float32) / np.float32(DH))).astype(np.float32)
    theta = np.power(np.float32(10000.0), (-np.power(np.float32(2.0), np.arange(DH // 2, dtype=np.float32)) / np.float32(DH)).astype(np.float32)).astype(np.float32)
    for layer, ang in enumerate((pos[:, None] * inv, (pos + 1)[:, None] * theta)):
        cos, sin = np.cos(ang.astype(np.float32)), np.sin(ang.astype(np.float32))
        t = np.concatenate([cos, cos, -sin, sin], axis=1).reshape(HALVES, P, 2 * DH)
        at = C_ROPE + layer * ROPE_COLS
        c[:, at:at + ROPE_COLS] = t.transpose(1, 0, 2).reshape(P, ROPE_COLS)
    c[:, C_IOTA:C_IOTA + E0] = E0 - np.arange(E0)
    return c


class Stage:
    pass


class Ring:

    def __init__(self, banks, full, **free):
        self.banks, self.full, self.free, self.order, self.at = banks, full, free, [], {}

    def plan(self, key, engine):
        ordinal = 1 + sum(e == engine for e, _ in self.order)
        self.at[key] = len(self.order)
        self.order.append((engine, ordinal))

    def bank(self, key):
        return self.banks[self.at[key] % len(self.banks)]

    def wait_free(self, pe, key):
        before = self.at[key] - len(self.banks)
        if before >= 0:
            engine, ordinal = self.order[before]
            pe.wait_ge(self.free[engine], ordinal)

    def wait_full(self, eng, key):
        eng.wait_ge(self.full, self.at[key] + 1)

    def emptied(self, key):
        engine, ordinal = self.order[self.at[key]]
        return self.free[engine], ordinal

    def wait_drained(self, pe):
        for name, s in self.free.items():
            n = sum(e == name for e, _ in self.order)
            if n:
                pe.wait_ge(s, n)


def program(nc, x_d, consts_d, wqkv0_d, wo0_d, lam_d, gn_d, gate0_d, w13_d, w2_d,
            wqkv1_d, bqkv_d, wo1_d, bo_d, gate1_d, f1a_d, f1b_d, out_d):
    with ExitStack() as ctx:
        def sb(name, shape, dt=F32):
            return ctx.enter_context(nc.sbuf_tensor(name, shape, dt))

        def sem(name):
            return ctx.enter_context(nc.semaphore(name))

        banks = [ctx.enter_context(nc.psum_tensor(f"bank{i}", [P, 512], F32)) for i in range(8)]

        class Arena:

            def __init__(self, name, words):
                self.t, self.words, self.at = sb(name, [P, words]), words, 0

            def piece(self, shape, dt=F32):
                n = int(np.prod(shape))
                words = n if dt == F32 else (n + 1) // 2
                assert self.at + words <= self.words, (self.at, words, self.words)
                v = self.t[:, self.at:self.at + words]
                self.at += words
                if dt != F32:
                    v = v.bitcast(dt)
                if len(shape) > 1:
                    names = "abcdef"[:len(shape)]
                    v = v.rearrange(f"p ({' '.join(names)}) -> p {' '.join(names)}", **dict(zip(names, shape)))
                return v

            def restart(self):
                self.at = 0

        cst = sb("cst", [P, C_KEPT])
        ident = cst[:, C_IDENT:C_IDENT + P]
        iota = cst[:, C_IOTA:C_IOTA + E0]
        identb = sb("identb", [P, P], BF16)
        neg_ts = sb("neg_ts", [P, P], BF16)
        neg_st = sb("neg_st", [P, P], BF16)
        triu = sb("triu", [P, P], BF16)
        ones = sb("ones", [P, P], BF16)
        head_mean = sb("head_mean", [P, P])
        xnT = sb("xnT", [P, KD, TILES, P])
        xres = sb("xres", [P, TILES, D])
        wqkv = sb("wqkv", [P, KD, 3 * D])
        wo = sb("wo", [P, 4, D])
        gate = sb("gate", [P, KD, E0])
        gate1 = sb("gate1", [P, KD, E1])
        lamv = sb("lamv", [P, 4, DH])
        gn = sb("gn", [P, 2, 2 * D])
        gn_flat = gn[:, :, :].rearrange("p a n -> p (a n)")
        bqkv, bo = gn_flat[:, 0:3 * D], gn_flat[:, 3 * D:4 * D]
        small = sb("small", [P, 256])
        route = sb("route", [P, TILES, EXPERTS0])
        route1 = sb("route1", [P, TILES, E1])

        moe = Arena("moe", EXPERTS0 * KD * (2 * F0 + D))
        w13 = moe.piece([EXPERTS0, KD, 2 * F0])
        w2 = moe.piece([EXPERTS0, 2, D])
        moe.restart()
        f1a = moe.piece([E1, KD, F1])
        f1b = moe.piece([E1, F1 // P, D])
        s1 = moe.piece([TILES, D])

        work = Arena("work", 22144)
        x_in, xn = work.piece([TILES, D]), work.piece([TILES, D])
        masks = work.piece([C_COLS - C_KEPT])
        work.restart()
        qkT = work.piece([2, 40, SEQ], BF16)
        stack = work.piece([40, 6, DH], BF16)
        rotary = work.piece([2 * 40 * DH])
        rot_a, rot_b = (rotary[:, k * 40 * DH:(k + 1) * 40 * DH].rearrange("p (g d) -> p g d", d=DH) for k in range(2))
        rot_x = work.piece([32, DH])
        o_n = rotary[:, 0:32 * 32].rearrange("p (m w) -> p m w", w=32)
        pT = [work.piece([512]) for _ in range(6)]
        vaug = work.piece([2, HALVES, 16 * 17])
        o_raw = work.piece([HALVES, 32 * 33])
        o_d = work.piece([HALVES, 2 * D])
        zT = work.piece([4, P])
        nmax = work.piece([32])
        nmax_r = work.piece([32])
        nparts = work.piece([2, PARTS * 32], BF16)
        nT = work.piece([2, P], BF16)
        rsum = work.piece([32])
        work.restart()
        x_again = work.piece([TILES, D])
        acc = work.piece([TILES, D])
        silu_a = work.piece([2, F0])
        hid = work.piece([2, F0])
        hidT = work.piece([2, 2, P])
        gelT = work.piece([2, 2, 512])
        gval = work.piece([TILES, D])
        xn1 = work.piece([TILES, D])
        sc = work.piece([6, TILES * E0])

        ld = {n: sem("ld_" + n) for n in ("x", "cst", "wqkv", "wo", "gate", "lam", "gn", "bias", "w13", "w2",
                                          "x2", "wqkv1", "wo1", "f1")}
        out_sem = sem("out_sem")
        dve_c, act_c, pool_c = sem("dve_chain"), sem("act_chain"), sem("pool_chain")
        s_cast = sem("s_cast")
        s_ones = sem("s_ones")
        s_lamx, s_lame = sem("s_lamx"), sem("s_lame")

        def norm_state(n):
            q = Stage()
            q.n = n
            q.tp = Ring(banks[0:2], sem(f"ln{n}_tp_full"), act=sem(f"ln{n}_tp_free"))
            for g in range(TILES // 2):
                q.tp.plan(g, "act")
            q.veps, q.pow = sem(f"ln{n}_veps"), sem(f"ln{n}_pow")
            q.xn = sem(f"ln{n}_xn")
            q.logits = sem(f"ln{n}_logits")
            q.routed, q.expin, q.expd = sem(f"ln{n}_routed"), sem(f"ln{n}_expin"), sem(f"ln{n}_expd")
            q.hot, q.cum = sem(f"ln{n}_hot"), sem(f"ln{n}_cum")
            return q

        norms = [norm_state(0), norm_state(1)]
        stats = small[:, 0:TILES * 6].rearrange("p (t s) -> p t s", s=6)
        mv = small[:, 48:64].rearrange("p (t s) -> p t s", s=2)
        veps, rstd, tmp8 = small[:, 64:72], small[:, 72:80], small[:, 80:88]
        r8a, r8b = small[:, 96:104], small[:, 104:112]
        lam2, lamx, lam = small[:, 112:114], small[:, 114:116], small[:, 116:117]
        gn_sum, gn_ve, gn_rs, gn_t = small[:, 120:152], small[:, 152:168], small[:, 168:184], small[:, 184:200]
        minus_half16 = small[:, 200:216]

        def attention_state(n, maps, kgroups, vheads, vwidth, kof, vof):
            a = Stage()
            a.n, a.maps, a.units, a.kgroups, a.groups = n, maps, maps // 4, kgroups, maps + kgroups
            a.vheads, a.vw, a.kof, a.vof = vheads, vwidth, kof, vof
            a.tgroups = a.groups // 8
            a.zchunks = vheads * vwidth * (4 if n == 0 else 1) // P
            p = f"a{n}_"
            a.pj = Ring(banks[0:2], sem(p + "pj_full"), act=sem(p + "pj_free_act"), dve=sem(p + "pj_free_dve"))
            a.s = Ring(banks[2:4], sem(p + "s_full"), dve=sem(p + "s_free"))
            a.st = Ring(banks[4:7], sem(p + "st_full"), act=sem(p + "st_free"))
            a.po = Ring(banks[7:8], sem(p + "po_full"), act=sem(p + "po_free_act"))
            a.stacked = sem(p + "stacked")
            a.nmax = sem(p + "nmax")
            a.rows = [sem(p + "rows0"), sem(p + "rows1")]
            a.ones = sem(p + "ones")
            a.sums = sem(p + "sums")
            a.gpow, a.z = sem(p + "gpow"), sem(p + "z")
            a.onorm = sem(p + "onorm") if n == 0 else a.z
            steps, u = [], a.units
            for b in range(BATCH + 2):
                slots = [[[], []] for _ in range(u + 1)]
                if b >= 2:
                    i0, i1 = 2 * b - 4, 2 * b - 3
                    slots[0][0] += [("divide", i0), ("divide", i1)]
                    slots[u * 3 // 4][1] += [("turn", i0), ("out", i0)]
                    slots[u][1] += [("turn", i1), ("out", i1)]
                    if n == 0:
                        slots[2][1] += [("mean", b - 2)]
                        slots[4][1] += [("variance", b - 2)]
                if b < BATCH:
                    slots[0][0] += [("project", 2 * b)]
                    second = [("parts", 2 * b), ("project", 2 * b + 1)]
                    if u == 8:
                        slots[1][0] += second
                    else:
                        slots[0][1] += second
                    slots[u // 4][0] += [("parts", 2 * b + 1)]
                    for q in range(3 * u):
                        slots[u // 4 + q // 4][1].insert(q % 4, ("max", (b, q)))
                    slots[u // 2 + 1][1] += [("rows", 2 * b)]
                    slots[u][1] += [("rows", 2 * b + 1)]
                for j, (before, after) in enumerate(slots):
                    steps += before
                    if 0 < b <= BATCH and j < u:
                        steps += [("exp", (b - 1, j))]
                    steps += after
                    if 0 < b <= BATCH and j > 0:
                        steps += [("value", (b - 1, j - 1))]
            a.steps = steps
            for kind, w in steps:
                if kind == "project":
                    a.pj.plan(("q", w), "dve")
                    a.pj.plan(("kv", w), "dve")
                elif kind == "parts":
                    for g in range(a.tgroups):
                        a.pj.plan(("t", w, g), "act")
                elif kind in ("mean", "variance"):
                    a.pj.plan((kind, w), "dve")
                elif kind == "turn":
                    a.pj.plan(("z", w), "act")
                elif kind == "out":
                    a.pj.plan(("o", w), "dve")
                elif kind == "max":
                    a.s.plan(w, "dve")
                elif kind == "exp":
                    for u in range(3):
                        a.st.plan((*w, u), "act")
                elif kind == "rows":
                    a.po.plan(("rows", w), "act")
                elif kind == "value":
                    a.po.plan(w, "act")
            return a

        attns = [attention_state(0, 32, 8, 4, 32, lambda m: m // 4, lambda m: m // 8),
                 attention_state(1, 16, 16, 16, 16, lambda m: m, lambda m: m)]

        def rope_tables(a, half):
            at = C_ROPE + a.n * ROPE_COLS + half * 2 * DH
            return cst[:, at:at + DH], cst[:, at + DH:at + 2 * DH]

        def max_use(a, q):
            return (0, range(4 * q, 4 * q + 4)) if q < a.units else (1, range(2 * (q - a.units), 2 * (q - a.units) + 2))

        def vaug_of(a, b):
            w = a.vw + 1
            return vaug[:, b % 2, :, 0:a.vheads * w].rearrange("p h (v w) -> p h v w", w=w)

        def raw_of(a):
            w = a.vw + 1
            return o_raw[:, :, 0:a.maps * w].rearrange("p h (m w) -> p h m w", w=w)

        def bfv(bank):
            return bank[:, :].bitcast(BF16).rearrange("p (m t) -> p m t", t=P)

        m0 = Stage()
        m0.up = Ring(banks[0:3], sem("m0_up_full"), dve=sem("m0_hid"))
        m0.ht = Ring(banks[3:5], sem("m0_ht_full"), act=sem("m0_hidT"))
        m0.dn = Ring(banks[5:7], sem("m0_dn_full"), dve=sem("m0_dn_free"))
        m0.silu, m0.g, m0.x = sem("m0_silu"), sem("m0_g"), sem("m0_x")
        N0 = EXPERTS0 * TILES
        for n in range(N0):
            m0.up.plan(n, "dve")
            m0.ht.plan(n, "act")
            m0.dn.plan(n, "dve")

        m1 = Stage()
        m1.up = Ring(banks[0:4], sem("m1_up_full"), act=sem("m1_up_free"))
        m1.dn = Ring(banks[4:8], sem("m1_dn_full"), dve=sem("m1_dn_free"))
        m1.g, m1.x = sem("m1_g"), sem("m1_x")
        N1 = E1 * 2
        for n in range(N1):
            for m in range(2):
                m1.up.plan((n, m), "act")
            for t in range(4):
                m1.dn.plan((n, t), "dve")

        block = ctx.enter_context(nc.Block())

        @block.sync
        def _(sp):
            sp.dma_start(x_in, x_d.rearrange("(t p) d -> p t d", p=P)).then_inc(ld["x"], 16)
            sp.dma_start(cst[:, :], consts_d[:, 0:C_KEPT]).then_inc(ld["cst"], 16)
            sp.dma_start(masks, consts_d[:, C_KEPT:]).then_inc(ld["cst"], 16)
            sp.dma_start(wqkv[:, :, :], wqkv0_d).then_inc(ld["wqkv"], 16)
            sp.dma_start(gate[:, :, :], gate0_d).then_inc(ld["gate"], 16)
            sp.dma_start(gate1[:, :, :], gate1_d).then_inc(ld["gate"], 16)
            sp.dma_start(lamv[:, :, :], lam_d.partition_broadcast(P)).then_inc(ld["lam"], 16)
            sp.dma_start(gn[:, :, :], gn_d.partition_broadcast(P)).then_inc(ld["gn"], 16)
            sp.dma_start(wo[:, :, :], wo0_d).then_inc(ld["wo"], 16)
            for e in range(0, EXPERTS0, 3):
                sp.dma_start(w13[:, e:e + 3], w13_d[:, e:e + 3]).then_inc(ld["w13"], 16)
            for e in range(0, EXPERTS0, 6):
                sp.dma_start(w2[0:FH, e:e + 6], w2_d[:, e:e + 6]).then_inc(ld["w2"], 16)

            def maximum_rows(a):
                for i in range(TILES):
                    b, half = divmod(i, HALVES)
                    sp.wait_ge(*a.po.emptied(("rows", i)))
                    if b >= 2:
                        sp.wait_ge(a.st.full, a.st.at[(b - 2, a.units - 1, 2)] + 1)
                    for k in range(PARTS):
                        sp.dma_start(qkT[STACK + k:STACK + k + 1, b % 2, 0:a.maps, half * P:half * P + P],
                                     nT[k * a.maps:(k + 1) * a.maps, i % 2, :]).then_inc(a.rows[b % 2], 16)

            maximum_rows(attns[0])
            sp.wait_ge(*attns[0].pj.emptied(("o", TILES - 1)))
            sp.dma_start(x_again, x_d.rearrange("(t p) d -> p t d", p=P)).then_inc(ld["x2"], 16)
            sp.dma_start(wqkv[:, :, :], wqkv1_d).then_inc(ld["wqkv1"], 16)
            sp.dma_start(wo[:, 0:2, :], wo1_d).then_inc(ld["wo1"], 16)
            sp.dma_start(bqkv, bqkv_d.partition_broadcast(P)).then_inc(ld["bias"], 16)
            sp.dma_start(bo, bo_d.partition_broadcast(P)).then_inc(ld["bias"], 16)
            sp.wait_ge(m0.dn.full, N0)
            sp.dma_start(f1a, f1a_d).then_inc(ld["f1"], 16)
            sp.dma_start(f1b, f1b_d).then_inc(ld["f1"], 16)
            maximum_rows(attns[1])
            for i in range(TILES):
                sp.wait_ge(m1.x, i + 1)
                sp.dma_start(out_d[i * P:i * P + P, :], xres[:, i, :]).then_inc(out_sem, 16)
            sp.wait_ge(out_sem, 16 * TILES)

        @block.tensor
        def _(pe):
            def layer_norm(q, experts, g_sb, xn_t, out_bank):
                for g in range(TILES // 2):
                    q.tp.wait_free(pe, g)
                    bank = q.tp.bank(g)
                    for u in range(2):
                        i = 2 * g + u
                        pe.wait_ge(q.xn, i + 1)
                        for k in range(KD):
                            mm = nc.tensor.transpose(bank[:, (2 * u + k) * P:(2 * u + k + 1) * P],
                                                     xn_t[:, i, k * P:(k + 1) * P], ident)
                    mm.then_inc(q.tp.full, 1)
                pe.wait_ge(ld["gate"], 32)
                for i in range(TILES):
                    pe.wait_ge(*q.tp.emptied(i // 2))
                    for k in range(KD):
                        mm = nc.tensor.matmul(out_bank[:, i * experts:(i + 1) * experts], xnT[:, k, i, :],
                                              g_sb[:, k, :], start=(k == 0), stop=(k == KD - 1))
                mm.then_inc(q.logits, 1)

            def project(a, i):
                cols = {"q": slice(0, 512), "kv": slice(512, 768)}
                for use, n in (("q", 512), ("kv", 256)):
                    key = (use, i)
                    a.pj.wait_free(pe, key)
                    for k in range(KD):
                        mm = nc.tensor.matmul(a.pj.bank(key)[:, 0:n], xnT[:, k, i, :], wqkv[:, k, cols[use]],
                                              start=(k == 0), stop=(k == KD - 1))
                    mm.then_inc(a.pj.full, 1)

            def parts(a, i):
                pe.wait_ge(a.stacked, i + 1)
                for g in range(a.tgroups):
                    key = ("t", i, g)
                    a.pj.wait_free(pe, key)
                    for u in range(8):
                        mm = nc.tensor.transpose(bfv(a.pj.bank(key))[0:STACK, u, :],
                                                 stack[:, 8 * g + u].rearrange("p s d -> p (s d)"), identb[:, :])
                    mm.then_inc(a.pj.full, 1)

            def transposed(a, i):
                pe.wait_ge(*a.pj.emptied(("t", i, a.tgroups - 1)))

            def scores(a, b, q):
                half, ms = max_use(a, q)
                transposed(a, 2 * b + half)
                a.s.wait_free(pe, (b, q))
                bank = a.s.bank((b, q))
                n = P * (half + 1)
                view = bank[:, :].rearrange("p (m s) -> p m s", s=n)
                nc.tensor.matmul(view[:, :, half * P:half * P + P], identb[:, :],
                                 neg_ts[:, :].unsqueeze(1).to_broadcast([P, len(ms), P]),
                                 start=True, stop=False, skip_group_check=True)
                for u, m in enumerate(ms):
                    mm = nc.tensor.matmul(view[:, u, :], qkT[0:STACK, b % 2, m, half * P:half * P + P],
                                          qkT[0:STACK, b % 2, a.maps + a.kof(m), 0:n],
                                          start=False, stop=True, skip_group_check=True)
                mm.then_inc(a.s.full, 1)

            def exp_scores(a, b, j):
                pe.wait_ge(a.rows[b % 2], 16 * PARTS * HALVES * (b // 2 + 1))
                pe.wait_ge(a.ones, 1)
                for u in range(3):
                    key = (b, j, u)
                    a.st.wait_free(pe, key)
                    bank = a.st.bank(key)
                    if u < 2:
                        keys, ms, t0, n = 0, (4 * j + 2 * u, 4 * j + 2 * u + 1), 0, SEQ
                    else:
                        keys, ms, t0, n = 1, range(4 * j, 4 * j + 4), P, P
                    view = bank[:, :].rearrange("p (m t) -> p m t", t=n)
                    nc.tensor.matmul(view[:, :, 0:P], identb[:, :],
                                     neg_st[:, :].unsqueeze(1).to_broadcast([P, len(ms), P]),
                                     start=True, stop=False, skip_group_check=True)
                    for v, m in enumerate(ms):
                        mm = nc.tensor.matmul(view[:, v, :],
                                              qkT[0:DEEP, b % 2, a.maps + a.kof(m), keys * P:keys * P + P],
                                              qkT[0:DEEP, b % 2, m, t0:t0 + n],
                                              start=False, stop=True, skip_group_check=True)
                    mm.then_inc(a.st.full, 1)

            def rows(a, i):
                pe.wait_ge(a.nmax, i + 1)
                key = ("rows", i)
                a.po.wait_free(pe, key)
                n = PARTS * a.maps
                nc.tensor.transpose(bfv(a.po.bank(key))[0:n, 0, :], nparts[:, i % 2, 0:n], identb[:, :])\
                    .then_inc(a.po.full, 1)

            def value(a, b, j):
                key = (b, j)
                a.po.wait_free(pe, key)
                w = a.vw + 1
                out = a.po.bank(key)[:, 0:HALVES * 4 * w].rearrange("p (h m w) -> p h m w", h=HALVES, w=w)
                v = vaug_of(a, b)
                pe.wait_ge(*a.st.emptied((b, j, 2)))
                probs = [pT[a.st.at[(b, j, u)] % 6] for u in range(3)]
                for r in range(4):
                    vh = a.vof(4 * j + r)
                    p0 = probs[r // 2][:, (r % 2) * SEQ:(r % 2) * SEQ + SEQ]
                    nc.tensor.matmul(out[:, 0, r, :], p0[:, 0:P], v[:, 0, vh, :], start=True, stop=True)
                    nc.tensor.matmul(out[:, 1, r, :], p0[:, P:SEQ], v[:, 0, vh, :], start=True, stop=False)
                    mm = nc.tensor.matmul(out[:, 1, r, :], probs[2][:, r * P:r * P + P], v[:, 1, vh, :],
                                          start=False, stop=True)
                mm.then_inc(a.po.full, 1)

            def head_statistic(a, kind, b):
                key = (kind, b)
                pe.wait_ge(a.sums, 2 * b + (1 if kind == "mean" else 2))
                a.pj.wait_free(pe, key)
                for half in range(HALVES):
                    mm = nc.tensor.matmul(a.pj.bank(key)[:, 0:16], head_mean[:, :], gn_sum[:, 16 * half:16 * half + 16],
                                          start=(half == 0), stop=(half == HALVES - 1))
                mm.then_inc(a.pj.full, 1)

            def turn(a, i):
                pe.wait_ge(a.z, i + 1 if a.n == 1 else i // HALVES + 1)
                key = ("z", i)
                a.pj.wait_free(pe, key)
                for c in range(a.zchunks):
                    mm = nc.tensor.transpose(a.pj.bank(key)[:, c * P:(c + 1) * P], o_d[:, i % 2, c * P:(c + 1) * P], ident)
                mm.then_inc(a.pj.full, 1)

            def out(a, i):
                pe.wait_ge(*a.pj.emptied(("z", i)))
                pe.wait_ge(ld["wo" if a.n == 0 else "wo1"], 16)
                key = ("o", i)
                a.pj.wait_free(pe, key)
                for c in range(a.zchunks):
                    mm = nc.tensor.matmul(a.pj.bank(key)[:, 0:D], zT[:, c, :], wo[:, c, :],
                                          start=(c == 0), stop=(c == a.zchunks - 1))
                mm.then_inc(a.pj.full, 1)

            def attention(a):
                pe.wait_ge(ld["wqkv" if a.n == 0 else "wqkv1"], 16)
                for kind, w in a.steps:
                    if kind == "project":
                        project(a, w)
                    elif kind == "parts":
                        parts(a, w)
                    elif kind == "max":
                        scores(a, *w)
                    elif kind == "exp":
                        exp_scores(a, *w)
                    elif kind == "rows":
                        rows(a, w)
                    elif kind == "value":
                        value(a, *w)
                    elif kind in ("mean", "variance"):
                        head_statistic(a, kind, w)
                    elif kind == "turn":
                        turn(a, w)
                    elif kind == "out":
                        out(a, w)
                for ring in (a.pj, a.s, a.st, a.po):
                    ring.wait_drained(pe)

            def experts0():
                def up(n):
                    e, t = divmod(n, TILES)
                    m0.up.wait_free(pe, n)
                    for k in range(KD):
                        mm = nc.tensor.matmul(m0.up.bank(n)[:, 0:2 * F0], xnT[:, k, t, :], w13[:, e, k, :],
                                              start=(k == 0), stop=(k == KD - 1))
                    mm.then_inc(m0.up.full, 1)

                def turn_hidden(n):
                    pe.wait_ge(*m0.up.emptied(n))
                    m0.ht.wait_free(pe, n)
                    for f in range(2):
                        mm = nc.tensor.transpose(m0.ht.bank(n)[0:FH, f * P:(f + 1) * P],
                                                 hid[:, n % 2, f * FH:(f + 1) * FH], ident)
                    mm.then_inc(m0.ht.full, 1)

                def down(n):
                    e = n // TILES
                    pe.wait_ge(*m0.ht.emptied(n))
                    m0.dn.wait_free(pe, n)
                    for f in range(2):
                        mm = nc.tensor.matmul(m0.dn.bank(n)[:, 0:D], hidT[0:FH, n % 2, f, :], w2[0:FH, e, f, :],
                                              start=(f == 0), stop=(f == 1))
                    mm.then_inc(m0.dn.full, 1)

                pe.wait_ge(ld["w13"], 16 * 6)
                pe.wait_ge(ld["w2"], 16 * 3)
                for n in range(N0 + 2):
                    if n < N0:
                        up(n)
                    if 1 <= n <= N0:
                        turn_hidden(n - 1)
                    if n >= 2:
                        down(n - 2)
                for ring in (m0.up, m0.ht, m0.dn):
                    ring.wait_drained(pe)

            def experts1():
                def up(n):
                    e, half = divmod(n, 2)
                    for m in range(2):
                        m1.up.wait_free(pe, (n, m))
                        for k in range(KD):
                            mm = nc.tensor.matmul(m1.up.bank((n, m))[:, :], f1a[:, e, k, m * P:(m + 1) * P],
                                                  xnT[:, k, 4 * half:4 * half + 4, :],
                                                  start=(k == 0), stop=(k == KD - 1))
                        mm.then_inc(m1.up.full, 1)

                def down(n):
                    e = n // 2
                    pe.wait_ge(*m1.up.emptied((n, 1)))
                    for t in range(4):
                        m1.dn.wait_free(pe, (n, t))
                        for f in range(2):
                            mm = nc.tensor.matmul(m1.dn.bank((n, t))[:, 0:D], gelT[:, n % 2, f, t * P:(t + 1) * P],
                                                  f1b[:, e, f, :], start=(f == 0), stop=(f == 1))
                        mm.then_inc(m1.dn.full, 1)

                pe.wait_ge(ld["f1"], 32)
                for n in range(N1 + 1):
                    if n < N1:
                        up(n)
                    if n:
                        down(n - 1)

            pe.wait_ge(ld["cst"], 32)
            pe.wait_ge(s_cast, 4)
            layer_norm(norms[0], E0, gate, xn, banks[2])
            norms[0].tp.wait_drained(pe)
            pe.wait_ge(norms[0].routed, 1)
            attention(attns[0])
            experts0()
            layer_norm(norms[1], E1, gate1, xn1, banks[2])
            pe.wait_ge(norms[1].hot, 1)
            hot = sc[:, 5, :].bitcast(BF16)[:, 0:TILES * E1]
            for i in range(TILES):
                for j in range(i + 1):
                    mm = nc.tensor.matmul(banks[3][:, i * E1:(i + 1) * E1], (triu if j == i else ones)[:, :],
                                          hot[:, j * E1:(j + 1) * E1], start=(j == 0), stop=(j == i))
            mm.then_inc(norms[1].cum, 1)
            pe.wait_ge(norms[1].routed, 1)
            norms[1].tp.wait_drained(pe)
            attention(attns[1])
            experts1()

        @block.scalar
        def _(act):
            def copy(dst, src):
                return nc.scalar.activation(dst, src, ACT.Copy)

            def layer_norm(q, experts, out_bank):
                for g in range(TILES // 2):
                    q.tp.wait_full(act, g)
                    copy(xnT[:, :, 2 * g:2 * g + 2, :].rearrange("p k u t -> p u k t"),
                         q.tp.bank(g)[:, :].rearrange("p (u k t) -> p u k t", u=2, k=KD)).then_inc(q.tp.free["act"], 1)
                act.wait_ge(q.expin, 1)
                nc.scalar.activation(sc[:, 1, 0:TILES * experts], sc[:, 0, 0:TILES * experts], ACT.Exp)\
                    .then_inc(q.expd, 1)

            def attention(a):
                for kind, w in a.steps:
                    if kind == "parts":
                        b, half = divmod(w, HALVES)
                        if b >= 2:
                            act.wait_ge(a.st.full, a.st.at[(b - 2, a.units - 1, 2)] + 1)
                        for g in range(a.tgroups):
                            key = ("t", w, g)
                            a.pj.wait_full(act, key)
                            copy(qkT[0:STACK, b % 2, 8 * g:8 * g + 8, half * P:half * P + P],
                                 bfv(a.pj.bank(key))[0:STACK, :, :]).then_inc(a.pj.free["act"], 1)
                    elif kind == "rows":
                        b = w // HALVES
                        if w >= 2:
                            for p in range(2):
                                done = [i for i in range(w - 1) if (i // HALVES) % 2 == p]
                                if done:
                                    act.wait_ge(a.rows[p], 16 * PARTS * len(done))
                        a.po.wait_full(act, ("rows", w))
                        n = PARTS * a.maps
                        copy(nT[0:n, w % 2, :], bfv(a.po.bank(("rows", w)))[0:n, 0, :]).then_inc(a.po.free["act"], 1)
                    elif kind == "exp":
                        for u in range(3):
                            key = (*w, u)
                            at = a.st.at[key]
                            if at >= 6:
                                a.po.wait_full(act, divmod(at // 3 - 2, a.units))
                            a.st.wait_full(act, key)
                            nc.scalar.activation(pT[at % 6], a.st.bank(key)[:, :], ACT.Exp, scale=SCALE)\
                                .then_inc(a.st.free["act"], 1)
                    elif kind == "value":
                        b, j = w
                        if b >= 1:
                            act.wait_ge(a.onorm, HALVES * b)
                        a.po.wait_full(act, w)
                        n = a.vw + 1
                        copy(raw_of(a)[:, :, 4 * j:4 * j + 4, :],
                             a.po.bank(w)[:, 0:HALVES * 4 * n].rearrange("p (h m w) -> p h m w", h=HALVES, w=n))\
                            .then_inc(a.po.free["act"], 1)
                    elif kind == "turn":
                        if w:
                            a.pj.wait_full(act, ("o", w - 1))
                        a.pj.wait_full(act, ("z", w))
                        copy(zT[:, 0:a.zchunks, :], a.pj.bank(("z", w))[:, 0:a.zchunks * P]
                             .rearrange("p (c t) -> p c t", t=P)).then_inc(a.pj.free["act"], 1)

            layer_norm(norms[0], E0, banks[2])
            act.wait_ge(s_lamx, 1)
            nc.scalar.activation(lamx, lam2, ACT.Exp).then_inc(s_lame, 1)
            attention(attns[0])

            for n in range(N0 + 1):
                if n < N0:
                    m0.up.wait_full(act, n)
                    if n >= 2:
                        act.wait_ge(*m0.up.emptied(n - 2))
                    nc.scalar.activation(silu_a[:, n % 2, :], m0.up.bank(n)[:, 0:F0], ACT.Silu).then_inc(m0.silu, 1)
                if n:
                    m0.ht.wait_full(act, n - 1)
                    if n >= 3:
                        m0.dn.wait_full(act, n - 3)
                    copy(hidT[0:FH, (n - 1) % 2, :, :], m0.ht.bank(n - 1)[0:FH, 0:2 * P]
                         .rearrange("p (f t) -> p f t", t=P)).then_inc(m0.ht.free["act"], 1)
            for i in range(TILES):
                act.wait_ge(m0.dn.free["dve"], N0 - TILES + i + 1)
                nc.scalar.activation(gval[:, i, :], acc[:, i, :], ACT.Silu).then_inc(m0.g, 1)
            layer_norm(norms[1], E1, banks[2])
            attention(attns[1])
            for n in range(N1):
                for m in range(2):
                    m1.up.wait_full(act, (n, m))
                    if n >= 2:
                        m1.dn.wait_full(act, (n - 2, 3))
                    nc.scalar.activation(gelT[:, n % 2, m, :], m1.up.bank((n, m))[:, :], ACT.Gelu)\
                        .then_inc(m1.up.free["act"], 1)
            for i in range(TILES):
                act.wait_ge(m1.dn.free["dve"], (N1 - 2 + i // 4) * 4 + i % 4 + 1)
                nc.scalar.activation(gval[:, i, :], acc[:, i, :], ACT.Silu).then_inc(m1.g, 1)

        @block.gpsimd
        def _(pool):
            nc.gpsimd.memset(ones[:, :], 1.0).then_inc(s_ones, 1)
            nc.gpsimd.memset(minus_half16, -0.5).then_inc(s_ones, 1)
            nc.gpsimd.memset(head_mean[:, :], 1.0 / (SEQ * 2 * DH)).then_inc(s_ones, 1)
            pool.wait_ge(s_ones, 3)

            def power(ready, n, done, dst, src, width):
                pool.wait_ge(ready, n)
                nc.gpsimd.tensor_tensor(dst, src, minus_half16[:, 0:width], ALU.pow).then_inc(done, 1)

            def attention(a):
                for kind, w in a.steps:
                    if kind == "variance":
                        power(*a.pj.emptied((kind, w)), a.gpow, gn_rs, gn_ve, 16)

            power(norms[0].veps, 1, norms[0].pow, rstd, veps, TILES)
            attention(attns[0])
            power(norms[1].veps, 1, norms[1].pow, rstd, veps, TILES)
            attention(attns[1])

        @block.vector
        def _(dve):
            chain = [0]

            def link(ins):
                chain[0] += 1
                ins.then_inc(dve_c, 1)
                dve.wait_ge(dve_c, chain[0])

            def newton(y, v, t):
                link(nc.vector.tensor_tensor(t, y, y, ALU.mult))
                link(nc.vector.tensor_tensor(t, t, v, ALU.mult))
                link(nc.vector.tensor_scalar(t, t, -0.5, 1.5, ALU.mult, ALU.add))
                link(nc.vector.tensor_tensor(y, y, t, ALU.mult))

            def layer_norm(q, x_t, xn_t, arrived):
                for i in range(TILES):
                    arrived(i)
                    link(nc.vector.bn_stats(stats[:, i, :], x_t[:, i, :]))
                    link(nc.vector.bn_aggr(mv[:, i, :], stats[:, i, :]))
                nc.vector.tensor_scalar(veps, mv[:, :, 1], EPS, None, ALU.add).then_inc(q.veps, 1)
                dve.wait_ge(q.pow, 1)
                newton(rstd, veps, tmp8)
                for i in range(TILES):
                    nc.vector.tensor_scalar(xn_t[:, i, :], x_t[:, i, :], mv[:, i, 0:1], rstd[:, i:i + 1],
                                            ALU.subtract, ALU.mult).then_inc(q.xn, 1)

            def softmax(q, experts, bank):
                n = TILES * experts

                def v(k):
                    return sc[:, k, 0:n].rearrange("p (t e) -> p t e", e=experts)

                def over(x):
                    return x.unsqueeze(2).to_broadcast([P, TILES, experts])

                dve.wait_ge(q.logits, 1)
                link(nc.vector.tensor_copy(sc[:, 2, 0:n], bank[:, 0:n]))
                link(nc.vector.tensor_reduce(r8a, v(2), AX_X, ALU.max))
                nc.vector.tensor_tensor(v(0), v(2), over(r8a), ALU.subtract).then_inc(q.expin, 1)
                dve.wait_ge(q.expd, 1)
                link(nc.vector.tensor_reduce(r8b, v(1), AX_X, ALU.add))
                link(nc.vector.reciprocal(r8b, r8b))
                link(nc.vector.tensor_tensor(v(1), v(1), over(r8b), ALU.mult))
                return v, over

            def first_largest(v, over, experts, src, dst):
                link(nc.vector.tensor_reduce(r8a, src, AX_X, ALU.max))
                link(nc.vector.tensor_tensor(dst, src, over(r8a), ALU.is_ge))
                count = iota[:, 0:experts].unsqueeze(1).to_broadcast([P, TILES, experts])
                link(nc.vector.tensor_tensor(dst, dst, count, ALU.mult))
                link(nc.vector.tensor_reduce(r8a, dst, AX_X, ALU.max))
                link(nc.vector.tensor_tensor(dst, dst, over(r8a), ALU.is_ge))

            def project(a, i):
                b, half = divmod(i, HALVES)
                cos, sin = rope_tables(a, half)
                nq = 32 if a.n == 0 else 32

                def rotate(src, g0, g1):
                    n = g1 - g0
                    nc.vector.tensor_tensor(rot_a[:, g0:g1, :], src, cos.unsqueeze(1).to_broadcast([P, n, DH]), ALU.mult)
                    h = DH // 2
                    nc.vector.tensor_tensor(rot_b[:, g0:g1, 0:h], src[:, :, h:DH],
                                            sin[:, 0:h].unsqueeze(1).to_broadcast([P, n, h]), ALU.mult)
                    return nc.vector.tensor_tensor(rot_b[:, g0:g1, h:DH], src[:, :, 0:h],
                                                   sin[:, h:DH].unsqueeze(1).to_broadcast([P, n, h]), ALU.mult)

                a.pj.wait_full(dve, ("q", i))
                first = a.pj.bank(("q", i))[:, :].rearrange("p (g d) -> p g d", d=DH)
                if a.n == 0:
                    rotate(first, 0, nq).then_inc(a.pj.free["dve"], 1)
                else:
                    nc.vector.tensor_tensor(rot_x, first, bqkv[:, 0:512].rearrange("p (g d) -> p g d", d=DH), ALU.add)\
                        .then_inc(a.pj.free["dve"], 1)
                    dve.wait_ge(*a.pj.emptied(("q", i)))
                    link(rotate(rot_x, 0, nq))
                a.pj.wait_full(dve, ("kv", i))
                second = a.pj.bank(("kv", i))
                v0 = 2 * D // 4 if a.n == 0 else 0
                if a.n == 0:
                    rotate(second[:, 0:v0].rearrange("p (g d) -> p g d", d=DH), nq, a.groups)
                vals = second[:, v0:v0 + a.vheads * a.vw].rearrange("p (v w) -> p v w", w=a.vw)
                if b >= 2:
                    a.po.wait_full(dve, (b - 2, a.units - 1))
                dst = vaug_of(a, b)[:, half, :, 0:a.vw]
                if a.n == 0:
                    nc.vector.tensor_copy(dst, vals).then_inc(a.pj.free["dve"], 1)
                else:
                    nc.vector.tensor_tensor(dst, vals, bqkv[:, 512:768].rearrange("p (v w) -> p v w", w=a.vw), ALU.add)\
                        .then_inc(a.pj.free["dve"], 1)
                dve.wait_ge(*a.pj.emptied(("kv", i)))
                ng, m = a.groups, a.maps
                link(nc.vector.tensor_tensor(rot_a[:, 0:ng, :], rot_a[:, 0:ng, :], rot_b[:, 0:ng, :], ALU.add))
                if i:
                    a.pj.wait_full(dve, ("t", i - 1, a.tgroups - 1))
                link(nc.vector.tensor_copy(stack[:, 0:ng, 0, :], rot_a[:, 0:ng, :]))
                link(nc.vector.tensor_tensor(rot_a[:, 0:ng, :], rot_a[:, 0:ng, :], stack[:, 0:ng, 0, :], ALU.subtract))
                nc.vector.tensor_copy(stack[:, 0:m, 1:3, :], stack[:, 0:m, 0:1, :].to_broadcast([P, m, 2, DH]))
                link(nc.vector.tensor_copy(stack[:, 0:ng, 4, :], rot_a[:, 0:ng, :]))
                nc.vector.tensor_copy(stack[:, m:ng, 3, :], stack[:, m:ng, 0, :])
                nc.vector.tensor_copy(stack[:, m:ng, 5, :], stack[:, m:ng, 0, :])
                nc.vector.tensor_copy(stack[:, 0:m, 3, :], stack[:, 0:m, 4, :])
                nc.vector.tensor_copy(stack[:, m:ng, 1, :], stack[:, m:ng, 4, :])
                nc.vector.tensor_tensor(stack[:, 0:m, 5, :], rot_a[:, 0:m, :], stack[:, 0:m, 4, :], ALU.subtract)
                nc.vector.tensor_tensor(stack[:, m:ng, 2, :], rot_a[:, m:ng, :], stack[:, m:ng, 4, :], ALU.subtract)\
                    .then_inc(a.stacked, 1)

            def row_max(a, b, q):
                half, ms = max_use(a, q)
                a.s.wait_full(dve, (b, q))
                n = P * (half + 1)
                nc.vector.tensor_reduce(nmax[:, ms[0]:ms[-1] + 1], a.s.bank((b, q))[:, :].rearrange("p (m s) -> p m s", s=n),
                                        AX_X, ALU.max, negate=True).then_inc(a.s.free["dve"], 1)
                last = a.units - 1 if half == 0 else 3 * a.units - 1
                if q != last:
                    return
                i = 2 * b + half
                m = a.maps
                dve.wait_ge(*a.s.emptied((b, q)))
                if i >= 2:
                    a.po.wait_full(dve, ("rows", i - 2))
                parts = nparts[:, i % 2, 0:PARTS * m].rearrange("p (k m) -> p k m", m=m)
                link(nc.vector.tensor_copy(parts[:, 0, :], nmax[:, 0:m]))
                link(nc.vector.tensor_tensor(nmax_r[:, 0:m], nmax[:, 0:m], parts[:, 0, :], ALU.subtract))
                link(nc.vector.tensor_copy(parts[:, 1, :], nmax_r[:, 0:m]))
                nc.vector.tensor_tensor(parts[:, 2, :], nmax_r[:, 0:m], parts[:, 1, :], ALU.subtract)\
                    .then_inc(a.nmax, 1)

            def divide(a, i):
                b, half = divmod(i, HALVES)
                raw = raw_of(a)[:, half]
                m = a.maps
                dve.wait_ge(*a.po.emptied((b, a.units - 1)))
                link(nc.vector.reciprocal(rsum[:, 0:m].unsqueeze(2), raw[:, :, a.vw:a.vw + 1]))
                bc = rsum[:, 0:m].unsqueeze(2).to_broadcast([P, m, a.vw])
                if i >= 2:
                    a.pj.wait_full(dve, ("z", i - 2))
                if a.n == 1:
                    nc.vector.tensor_tensor(o_d[:, half, 0:D].rearrange("p (m w) -> p m w", w=a.vw), raw[:, :, 0:a.vw],
                                            bc, ALU.mult).then_inc(a.z, 1)
                    dve.wait_ge(a.z, i + 1)
                    return
                second = rsum[:, :].rearrange("p (v c r) -> p v c r", c=2, r=4)[:, :, 1, :]
                link(nc.vector.tensor_scalar(second, second, lam, None, ALU.mult))
                nc.vector.tensor_tensor(o_n, raw[:, :, 0:a.vw], bc, ALU.mult).then_inc(a.onorm, 1)
                dve.wait_ge(a.onorm, i + 1)
                maps = o_n.rearrange("p (v c r) w -> p v c (r w)", c=2, r=4)
                link(nc.vector.tensor_tensor(o_d[:, half, :].rearrange("p (v n) -> p v n", v=4), maps[:, :, 0],
                                             maps[:, :, 1], ALU.subtract))
                if half == HALVES - 1:
                    nc.vector.tensor_reduce(gn_sum, o_d.rearrange("p h (m w) -> p (h m) w", w=32), AX_X, ALU.add)\
                        .then_inc(a.sums, 1)

            def by_head(x):
                return x.unsqueeze(1).unsqueeze(3).to_broadcast([P, HALVES, 16, 32])

            o_heads = o_d.rearrange("p h (m w) -> p h m w", w=32)
            squares = o_n.rearrange("p (h m) w -> p h m w", h=HALVES)

            def center(a, b):
                a.pj.wait_full(dve, ("mean", b))
                nc.vector.tensor_tensor(o_heads, o_heads, by_head(a.pj.bank(("mean", b))[:, 0:16]), ALU.subtract)\
                    .then_inc(a.pj.free["dve"], 1)
                dve.wait_ge(*a.pj.emptied(("mean", b)))
                link(nc.vector.tensor_tensor(squares, o_heads, o_heads, ALU.mult))
                nc.vector.tensor_reduce(gn_sum, o_n, AX_X, ALU.add).then_inc(a.sums, 1)

            def scale(a, b):
                a.pj.wait_full(dve, ("variance", b))
                nc.vector.tensor_scalar(gn_ve, a.pj.bank(("variance", b))[:, 0:16], EPS, None, ALU.add)\
                    .then_inc(a.pj.free["dve"], 1)
                dve.wait_ge(*a.pj.emptied(("variance", b)))
                dve.wait_ge(a.gpow, b + 1)
                newton(gn_rs, gn_ve, gn_t)
                gw = o_n.rearrange("p a b -> p (a b)")[:, 0:2 * D]
                link(nc.vector.tensor_tensor(gw.rearrange("p (m w) -> p m w", w=32),
                                             gn[:, 0, :].rearrange("p (m w) -> p m w", w=32),
                                             gn_rs.unsqueeze(2).to_broadcast([P, 16, 32]), ALU.mult))
                link(nc.vector.tensor_tensor(o_d, o_d, gw.unsqueeze(1).to_broadcast([P, HALVES, 2 * D]), ALU.mult))
                nc.vector.tensor_tensor(o_d, o_d, gn[:, 1, :].unsqueeze(1).to_broadcast([P, HALVES, 2 * D]), ALU.add)\
                    .then_inc(a.z, 1)

            def attention(a, dst):
                nc.vector.memset(qkT[STACK:P, :, a.maps:a.groups, :], 1.0).then_inc(a.ones, 1)
                w = a.vw + 1
                v = vaug[:, :, :, 0:a.vheads * w]
                for b in range(2):
                    for half in range(HALVES):
                        nc.vector.memset(vaug_of(a, b)[:, half, :, a.vw:w], 1.0)
                for kind, w in a.steps:
                    if kind == "project":
                        project(a, w)
                    elif kind == "max":
                        row_max(a, *w)
                    elif kind == "divide":
                        divide(a, w)
                    elif kind == "mean":
                        center(a, w)
                    elif kind == "variance":
                        scale(a, w)
                    elif kind == "out":
                        a.pj.wait_full(dve, ("o", w))
                        src = a.pj.bank(("o", w))[:, 0:D]
                        if a.n == 0:
                            nc.vector.tensor_copy(dst[:, w, :], src).then_inc(a.pj.free["dve"], 1)
                        else:
                            nc.vector.tensor_tensor(dst[:, w, :], src, bo, ALU.add).then_inc(a.pj.free["dve"], 1)

            dve.wait_ge(ld["cst"], 32)
            nc.vector.tensor_copy(identb[:, :], ident).then_inc(s_cast, 1)
            for dst, at in ((neg_ts, C_NEG1), (neg_st, C_NEG2), (triu, C_TRIU)):
                nc.vector.tensor_copy(dst[:, :], masks[:, at - C_KEPT:at - C_KEPT + P]).then_inc(s_cast, 1)

            def x_loaded(i):
                if i == 0:
                    dve.wait_ge(ld["x"], 16)

            layer_norm(norms[0], x_in, xn, x_loaded)

            dve.wait_ge(ld["lam"], 16)
            link(nc.vector.tensor_tensor(lamv[:, 0::2, :], lamv[:, 0::2, :], lamv[:, 1::2, :], ALU.mult))
            nc.vector.tensor_reduce(lam2, lamv[:, 0::2, :], AX_X, ALU.add).then_inc(s_lamx, 1)

            v, over = softmax(norms[0], E0, banks[2])
            dve.wait_ge(s_lame, 1)
            link(nc.vector.tensor_tensor(lam, lamx[:, 0:1], lamx[:, 1:2], ALU.subtract))
            link(nc.vector.tensor_scalar(lam, lam, LAMBDA_INIT, None, ALU.add))
            first_largest(v, over, E0, v(1), v(3))
            link(nc.vector.scalar_tensor_tensor(out=v(4), in0=v(3), scalar=-2.0, in1=v(1), op0=ALU.mult, op1=ALU.add))
            first_largest(v, over, E0, v(4), v(0))
            link(nc.vector.tensor_tensor(v(3), v(3), v(0), ALU.add))
            nc.vector.memset(route[:, :, E0:], 1.0)
            nc.vector.tensor_tensor(route[:, :, 0:E0], v(3), v(1), ALU.mult).then_inc(norms[0].routed, 1)
            dve.wait_ge(ld["gn"], 16)
            dve.wait_ge(norms[0].routed, 1)
            attention(attns[0], xres)

            for n in range(N0 + 2):
                if n < N0:
                    if n >= 2:
                        m0.ht.wait_full(dve, n - 2)
                    dve.wait_ge(m0.silu, n + 1)
                    nc.vector.tensor_tensor(hid[:, n % 2, :], silu_a[:, n % 2, :], m0.up.bank(n)[:, F0:2 * F0], ALU.mult)\
                        .then_inc(m0.up.free["dve"], 1)
                if n >= 2:
                    e, t = divmod(n - 2, TILES)
                    m0.dn.wait_full(dve, n - 2)
                    src = m0.dn.bank(n - 2)[:, 0:D]
                    w = route[:, t, e:e + 1]
                    if e == 0:
                        nc.vector.tensor_scalar(acc[:, t, :], src, w, None, ALU.mult).then_inc(m0.dn.free["dve"], 1)
                    else:
                        dve.wait_ge(*m0.dn.emptied(n - 2 - TILES))
                        nc.vector.scalar_tensor_tensor(out=acc[:, t, :], in0=src, scalar=w, in1=acc[:, t, :],
                                                       op0=ALU.mult, op1=ALU.add).then_inc(m0.dn.free["dve"], 1)

            def gated(m, scale, base):
                def one(i):
                    dve.wait_ge(m.g, i + 1)
                    src, add = base(i)
                    link(nc.vector.scalar_tensor_tensor(out=gval[:, i, :], in0=src, scalar=scale, in1=gval[:, i, :],
                                                        op0=ALU.mult, op1=ALU.mult))
                    nc.vector.tensor_tensor(xres[:, i, :], gval[:, i, :], add, ALU.add).then_inc(m.x, 1)
                    dve.wait_ge(m.x, i + 1)
                return one

            dve.wait_ge(ld["x2"], 16)
            layer_norm(norms[1], xres, xn1,
                       gated(m0, 1.0 - LAMBDA_INIT, lambda i: (xres[:, i, :], x_again[:, i, :])))
            v, over = softmax(norms[1], E1, banks[2])
            first_largest(v, over, E1, v(2), v(3))
            hot = sc[:, 5, :].bitcast(BF16)[:, 0:TILES * E1]
            nc.vector.tensor_copy(hot, sc[:, 3, 0:TILES * E1]).then_inc(norms[1].hot, 1)
            link(nc.vector.tensor_tensor(v(3), v(3), v(1), ALU.mult))
            dve.wait_ge(norms[1].cum, 1)
            link(nc.vector.tensor_scalar(sc[:, 4, 0:TILES * E1], banks[3][:, 0:TILES * E1], CAPACITY + 0.5, None, ALU.is_lt))
            nc.vector.tensor_tensor(route1[:, :, :], v(3), v(4), ALU.mult).then_inc(norms[1].routed, 1)
            dve.wait_ge(norms[1].routed, 1)
            dve.wait_ge(ld["bias"], 32)
            attention(attns[1], s1)
            for n in range(N1):
                e, half = divmod(n, 2)
                for u in range(4):
                    t = 4 * half + u
                    m1.dn.wait_full(dve, (n, u))
                    src = m1.dn.bank((n, u))[:, 0:D]
                    w = route1[:, t, e:e + 1]
                    if e == 0:
                        nc.vector.tensor_scalar(acc[:, t, :], src, w, None, ALU.mult).then_inc(m1.dn.free["dve"], 1)
                    else:
                        nc.vector.scalar_tensor_tensor(out=acc[:, t, :], in0=src, scalar=w, in1=acc[:, t, :],
                                                       op0=ALU.mult, op1=ALU.add).then_inc(m1.dn.free["dve"], 1)
            one = gated(m1, 1.0, lambda i: (s1[:, i, :], xres[:, i, :]))
            for i in range(TILES):
                one(i)


def kernel(**inputs):
    import concourse.bacc as bacc
    from concourse.bass_utils import run_bass_kernel_spmd as run

    def f(name):
        return np.asarray(inputs[name])

    def kt(a, parts=P):
        return a.reshape(a.shape[0] // parts, parts, a.shape[1]).transpose(1, 0, 2)

    H, KV = 16, 4
    rep = H // KV
    even_odd = np.concatenate([np.arange(0, DH, 2), np.arange(1, DH, 2)])
    wq = f("L0_attn_Wq").reshape(D, KV, rep, 2, DH)[..., even_odd].transpose(0, 1, 3, 2, 4).reshape(D, 2 * D)
    wk = f("L0_attn_Wk").reshape(D, KV, 2, DH)[..., even_odd].reshape(D, D // 2)
    w1, w3, w2 = f("L0_ffn_w1"), f("L0_ffn_w3"), f("L0_ffn_w2")
    up = np.concatenate([w1, w3], axis=1)
    down = w2.transpose(0, 2, 1)
    sw1, sw3, sw2 = (f("L0_ffn_" + n) for n in ("sw1", "sw3", "sw2"))
    sup = np.concatenate([sw1.reshape(SHARED, F0, D), sw3.reshape(SHARED, F0, D)], axis=1)
    sdown = sw2.T.reshape(SHARED, F0, D)
    up = np.concatenate([up, sup]).transpose(0, 2, 1).reshape(EXPERTS0, KD, P, 2 * F0).transpose(2, 0, 1, 3)
    down = np.concatenate([down, sdown]).reshape(EXPERTS0, 2, FH, D).transpose(2, 0, 1, 3)
    arrays = {
        "x": f("L0_attn_x").reshape(-1, D),
        "consts": constants(),
        "wqkv0": kt(np.concatenate([wq, wk, f("L0_attn_Wv")], axis=1)),
        "wo0": kt(f("L0_attn_Wo")),
        "lam": np.stack([f("L0_attn_lambda_" + n) for n in ("q1", "k1", "q2", "k2")]),
        "gn": np.stack([f("L0_attn_gn_w"), f("L0_attn_gn_b")]),
        "gate0": kt(f("L0_ffn_gate_w").T),
        "w13": up,
        "w2": down,
        "wqkv1": kt(f("L1_attn_Wqkv").T),
        "bqkv": f("L1_attn_bqkv"),
        "wo1": kt(f("L1_attn_Wo").T),
        "bo": f("L1_attn_bo"),
        "gate1": kt(f("L1_ffn_gate_weight").T),
        "f1a": f("L1_ffn_w1").reshape(E1, KD, P, F1).transpose(2, 0, 1, 3),
        "f1b": f("L1_ffn_w2").reshape(E1, F1 // P, P, D).transpose(2, 0, 1, 3),
    }
    arrays = {n + "_in": np.ascontiguousarray(a) for n, a in arrays.items()}
    nc = bacc.Bacc("TRN2", target_bir_lowering=False, num_devices=1)
    args = [nc.dram_tensor(n, a.shape, F32, kind="ExternalInput").ap() for n, a in arrays.items()]
    out = nc.dram_tensor("out", (BATCH * SEQ, D), F32, kind="ExternalOutput").ap()
    program(nc, *args, out)
    r = run(nc, [arrays], core_ids=[0])
    return r.results[0]["out"].reshape(BATCH, SEQ, D)
```

```python
from contextlib import ExitStack

import concourse.bass as bass
from concourse import mybir
import numpy as np

P = 128
ALU = mybir.AluOpType
ACT = mybir.ActivationFunctionType
F32 = mybir.dt.float32
I32 = mybir.dt.int32
U32 = mybir.dt.uint32
BF16 = mybir.dt.bfloat16
AX_X = mybir.AxisListType.X

BATCH, SEQ, D = 4, 256, 256
TILES = BATCH * SEQ // P
HALVES = SEQ // P
KD = D // P
DH = 16
EPS = 1e-5
LAMBDA_INIT = 0.2
MASKED = -1e30
PARTS = 3
STACK = 6 * DH
DEEP = STACK + PARTS
SCALE = DH ** -0.5

E0, SHARED, F0 = 16, 2, 176
EXPERTS0 = E0 + SHARED
FH = F0 // 2
TOP = 2
TOKENS = BATCH * SEQ
SLOT_TILES0 = (TOP * TOKENS + E0 * (P - 1)) // P
E1, F1 = 8, 256
CAPACITY = 160
SLOTS1 = E1 * CAPACITY
SLOT_TILES1 = SLOTS1 // P

ROPE_COLS = HALVES * 2 * DH
C_IDENT, C_ROPE = 0, P
C_IOTA = C_ROPE + 2 * ROPE_COLS
C_SLOT1 = C_IOTA + E0
C_SPARE = C_SLOT1 + E1
C_NEG1 = C_KEPT = C_SPARE + TILES
C_NEG2, C_TRIU = C_NEG1 + P, C_NEG1 + 2 * P
C_FILLED = C_TRIU + P
C_BEFORE = C_FILLED + TILES
C_TILE = C_BEFORE + E0 * E0
C_COLS = C_TILE + SLOT_TILES0


def constants():
    c = np.zeros((P, C_COLS), np.float32)
    r = np.arange(P)
    c[:, C_IDENT:C_IDENT + P] = np.eye(P)
    c[:, C_NEG1:C_NEG1 + P] = np.where(r[None, :] > r[:, None], MASKED, 0.0)
    c[:, C_NEG2:C_NEG2 + P] = np.where(r[:, None] > r[None, :], MASKED, 0.0)
    c[:, C_TRIU:C_TRIU + P] = r[:, None] <= r[None, :]
    pos = np.arange(SEQ, dtype=np.float32)
    inv = (np.float32(1.0) / np.power(np.float32(10000.0), np.arange(0, DH, 2, dtype=np.float32) / np.float32(DH))).astype(np.float32)
    theta = np.power(np.float32(10000.0), (-np.power(np.float32(2.0), np.arange(DH // 2, dtype=np.float32)) / np.float32(DH)).astype(np.float32)).astype(np.float32)
    for layer, ang in enumerate((pos[:, None] * inv, (pos + 1)[:, None] * theta)):
        cos, sin = np.cos(ang.astype(np.float32)), np.sin(ang.astype(np.float32))
        t = np.concatenate([cos, cos, -sin, sin], axis=1).reshape(HALVES, P, 2 * DH)
        at = C_ROPE + layer * ROPE_COLS
        c[:, at:at + ROPE_COLS] = t.transpose(1, 0, 2).reshape(P, ROPE_COLS)
    c[:, C_IOTA:C_IOTA + E0] = E0 - np.arange(E0)
    c[:, C_SLOT1:C_SLOT1 + E1] = CAPACITY * np.arange(E1) - 1
    c[:, C_SPARE:C_SPARE + TILES] = SLOTS1 + P * np.arange(TILES) + r[:, None]
    c[:, C_FILLED:C_FILLED + TILES] = P * np.arange(TILES)
    c[:, C_BEFORE:C_BEFORE + E0 * E0] = np.tril(np.ones((E0, E0)), -1).reshape(-1)
    c[:, C_TILE:C_TILE + SLOT_TILES0] = np.arange(SLOT_TILES0)
    return c


class Stage:
    pass


class Ring:

    def __init__(self, banks, full, **free):
        self.banks, self.full, self.free, self.order, self.at = banks, full, free, [], {}

    def plan(self, key, engine):
        ordinal = 1 + sum(e == engine for e, _ in self.order)
        self.at[key] = len(self.order)
        self.order.append((engine, ordinal))

    def bank(self, key):
        return self.banks[self.at[key] % len(self.banks)]

    def wait_free(self, pe, key):
        before = self.at[key] - len(self.banks)
        if before >= 0:
            engine, ordinal = self.order[before]
            pe.wait_ge(self.free[engine], ordinal)

    def wait_full(self, eng, key):
        eng.wait_ge(self.full, self.at[key] + 1)

    def emptied(self, key):
        engine, ordinal = self.order[self.at[key]]
        return self.free[engine], ordinal

    def wait_drained(self, pe):
        for name, s in self.free.items():
            n = sum(e == name for e, _ in self.order)
            if n:
                pe.wait_ge(s, n)


def program(nc, x_d, consts_d, wqkv0_d, wo0_d, lam_d, gn_d, gate0_d, w13_d, w2_d,
            wqkv1_d, bqkv_d, wo1_d, bo_d, gate1_d, f1a_d, f1b_d, out_d, x0_slots_d, y0_slots_d, x1_slots_d, y1_slots_d):
    with ExitStack() as ctx:
        def sb(name, shape, dt=F32):
            return ctx.enter_context(nc.sbuf_tensor(name, shape, dt))

        def sem(name):
            return ctx.enter_context(nc.semaphore(name))

        banks = [ctx.enter_context(nc.psum_tensor(f"bank{i}", [P, 512], F32)) for i in range(8)]

        class Arena:

            def __init__(self, name, words):
                self.t, self.words, self.at = sb(name, [P, words]), words, 0

            def piece(self, shape, dt=F32):
                n = int(np.prod(shape))
                words = n if dt == F32 else (n + 1) // 2
                assert self.at + words <= self.words, (self.at, words, self.words)
                v = self.t[:, self.at:self.at + words]
                self.at += words
                if dt != F32:
                    v = v.bitcast(dt)
                if len(shape) > 1:
                    names = "abcdef"[:len(shape)]
                    v = v.rearrange(f"p ({' '.join(names)}) -> p {' '.join(names)}", **dict(zip(names, shape)))
                return v

            def restart(self):
                self.at = 0

        cst = sb("cst", [P, C_KEPT])
        ident = cst[:, C_IDENT:C_IDENT + P]
        iota = cst[:, C_IOTA:C_IOTA + E0]
        identb = sb("identb", [P, P], BF16)
        neg_ts = sb("neg_ts", [P, P], BF16)
        neg_st = sb("neg_st", [P, P], BF16)
        triu = sb("triu", [P, P], BF16)
        ones = sb("ones", [P, P], BF16)
        head_mean = sb("head_mean", [P, P])
        xnT = sb("xnT", [P, KD, TILES, P])
        xres = sb("xres", [P, TILES, D])
        wqkv = sb("wqkv", [P, KD, 3 * D])
        wo = sb("wo", [P, 4, D])
        gate = sb("gate", [P, KD, E0])
        gate1 = sb("gate1", [P, KD, E1])
        lamv = sb("lamv", [P, 4, DH])
        gn = sb("gn", [P, 2, 2 * D])
        gn_flat = gn[:, :, :].rearrange("p a n -> p (a n)")
        bqkv, bo = gn_flat[:, 0:3 * D], gn_flat[:, 3 * D:4 * D]
        small = sb("small", [P, 256])
        slot0 = sb("slot0", [P, TILES, TOP], U32)
        weight0 = sb("weight0", [P, TILES, TOP])
        tile_expert = sb("tile_expert", [P, SLOT_TILES0], I32)
        slot1_in = sb("slot1_in", [P, TILES], U32)
        slot1_out = sb("slot1_out", [P, TILES], U32)
        weight1 = sb("weight1", [P, TILES])

        moe = Arena("moe", EXPERTS0 * KD * (2 * F0 + D))
        w13 = moe.piece([EXPERTS0, KD, 2 * F0])
        w2 = moe.piece([EXPERTS0, 2, D])
        moe.restart()
        f1a = moe.piece([E1, KD, F1])
        f1b = moe.piece([E1, F1 // P, D])
        s1 = moe.piece([TILES, D])
        xs1 = moe.piece([SLOT_TILES1, D])
        xs1T = moe.piece([KD, SLOTS1])
        gelT = moe.piece([2, F1 // P, CAPACITY])
        ys1 = moe.piece([2, 2, D])

        work = Arena("work", 22144)
        x_in = work.piece([TILES, D])
        xn = xres[:, :, :]
        masks = work.piece([C_COLS - C_KEPT])
        zeros = work.piece([D])
        tally = work.piece([SLOT_TILES0 * E0])
        work.restart()
        qkT = work.piece([2, 40, SEQ], BF16)
        stack = work.piece([40, 6, DH], BF16)
        rotary = work.piece([2 * 40 * DH])
        rot_a, rot_b = (rotary[:, k * 40 * DH:(k + 1) * 40 * DH].rearrange("p (g d) -> p g d", d=DH) for k in range(2))
        rot_x = work.piece([32, DH])
        o_n = rotary[:, 0:32 * 32].rearrange("p (m w) -> p m w", w=32)
        pT = [work.piece([512]) for _ in range(6)]
        vaug = work.piece([2, HALVES, 16 * 17])
        o_raw = work.piece([HALVES, 32 * 33])
        o_d = work.piece([HALVES, 2 * D])
        zT = work.piece([4, P])
        nmax = work.piece([32])
        nmax_r = work.piece([32])
        nparts = work.piece([2, PARTS * 32], BF16)
        nT = work.piece([2, P], BF16)
        rsum = work.piece([32])
        work.restart()
        x_again = work.piece([TILES, D])
        acc = work.piece([TILES, D])
        silu_a = work.piece([2, F0])
        hid = work.piece([2, F0])
        hidT = work.piece([2, 2, P])
        xs = work.piece([4, D])
        xsT = work.piece([2, KD, P])
        ys = work.piece([4, D])
        y_back = work.piece([TILES, TOP, D])
        gval = work.piece([TILES, D])
        xn1 = work.piece([TILES, D])
        sc = work.piece([6, TILES * E0])

        ld = {n: sem("ld_" + n) for n in ("x", "cst", "wqkv", "wo", "gate", "lam", "gn", "bias", "w13", "w2",
                                          "x2", "wqkv1", "wo1", "f1")}
        out_sem = sem("out_sem")
        filled = sem("filled")
        zeroed = sem("zeroed")
        sent0, sent1 = sem("sent0"), sem("sent1")
        xs_loaded = [sem(f"xs_loaded{k}") for k in range(4)]
        ys_stored = [sem(f"ys_stored{k}") for k in range(4)]
        xs1_loaded = sem("xs1_loaded")
        ys1_stored = [sem(f"ys1_stored{k}") for k in range(2)]
        back0, back1 = sem("back0"), sem("back1")
        dve_c, act_c, pool_c = sem("dve_chain"), sem("act_chain"), sem("pool_chain")
        s_cast = sem("s_cast")
        s_ones = sem("s_ones")
        s_lamx, s_lame = sem("s_lamx"), sem("s_lame")

        def norm_state(n):
            q = Stage()
            q.n = n
            q.tp = Ring(banks[0:2], sem(f"ln{n}_tp_full"), act=sem(f"ln{n}_tp_free"))
            for g in range(TILES // 2):
                q.tp.plan(g, "act")
            q.veps, q.pow = sem(f"ln{n}_veps"), sem(f"ln{n}_pow")
            q.xn = sem(f"ln{n}_xn")
            q.logits = sem(f"ln{n}_logits")
            q.routed, q.expin, q.expd = sem(f"ln{n}_routed"), sem(f"ln{n}_expin"), sem(f"ln{n}_expd")
            q.hot, q.cum = sem(f"ln{n}_hot"), sem(f"ln{n}_cum")
            return q

        norms = [norm_state(0), norm_state(1)]
        stats = small[:, 0:TILES * 6].rearrange("p (t s) -> p t s", s=6)
        mv = small[:, 48:64].rearrange("p (t s) -> p t s", s=2)
        veps, rstd, tmp8 = small[:, 64:72], small[:, 72:80], small[:, 80:88]
        r16, r32 = small[:, 120:168].rearrange("p (k e) -> p k e", e=16), small[:, 168:200]
        r8a, r8b = small[:, 96:104], small[:, 104:112]
        lam2, lamx, lam = small[:, 112:114], small[:, 114:116], small[:, 116:117]
        gn_sum, gn_ve, gn_rs, gn_t = small[:, 120:152], small[:, 152:168], small[:, 168:184], small[:, 184:200]
        minus_half16 = small[:, 200:216]

        def attention_state(n, maps, kgroups, vheads, vwidth, kof, vof):
            a = Stage()
            a.n, a.maps, a.units, a.kgroups, a.groups = n, maps, maps // 4, kgroups, maps + kgroups
            a.vheads, a.vw, a.kof, a.vof = vheads, vwidth, kof, vof
            a.tgroups = a.groups // 8
            a.zchunks = vheads * vwidth * (4 if n == 0 else 1) // P
            p = f"a{n}_"
            a.pj = Ring(banks[0:2], sem(p + "pj_full"), act=sem(p + "pj_free_act"), dve=sem(p + "pj_free_dve"))
            a.s = Ring(banks[2:4], sem(p + "s_full"), dve=sem(p + "s_free"))
            a.st = Ring(banks[4:7], sem(p + "st_full"), act=sem(p + "st_free"))
            a.po = Ring(banks[7:8], sem(p + "po_full"), act=sem(p + "po_free_act"))
            a.stacked = sem(p + "stacked")
            a.nmax = sem(p + "nmax")
            a.rows = [sem(p + "rows0"), sem(p + "rows1")]
            a.ones = sem(p + "ones")
            a.sums = sem(p + "sums")
            a.gpow, a.z = sem(p + "gpow"), sem(p + "z")
            a.onorm = sem(p + "onorm") if n == 0 else a.z
            steps, u = [], a.units
            for b in range(BATCH + 2):
                slots = [[[], []] for _ in range(u + 1)]
                if b >= 2:
                    i0, i1 = 2 * b - 4, 2 * b - 3
                    slots[0][0] += [("divide", i0), ("divide", i1)]
                    slots[u * 3 // 4][1] += [("turn", i0), ("out", i0)]
                    slots[u][1] += [("turn", i1), ("out", i1)]
                    if n == 0:
                        slots[2][1] += [("mean", b - 2)]
                        slots[4][1] += [("variance", b - 2)]
                if b < BATCH:
                    slots[0][0] += [("project", 2 * b)]
                    second = [("parts", 2 * b), ("project", 2 * b + 1)]
                    if u == 8:
                        slots[1][0] += second
                    else:
                        slots[0][1] += second
                    slots[u // 4][0] += [("parts", 2 * b + 1)]
                    for q in range(3 * u):
                        slots[u // 4 + q // 4][1].insert(q % 4, ("max", (b, q)))
                    slots[u // 2 + 1][1] += [("rows", 2 * b)]
                    slots[u][1] += [("rows", 2 * b + 1)]
                for j, (before, after) in enumerate(slots):
                    steps += before
                    if 0 < b <= BATCH and j < u:
                        steps += [("exp", (b - 1, j))]
                    steps += after
                    if 0 < b <= BATCH and j > 0:
                        steps += [("value", (b - 1, j - 1))]
            a.steps = steps
            for kind, w in steps:
                if kind == "project":
                    a.pj.plan(("q", w), "dve")
                    a.pj.plan(("kv", w), "dve")
                elif kind == "parts":
                    for g in range(a.tgroups):
                        a.pj.plan(("t", w, g), "act")
                elif kind in ("mean", "variance"):
                    a.pj.plan((kind, w), "dve")
                elif kind == "turn":
                    a.pj.plan(("z", w), "act")
                elif kind == "out":
                    a.pj.plan(("o", w), "dve")
                elif kind == "max":
                    a.s.plan(w, "dve")
                elif kind == "exp":
                    for u in range(3):
                        a.st.plan((*w, u), "act")
                elif kind == "rows":
                    a.po.plan(("rows", w), "act")
                elif kind == "value":
                    a.po.plan(w, "act")
            return a

        attns = [attention_state(0, 32, 8, 4, 32, lambda m: m // 4, lambda m: m // 8),
                 attention_state(1, 16, 16, 16, 16, lambda m: m, lambda m: m)]

        def rope_tables(a, half):
            at = C_ROPE + a.n * ROPE_COLS + half * 2 * DH
            return cst[:, at:at + DH], cst[:, at + DH:at + 2 * DH]

        def max_use(a, q):
            return (0, range(4 * q, 4 * q + 4)) if q < a.units else (1, range(2 * (q - a.units), 2 * (q - a.units) + 2))

        def vaug_of(a, b):
            w = a.vw + 1
            return vaug[:, b % 2, :, 0:a.vheads * w].rearrange("p h (v w) -> p h v w", w=w)

        def raw_of(a):
            w = a.vw + 1
            return o_raw[:, :, 0:a.maps * w].rearrange("p h (m w) -> p h m w", w=w)

        def bfv(bank):
            return bank[:, :].bitcast(BF16).rearrange("p (m t) -> p m t", t=P)

        m0 = Stage()
        m0.xt = Ring(banks[7:8], sem("m0_xt_full"), act=sem("m0_xsT"))
        m0.up = Ring(banks[0:3], sem("m0_up_full"), dve=sem("m0_hid"))
        m0.ht = Ring(banks[3:5], sem("m0_ht_full"), act=sem("m0_hidT"))
        m0.dn = Ring(banks[5:7], sem("m0_dn_full"), dve=sem("m0_dn_free"))
        m0.silu, m0.g, m0.x = sem("m0_silu"), sem("m0_g"), sem("m0_x")
        m0.sum = sem("m0_sum")
        N0 = SLOT_TILES0 + SHARED * TILES
        for n in range(N0):
            if n < SLOT_TILES0:
                m0.xt.plan(n, "act")
            m0.up.plan(n, "dve")
            m0.ht.plan(n, "act")
            m0.dn.plan(n, "dve")

        m1 = Stage()
        m1.xt = Ring(banks[6:8], sem("m1_xt_full"), act=sem("m1_xt_free"))
        m1.up = Ring(banks[0:3], sem("m1_up_full"), act=sem("m1_up_free"))
        m1.dn = Ring(banks[3:6], sem("m1_dn_full"), dve=sem("m1_dn_free"))
        m1.g, m1.x = sem("m1_g"), sem("m1_x")
        DN1 = ((0, P), (P, CAPACITY - P))
        for g in range(SLOT_TILES1 // 2):
            m1.xt.plan(g, "act")
        for e in range(E1):
            m1.up.plan(e, "act")
            for c in range(2):
                m1.dn.plan((e, c), "dve")

        block = ctx.enter_context(nc.Block())

        @block.sync
        def _(sp):
            sp.dma_start(x_in, x_d.rearrange("(t p) d -> p t d", p=P)).then_inc(ld["x"], 16)
            sp.dma_start(cst[:, :], consts_d[:, 0:C_KEPT]).then_inc(ld["cst"], 16)
            sp.dma_start(masks, consts_d[:, C_KEPT:]).then_inc(ld["cst"], 16)
            sp.dma_start(wqkv[:, :, :], wqkv0_d).then_inc(ld["wqkv"], 16)
            sp.dma_start(gate[:, :, :], gate0_d).then_inc(ld["gate"], 16)
            sp.dma_start(gate1[:, :, :], gate1_d).then_inc(ld["gate"], 16)
            sp.dma_start(lamv[:, :, :], lam_d.partition_broadcast(P)).then_inc(ld["lam"], 16)
            sp.dma_start(gn[:, :, :], gn_d.partition_broadcast(P)).then_inc(ld["gn"], 16)
            sp.dma_start(wo[:, :, :], wo0_d).then_inc(ld["wo"], 16)
            sp.wait_ge(zeroed, 1)
            for j in range(SLOT_TILES0):
                sp.dma_start(x0_slots_d[j * P:j * P + P, :], zeros).then_inc(filled, 16)
            for j in range(SLOT_TILES1):
                sp.dma_start(x1_slots_d[j * P:j * P + P, :], zeros).then_inc(filled, 16)
            for e in range(0, EXPERTS0, 3):
                sp.dma_start(w13[:, e:e + 3], w13_d[:, e:e + 3]).then_inc(ld["w13"], 16)
            for e in range(0, EXPERTS0, 6):
                sp.dma_start(w2[0:FH, e:e + 6], w2_d[:, e:e + 6]).then_inc(ld["w2"], 16)

            def maximum_rows(a):
                for i in range(TILES):
                    b, half = divmod(i, HALVES)
                    sp.wait_ge(*a.po.emptied(("rows", i)))
                    if b >= 2:
                        sp.wait_ge(a.st.full, a.st.at[(b - 2, a.units - 1, 2)] + 1)
                    for k in range(PARTS):
                        sp.dma_start(qkT[STACK + k:STACK + k + 1, b % 2, 0:a.maps, half * P:half * P + P],
                                     nT[k * a.maps:(k + 1) * a.maps, i % 2, :]).then_inc(a.rows[b % 2], 16)

            maximum_rows(attns[0])
            sp.wait_ge(*attns[0].pj.emptied(("o", TILES - 1)))
            sp.dma_start(x_again, x_d.rearrange("(t p) d -> p t d", p=P)).then_inc(ld["x2"], 16)
            sp.dma_start(wqkv[:, :, :], wqkv1_d).then_inc(ld["wqkv1"], 16)
            sp.dma_start(wo[:, 0:2, :], wo1_d).then_inc(ld["wo1"], 16)
            sp.dma_start(bqkv, bqkv_d.partition_broadcast(P)).then_inc(ld["bias"], 16)
            sp.dma_start(bo, bo_d.partition_broadcast(P)).then_inc(ld["bias"], 16)
            sp.wait_ge(sent0, 16 * TOP * TILES)
            for n in range(SLOT_TILES0 + 5):
                if n < SLOT_TILES0:
                    if n >= 4:
                        m0.xt.wait_full(sp, n - 4)
                    sp.dma_start(xs[:, n % 4, :], x0_slots_d[n * P:n * P + P, :]).then_inc(xs_loaded[n % 4], 16)
                if n >= 5:
                    j = n - 5
                    sp.wait_ge(*m0.dn.emptied(j))
                    sp.dma_start(y0_slots_d[j * P:j * P + P, :], ys[:, j % 4, :]).then_inc(ys_stored[j % 4], 16)
            m0.dn.wait_full(sp, N0 - 1)
            sp.dma_start(f1a, f1a_d).then_inc(ld["f1"], 16)
            sp.dma_start(f1b, f1b_d).then_inc(ld["f1"], 16)
            sp.wait_ge(sent1, 16 * TILES)
            sp.dma_start(xs1, x1_slots_d[0:SLOTS1, :].rearrange("(t p) d -> p t d", p=P)).then_inc(xs1_loaded, 16)
            maximum_rows(attns[1])
            for e in range(E1):
                for c, (at, n) in enumerate(DN1):
                    sp.wait_ge(*m1.dn.emptied((e, c)))
                    row = e * CAPACITY + at
                    sp.dma_start(y1_slots_d[row:row + n, :], ys1[0:n, e % 2, c, :]).then_inc(ys1_stored[e % 2], 16)
            for i in range(TILES):
                sp.wait_ge(m1.x, i + 1)
                sp.dma_start(out_d[i * P:i * P + P, :], xres[:, i, :]).then_inc(out_sem, 16)
            sp.wait_ge(out_sem, 16 * TILES)

        @block.tensor
        def _(pe):
            def layer_norm(q, experts, g_sb, xn_t, out_bank):
                for g in range(TILES // 2):
                    q.tp.wait_free(pe, g)
                    bank = q.tp.bank(g)
                    for u in range(2):
                        i = 2 * g + u
                        pe.wait_ge(q.xn, i + 1)
                        for k in range(KD):
                            mm = nc.tensor.transpose(bank[:, (2 * u + k) * P:(2 * u + k + 1) * P],
                                                     xn_t[:, i, k * P:(k + 1) * P], ident)
                    mm.then_inc(q.tp.full, 1)
                pe.wait_ge(ld["gate"], 32)
                for i in range(TILES):
                    pe.wait_ge(*q.tp.emptied(i // 2))
                    for k in range(KD):
                        mm = nc.tensor.matmul(out_bank[:, i * experts:(i + 1) * experts], xnT[:, k, i, :],
                                              g_sb[:, k, :], start=(k == 0), stop=(k == KD - 1))
                mm.then_inc(q.logits, 1)

            def project(a, i):
                cols = {"q": slice(0, 512), "kv": slice(512, 768)}
                for use, n in (("q", 512), ("kv", 256)):
                    key = (use, i)
                    a.pj.wait_free(pe, key)
                    for k in range(KD):
                        mm = nc.tensor.matmul(a.pj.bank(key)[:, 0:n], xnT[:, k, i, :], wqkv[:, k, cols[use]],
                                              start=(k == 0), stop=(k == KD - 1))
                    mm.then_inc(a.pj.full, 1)

            def parts(a, i):
                pe.wait_ge(a.stacked, i + 1)
                for g in range(a.tgroups):
                    key = ("t", i, g)
                    a.pj.wait_free(pe, key)
                    for u in range(8):
                        mm = nc.tensor.transpose(bfv(a.pj.bank(key))[0:STACK, u, :],
                                                 stack[:, 8 * g + u].rearrange("p s d -> p (s d)"), identb[:, :])
                    mm.then_inc(a.pj.full, 1)

            def transposed(a, i):
                pe.wait_ge(*a.pj.emptied(("t", i, a.tgroups - 1)))

            def scores(a, b, q):
                half, ms = max_use(a, q)
                transposed(a, 2 * b + half)
                a.s.wait_free(pe, (b, q))
                bank = a.s.bank((b, q))
                n = P * (half + 1)
                view = bank[:, :].rearrange("p (m s) -> p m s", s=n)
                nc.tensor.matmul(view[:, :, half * P:half * P + P], identb[:, :],
                                 neg_ts[:, :].unsqueeze(1).to_broadcast([P, len(ms), P]),
                                 start=True, stop=False, skip_group_check=True)
                for u, m in enumerate(ms):
                    mm = nc.tensor.matmul(view[:, u, :], qkT[0:STACK, b % 2, m, half * P:half * P + P],
                                          qkT[0:STACK, b % 2, a.maps + a.kof(m), 0:n],
                                          start=False, stop=True, skip_group_check=True)
                mm.then_inc(a.s.full, 1)

            def exp_scores(a, b, j):
                pe.wait_ge(a.rows[b % 2], 16 * PARTS * HALVES * (b // 2 + 1))
                pe.wait_ge(a.ones, 1)
                for u in range(3):
                    key = (b, j, u)
                    a.st.wait_free(pe, key)
                    bank = a.st.bank(key)
                    if u < 2:
                        keys, ms, t0, n = 0, (4 * j + 2 * u, 4 * j + 2 * u + 1), 0, SEQ
                    else:
                        keys, ms, t0, n = 1, range(4 * j, 4 * j + 4), P, P
                    view = bank[:, :].rearrange("p (m t) -> p m t", t=n)
                    nc.tensor.matmul(view[:, :, 0:P], identb[:, :],
                                     neg_st[:, :].unsqueeze(1).to_broadcast([P, len(ms), P]),
                                     start=True, stop=False, skip_group_check=True)
                    for v, m in enumerate(ms):
                        mm = nc.tensor.matmul(view[:, v, :],
                                              qkT[0:DEEP, b % 2, a.maps + a.kof(m), keys * P:keys * P + P],
                                              qkT[0:DEEP, b % 2, m, t0:t0 + n],
                                              start=False, stop=True, skip_group_check=True)
                    mm.then_inc(a.st.full, 1)

            def rows(a, i):
                pe.wait_ge(a.nmax, i + 1)
                key = ("rows", i)
                a.po.wait_free(pe, key)
                n = PARTS * a.maps
                nc.tensor.transpose(bfv(a.po.bank(key))[0:n, 0, :], nparts[:, i % 2, 0:n], identb[:, :])\
                    .then_inc(a.po.full, 1)

            def value(a, b, j):
                key = (b, j)
                a.po.wait_free(pe, key)
                w = a.vw + 1
                out = a.po.bank(key)[:, 0:HALVES * 4 * w].rearrange("p (h m w) -> p h m w", h=HALVES, w=w)
                v = vaug_of(a, b)
                pe.wait_ge(*a.st.emptied((b, j, 2)))
                probs = [pT[a.st.at[(b, j, u)] % 6] for u in range(3)]
                for r in range(4):
                    vh = a.vof(4 * j + r)
                    p0 = probs[r // 2][:, (r % 2) * SEQ:(r % 2) * SEQ + SEQ]
                    nc.tensor.matmul(out[:, 0, r, :], p0[:, 0:P], v[:, 0, vh, :], start=True, stop=True)
                    nc.tensor.matmul(out[:, 1, r, :], p0[:, P:SEQ], v[:, 0, vh, :], start=True, stop=False)
                    mm = nc.tensor.matmul(out[:, 1, r, :], probs[2][:, r * P:r * P + P], v[:, 1, vh, :],
                                          start=False, stop=True)
                mm.then_inc(a.po.full, 1)

            def head_statistic(a, kind, b):
                key = (kind, b)
                pe.wait_ge(a.sums, 2 * b + (1 if kind == "mean" else 2))
                a.pj.wait_free(pe, key)
                for half in range(HALVES):
                    mm = nc.tensor.matmul(a.pj.bank(key)[:, 0:16], head_mean[:, :], gn_sum[:, 16 * half:16 * half + 16],
                                          start=(half == 0), stop=(half == HALVES - 1))
                mm.then_inc(a.pj.full, 1)

            def turn(a, i):
                pe.wait_ge(a.z, i + 1 if a.n == 1 else i // HALVES + 1)
                key = ("z", i)
                a.pj.wait_free(pe, key)
                for c in range(a.zchunks):
                    mm = nc.tensor.transpose(a.pj.bank(key)[:, c * P:(c + 1) * P], o_d[:, i % 2, c * P:(c + 1) * P], ident)
                mm.then_inc(a.pj.full, 1)

            def out(a, i):
                pe.wait_ge(*a.pj.emptied(("z", i)))
                pe.wait_ge(ld["wo" if a.n == 0 else "wo1"], 16)
                key = ("o", i)
                a.pj.wait_free(pe, key)
                for c in range(a.zchunks):
                    mm = nc.tensor.matmul(a.pj.bank(key)[:, 0:D], zT[:, c, :], wo[:, c, :],
                                          start=(c == 0), stop=(c == a.zchunks - 1))
                mm.then_inc(a.pj.full, 1)

            def attention(a):
                pe.wait_ge(ld["wqkv" if a.n == 0 else "wqkv1"], 16)
                for kind, w in a.steps:
                    if kind == "project":
                        project(a, w)
                    elif kind == "parts":
                        parts(a, w)
                    elif kind == "max":
                        scores(a, *w)
                    elif kind == "exp":
                        exp_scores(a, *w)
                    elif kind == "rows":
                        rows(a, w)
                    elif kind == "value":
                        value(a, *w)
                    elif kind in ("mean", "variance"):
                        head_statistic(a, kind, w)
                    elif kind == "turn":
                        turn(a, w)
                    elif kind == "out":
                        out(a, w)
                for ring in (a.pj, a.s, a.st, a.po):
                    ring.wait_drained(pe)

            def experts0():
                chosen = {}

                def turn_rows(n):
                    m0.xt.wait_free(pe, n)
                    pe.wait_ge(xs_loaded[n % 4], 16 * (n // 4 + 1))
                    for k in range(KD):
                        mm = nc.tensor.transpose(m0.xt.bank(n)[:, k * P:(k + 1) * P], xs[:, n % 4, k * P:(k + 1) * P], ident)
                    mm.then_inc(m0.xt.full, 1)

                def up(n):
                    m0.up.wait_free(pe, n)
                    if n < SLOT_TILES0:
                        e = pe.value_load(tile_expert[0:1, n:n + 1], min_val=0, max_val=E0 - 1)
                        chosen[n] = e
                        pe.wait_ge(*m0.xt.emptied(n))
                    for k in range(KD):
                        if n < SLOT_TILES0:
                            x_t, w = xsT[:, n % 2, k, :], w13[:, bass.ds(e, 1), k, :]
                        else:
                            t, part = divmod(n - SLOT_TILES0, SHARED)
                            x_t, w = xnT[:, k, t, :], w13[:, E0 + part, k, :]
                        mm = nc.tensor.matmul(m0.up.bank(n)[:, 0:2 * F0], x_t, w, start=(k == 0), stop=(k == KD - 1))
                    mm.then_inc(m0.up.full, 1)

                def turn_hidden(n):
                    pe.wait_ge(*m0.up.emptied(n))
                    m0.ht.wait_free(pe, n)
                    for f in range(2):
                        mm = nc.tensor.transpose(m0.ht.bank(n)[0:FH, f * P:(f + 1) * P],
                                                 hid[:, n % 2, f * FH:(f + 1) * FH], ident)
                    mm.then_inc(m0.ht.full, 1)

                def down(n):
                    pe.wait_ge(*m0.ht.emptied(n))
                    m0.dn.wait_free(pe, n)
                    for f in range(2):
                        if n < SLOT_TILES0:
                            w = w2[0:FH, bass.ds(chosen[n], 1), f, :]
                        else:
                            w = w2[0:FH, E0 + (n - SLOT_TILES0) % SHARED, f, :]
                        mm = nc.tensor.matmul(m0.dn.bank(n)[:, 0:D], hidT[0:FH, n % 2, f, :], w,
                                              start=(f == 0), stop=(f == 1))
                    mm.then_inc(m0.dn.full, 1)

                pe.wait_ge(ld["w13"], 16 * 6)
                pe.wait_ge(ld["w2"], 16 * 3)
                turn_rows(0)
                for n in range(N0 + 2):
                    if n + 1 < SLOT_TILES0:
                        turn_rows(n + 1)
                    if n < N0:
                        up(n)
                    if 1 <= n <= N0:
                        turn_hidden(n - 1)
                    if n >= 2:
                        down(n - 2)
                for ring in (m0.up, m0.ht, m0.dn):
                    ring.wait_drained(pe)

            def experts1():
                pe.wait_ge(xs1_loaded, 16)
                for g in range(SLOT_TILES1 // 2):
                    m1.xt.wait_free(pe, g)
                    for u in range(2):
                        for k in range(KD):
                            mm = nc.tensor.transpose(m1.xt.bank(g)[:, (2 * k + u) * P:(2 * k + u + 1) * P],
                                                     xs1[:, 2 * g + u, k * P:(k + 1) * P], ident)
                    mm.then_inc(m1.xt.full, 1)

                def up(e):
                    m1.up.wait_free(pe, e)
                    pe.wait_ge(*m1.xt.emptied(((e + 1) * CAPACITY - 1) // (2 * P)))
                    for m in range(F1 // P):
                        for k in range(KD):
                            mm = nc.tensor.matmul(m1.up.bank(e)[:, m * CAPACITY:(m + 1) * CAPACITY],
                                                  f1a[:, e, k, m * P:(m + 1) * P],
                                                  xs1T[:, k, e * CAPACITY:(e + 1) * CAPACITY],
                                                  start=(k == 0), stop=(k == KD - 1))
                    mm.then_inc(m1.up.full, 1)

                def down(e):
                    pe.wait_ge(*m1.up.emptied(e))
                    for c, (at, n) in enumerate(DN1):
                        m1.dn.wait_free(pe, (e, c))
                        for f in range(2):
                            mm = nc.tensor.matmul(m1.dn.bank((e, c))[0:n, 0:D], gelT[:, e % 2, f, at:at + n],
                                                  f1b[:, e, f, :], start=(f == 0), stop=(f == 1))
                        mm.then_inc(m1.dn.full, 1)

                pe.wait_ge(ld["f1"], 32)
                for e in range(E1 + 1):
                    if e < E1:
                        up(e)
                    if e:
                        down(e - 1)

            def ranks(q, experts):
                pe.wait_ge(q.hot, 1)
                hot = sc[:, 5, :].bitcast(BF16)[:, 0:TILES * experts]
                for i in range(TILES + 1):
                    for j in range(min(i + 1, TILES)):
                        mm = nc.tensor.matmul(banks[3][:, i * experts:(i + 1) * experts], (triu if j == i else ones)[:, :],
                                              hot[:, j * experts:(j + 1) * experts], start=(j == 0),
                                              stop=(j == min(i, TILES - 1)))
                mm.then_inc(q.cum, 1)

            pe.wait_ge(ld["cst"], 32)
            pe.wait_ge(s_cast, 4)
            layer_norm(norms[0], E0, gate, xn, banks[2])
            norms[0].tp.wait_drained(pe)
            ranks(norms[0], E0)
            pe.wait_ge(norms[0].routed, 1)
            attention(attns[0])
            experts0()
            layer_norm(norms[1], E1, gate1, xn1, banks[2])
            ranks(norms[1], E1)
            pe.wait_ge(norms[1].routed, 1)
            norms[1].tp.wait_drained(pe)
            attention(attns[1])
            experts1()

        @block.scalar
        def _(act):
            def copy(dst, src):
                return nc.scalar.activation(dst, src, ACT.Copy)

            def layer_norm(q, experts, out_bank):
                for g in range(TILES // 2):
                    q.tp.wait_full(act, g)
                    copy(xnT[:, :, 2 * g:2 * g + 2, :].rearrange("p k u t -> p u k t"),
                         q.tp.bank(g)[:, :].rearrange("p (u k t) -> p u k t", u=2, k=KD)).then_inc(q.tp.free["act"], 1)
                act.wait_ge(q.expin, 1)
                nc.scalar.activation(sc[:, 1, 0:TILES * experts], sc[:, 0, 0:TILES * experts], ACT.Exp)\
                    .then_inc(q.expd, 1)

            def attention(a):
                for kind, w in a.steps:
                    if kind == "parts":
                        b, half = divmod(w, HALVES)
                        if b >= 2:
                            act.wait_ge(a.st.full, a.st.at[(b - 2, a.units - 1, 2)] + 1)
                        for g in range(a.tgroups):
                            key = ("t", w, g)
                            a.pj.wait_full(act, key)
                            copy(qkT[0:STACK, b % 2, 8 * g:8 * g + 8, half * P:half * P + P],
                                 bfv(a.pj.bank(key))[0:STACK, :, :]).then_inc(a.pj.free["act"], 1)
                    elif kind == "rows":
                        b = w // HALVES
                        if w >= 2:
                            for p in range(2):
                                done = [i for i in range(w - 1) if (i // HALVES) % 2 == p]
                                if done:
                                    act.wait_ge(a.rows[p], 16 * PARTS * len(done))
                        a.po.wait_full(act, ("rows", w))
                        n = PARTS * a.maps
                        copy(nT[0:n, w % 2, :], bfv(a.po.bank(("rows", w)))[0:n, 0, :]).then_inc(a.po.free["act"], 1)
                    elif kind == "exp":
                        for u in range(3):
                            key = (*w, u)
                            at = a.st.at[key]
                            if at >= 6:
                                a.po.wait_full(act, divmod(at // 3 - 2, a.units))
                            a.st.wait_full(act, key)
                            nc.scalar.activation(pT[at % 6], a.st.bank(key)[:, :], ACT.Exp, scale=SCALE)\
                                .then_inc(a.st.free["act"], 1)
                    elif kind == "value":
                        b, j = w
                        if b >= 1:
                            act.wait_ge(a.onorm, HALVES * b)
                        a.po.wait_full(act, w)
                        n = a.vw + 1
                        copy(raw_of(a)[:, :, 4 * j:4 * j + 4, :],
                             a.po.bank(w)[:, 0:HALVES * 4 * n].rearrange("p (h m w) -> p h m w", h=HALVES, w=n))\
                            .then_inc(a.po.free["act"], 1)
                    elif kind == "turn":
                        if w:
                            a.pj.wait_full(act, ("o", w - 1))
                        a.pj.wait_full(act, ("z", w))
                        copy(zT[:, 0:a.zchunks, :], a.pj.bank(("z", w))[:, 0:a.zchunks * P]
                             .rearrange("p (c t) -> p c t", t=P)).then_inc(a.pj.free["act"], 1)

            layer_norm(norms[0], E0, banks[2])
            act.wait_ge(s_lamx, 1)
            nc.scalar.activation(lamx, lam2, ACT.Exp).then_inc(s_lame, 1)
            attention(attns[0])

            def rows_turned(n):
                m0.xt.wait_full(act, n)
                if n >= 2:
                    m0.up.wait_full(act, n - 2)
                copy(xsT[:, n % 2, :, :], m0.xt.bank(n)[:, 0:KD * P].rearrange("p (k t) -> p k t", t=P))\
                    .then_inc(m0.xt.free["act"], 1)

            rows_turned(0)
            for n in range(N0 + 1):
                if n + 1 < SLOT_TILES0:
                    rows_turned(n + 1)
                if n < N0:
                    m0.up.wait_full(act, n)
                    if n >= 2:
                        act.wait_ge(*m0.up.emptied(n - 2))
                    nc.scalar.activation(silu_a[:, n % 2, :], m0.up.bank(n)[:, 0:F0], ACT.Silu).then_inc(m0.silu, 1)
                if n:
                    m0.ht.wait_full(act, n - 1)
                    if n >= 3:
                        m0.dn.wait_full(act, n - 3)
                    copy(hidT[0:FH, (n - 1) % 2, :, :], m0.ht.bank(n - 1)[0:FH, 0:2 * P]
                         .rearrange("p (f t) -> p f t", t=P)).then_inc(m0.ht.free["act"], 1)
            for i in range(TILES):
                act.wait_ge(m0.sum, i + 1)
                nc.scalar.activation(gval[:, i, :], acc[:, i, :], ACT.Silu).then_inc(m0.g, 1)
            layer_norm(norms[1], E1, banks[2])
            attention(attns[1])
            for g in range(SLOT_TILES1 // 2):
                m1.xt.wait_full(act, g)
                copy(xs1T[:, :, 2 * g * P:2 * (g + 1) * P], m1.xt.bank(g)[:, :].rearrange("p (k t) -> p k t", k=KD))\
                    .then_inc(m1.xt.free["act"], 1)
            for e in range(E1):
                m1.up.wait_full(act, e)
                if e >= 2:
                    m1.dn.wait_full(act, (e - 2, 1))
                nc.scalar.activation(gelT[:, e % 2, :, :], m1.up.bank(e)[:, 0:F1 // P * CAPACITY]
                                     .rearrange("p (m t) -> p m t", t=CAPACITY), ACT.Gelu).then_inc(m1.up.free["act"], 1)
            act.wait_ge(back1, 16 * TILES)
            for i in range(TILES):
                nc.scalar.activation(gval[:, i, :], y_back[:, i, 0, :], ACT.Silu, scale=weight1[:, i:i + 1])\
                    .then_inc(m1.g, 1)

        @block.gpsimd
        def _(pool):
            nc.gpsimd.memset(zeros, 0.0).then_inc(zeroed, 1)
            nc.gpsimd.memset(ones[:, :], 1.0).then_inc(s_ones, 1)
            nc.gpsimd.memset(minus_half16, -0.5).then_inc(s_ones, 1)
            nc.gpsimd.memset(head_mean[:, :], 1.0 / (SEQ * 2 * DH)).then_inc(s_ones, 1)
            pool.wait_ge(s_ones, 3)

            def power(ready, n, done, dst, src, width):
                pool.wait_ge(ready, n)
                nc.gpsimd.tensor_tensor(dst, src, minus_half16[:, 0:width], ALU.pow).then_inc(done, 1)

            def attention(a):
                for kind, w in a.steps:
                    if kind == "variance":
                        power(*a.pj.emptied((kind, w)), a.gpow, gn_rs, gn_ve, 16)

            def send(slots_d, slot, src, done):
                nc.gpsimd.indirect_dma_start(slots_d, bass.IndirectOffsetOnAxis(ap=slot, axis=0), src, None)\
                    .then_inc(done, 16)

            def fetch(slots_d, slot, dst, done):
                nc.gpsimd.indirect_dma_start(dst, None, slots_d, bass.IndirectOffsetOnAxis(ap=slot, axis=0))\
                    .then_inc(done, 16)

            power(norms[0].veps, 1, norms[0].pow, rstd, veps, TILES)
            pool.wait_ge(filled, 16 * (SLOT_TILES0 + SLOT_TILES1))
            pool.wait_ge(norms[0].routed, 1)
            for i in range(TILES):
                for c in range(TOP):
                    send(x0_slots_d, slot0[:, i, c:c + 1], xn[:, i, :], sent0)
            attention(attns[0])
            for k in range(4):
                pool.wait_ge(ys_stored[k], 16 * len(range(k, SLOT_TILES0, 4)))
            for i in range(TILES):
                for c in range(TOP):
                    fetch(y0_slots_d, slot0[:, i, c:c + 1], y_back[:, i, c, :], back0)
            power(norms[1].veps, 1, norms[1].pow, rstd, veps, TILES)
            pool.wait_ge(norms[1].routed, 1)
            for i in range(TILES):
                send(x1_slots_d, slot1_in[:, i:i + 1], xn1[:, i, :], sent1)
            attention(attns[1])
            for k in range(2):
                pool.wait_ge(ys1_stored[k], 16 * E1)
            for i in range(TILES):
                fetch(y1_slots_d, slot1_out[:, i:i + 1], y_back[:, i, 0, :], back1)

        @block.vector
        def _(dve):
            chain = [0]

            def link(ins):
                chain[0] += 1
                ins.then_inc(dve_c, 1)
                dve.wait_ge(dve_c, chain[0])

            def newton(y, v, t):
                link(nc.vector.tensor_tensor(t, y, y, ALU.mult))
                link(nc.vector.tensor_tensor(t, t, v, ALU.mult))
                link(nc.vector.tensor_scalar(t, t, -0.5, 1.5, ALU.mult, ALU.add))
                link(nc.vector.tensor_tensor(y, y, t, ALU.mult))

            def layer_norm(q, x_t, xn_t, arrived):
                for i in range(TILES):
                    arrived(i)
                    link(nc.vector.bn_stats(stats[:, i, :], x_t[:, i, :]))
                    link(nc.vector.bn_aggr(mv[:, i, :], stats[:, i, :]))
                nc.vector.tensor_scalar(veps, mv[:, :, 1], EPS, None, ALU.add).then_inc(q.veps, 1)
                dve.wait_ge(q.pow, 1)
                newton(rstd, veps, tmp8)
                for i in range(TILES):
                    nc.vector.tensor_scalar(xn_t[:, i, :], x_t[:, i, :], mv[:, i, 0:1], rstd[:, i:i + 1],
                                            ALU.subtract, ALU.mult).then_inc(q.xn, 1)

            def softmax(q, experts, bank):
                n = TILES * experts

                def v(k):
                    return sc[:, k, 0:n].rearrange("p (t e) -> p t e", e=experts)

                def over(x):
                    return x.unsqueeze(2).to_broadcast([P, TILES, experts])

                dve.wait_ge(q.logits, 1)
                link(nc.vector.tensor_copy(sc[:, 2, 0:n], bank[:, 0:n]))
                link(nc.vector.tensor_reduce(r8a, v(2), AX_X, ALU.max))
                nc.vector.tensor_tensor(v(0), v(2), over(r8a), ALU.subtract).then_inc(q.expin, 1)
                dve.wait_ge(q.expd, 1)
                link(nc.vector.tensor_reduce(r8b, v(1), AX_X, ALU.add))
                link(nc.vector.reciprocal(r8b, r8b))
                link(nc.vector.tensor_tensor(v(1), v(1), over(r8b), ALU.mult))
                return v, over

            def first_largest(v, over, experts, src, dst):
                link(nc.vector.tensor_reduce(r8a, src, AX_X, ALU.max))
                link(nc.vector.tensor_tensor(dst, src, over(r8a), ALU.is_ge))
                count = iota[:, 0:experts].unsqueeze(1).to_broadcast([P, TILES, experts])
                link(nc.vector.tensor_tensor(dst, dst, count, ALU.mult))
                link(nc.vector.tensor_reduce(r8a, dst, AX_X, ALU.max))
                link(nc.vector.tensor_tensor(dst, dst, over(r8a), ALU.is_ge))

            def project(a, i):
                b, half = divmod(i, HALVES)
                cos, sin = rope_tables(a, half)
                nq = 32 if a.n == 0 else 32

                def rotate(src, g0, g1):
                    n = g1 - g0
                    nc.vector.tensor_tensor(rot_a[:, g0:g1, :], src, cos.unsqueeze(1).to_broadcast([P, n, DH]), ALU.mult)
                    h = DH // 2
                    nc.vector.tensor_tensor(rot_b[:, g0:g1, 0:h], src[:, :, h:DH],
                                            sin[:, 0:h].unsqueeze(1).to_broadcast([P, n, h]), ALU.mult)
                    return nc.vector.tensor_tensor(rot_b[:, g0:g1, h:DH], src[:, :, 0:h],
                                                   sin[:, h:DH].unsqueeze(1).to_broadcast([P, n, h]), ALU.mult)

                a.pj.wait_full(dve, ("q", i))
                first = a.pj.bank(("q", i))[:, :].rearrange("p (g d) -> p g d", d=DH)
                if a.n == 0:
                    rotate(first, 0, nq).then_inc(a.pj.free["dve"], 1)
                else:
                    nc.vector.tensor_tensor(rot_x, first, bqkv[:, 0:512].rearrange("p (g d) -> p g d", d=DH), ALU.add)\
                        .then_inc(a.pj.free["dve"], 1)
                    dve.wait_ge(*a.pj.emptied(("q", i)))
                    link(rotate(rot_x, 0, nq))
                a.pj.wait_full(dve, ("kv", i))
                second = a.pj.bank(("kv", i))
                v0 = 2 * D // 4 if a.n == 0 else 0
                if a.n == 0:
                    rotate(second[:, 0:v0].rearrange("p (g d) -> p g d", d=DH), nq, a.groups)
                vals = second[:, v0:v0 + a.vheads * a.vw].rearrange("p (v w) -> p v w", w=a.vw)
                if b >= 2:
                    a.po.wait_full(dve, (b - 2, a.units - 1))
                dst = vaug_of(a, b)[:, half, :, 0:a.vw]
                if a.n == 0:
                    nc.vector.tensor_copy(dst, vals).then_inc(a.pj.free["dve"], 1)
                else:
                    nc.vector.tensor_tensor(dst, vals, bqkv[:, 512:768].rearrange("p (v w) -> p v w", w=a.vw), ALU.add)\
                        .then_inc(a.pj.free["dve"], 1)
                dve.wait_ge(*a.pj.emptied(("kv", i)))
                ng, m = a.groups, a.maps
                link(nc.vector.tensor_tensor(rot_a[:, 0:ng, :], rot_a[:, 0:ng, :], rot_b[:, 0:ng, :], ALU.add))
                if i:
                    a.pj.wait_full(dve, ("t", i - 1, a.tgroups - 1))
                link(nc.vector.tensor_copy(stack[:, 0:ng, 0, :], rot_a[:, 0:ng, :]))
                link(nc.vector.tensor_tensor(rot_a[:, 0:ng, :], rot_a[:, 0:ng, :], stack[:, 0:ng, 0, :], ALU.subtract))
                nc.vector.tensor_copy(stack[:, 0:m, 1:3, :], stack[:, 0:m, 0:1, :].to_broadcast([P, m, 2, DH]))
                link(nc.vector.tensor_copy(stack[:, 0:ng, 4, :], rot_a[:, 0:ng, :]))
                nc.vector.tensor_copy(stack[:, m:ng, 3, :], stack[:, m:ng, 0, :])
                nc.vector.tensor_copy(stack[:, m:ng, 5, :], stack[:, m:ng, 0, :])
                nc.vector.tensor_copy(stack[:, 0:m, 3, :], stack[:, 0:m, 4, :])
                nc.vector.tensor_copy(stack[:, m:ng, 1, :], stack[:, m:ng, 4, :])
                nc.vector.tensor_tensor(stack[:, 0:m, 5, :], rot_a[:, 0:m, :], stack[:, 0:m, 4, :], ALU.subtract)
                nc.vector.tensor_tensor(stack[:, m:ng, 2, :], rot_a[:, m:ng, :], stack[:, m:ng, 4, :], ALU.subtract)\
                    .then_inc(a.stacked, 1)

            def row_max(a, b, q):
                half, ms = max_use(a, q)
                a.s.wait_full(dve, (b, q))
                n = P * (half + 1)
                nc.vector.tensor_reduce(nmax[:, ms[0]:ms[-1] + 1], a.s.bank((b, q))[:, :].rearrange("p (m s) -> p m s", s=n),
                                        AX_X, ALU.max, negate=True).then_inc(a.s.free["dve"], 1)
                last = a.units - 1 if half == 0 else 3 * a.units - 1
                if q != last:
                    return
                i = 2 * b + half
                m = a.maps
                dve.wait_ge(*a.s.emptied((b, q)))
                if i >= 2:
                    a.po.wait_full(dve, ("rows", i - 2))
                parts = nparts[:, i % 2, 0:PARTS * m].rearrange("p (k m) -> p k m", m=m)
                link(nc.vector.tensor_copy(parts[:, 0, :], nmax[:, 0:m]))
                link(nc.vector.tensor_tensor(nmax_r[:, 0:m], nmax[:, 0:m], parts[:, 0, :], ALU.subtract))
                link(nc.vector.tensor_copy(parts[:, 1, :], nmax_r[:, 0:m]))
                nc.vector.tensor_tensor(parts[:, 2, :], nmax_r[:, 0:m], parts[:, 1, :], ALU.subtract)\
                    .then_inc(a.nmax, 1)

            def divide(a, i):
                b, half = divmod(i, HALVES)
                raw = raw_of(a)[:, half]
                m = a.maps
                dve.wait_ge(*a.po.emptied((b, a.units - 1)))
                link(nc.vector.reciprocal(rsum[:, 0:m].unsqueeze(2), raw[:, :, a.vw:a.vw + 1]))
                bc = rsum[:, 0:m].unsqueeze(2).to_broadcast([P, m, a.vw])
                if i >= 2:
                    a.pj.wait_full(dve, ("z", i - 2))
                if a.n == 1:
                    nc.vector.tensor_tensor(o_d[:, half, 0:D].rearrange("p (m w) -> p m w", w=a.vw), raw[:, :, 0:a.vw],
                                            bc, ALU.mult).then_inc(a.z, 1)
                    dve.wait_ge(a.z, i + 1)
                    return
                second = rsum[:, :].rearrange("p (v c r) -> p v c r", c=2, r=4)[:, :, 1, :]
                link(nc.vector.tensor_scalar(second, second, lam, None, ALU.mult))
                nc.vector.tensor_tensor(o_n, raw[:, :, 0:a.vw], bc, ALU.mult).then_inc(a.onorm, 1)
                dve.wait_ge(a.onorm, i + 1)
                maps = o_n.rearrange("p (v c r) w -> p v c (r w)", c=2, r=4)
                link(nc.vector.tensor_tensor(o_d[:, half, :].rearrange("p (v n) -> p v n", v=4), maps[:, :, 0],
                                             maps[:, :, 1], ALU.subtract))
                if half == HALVES - 1:
                    nc.vector.tensor_reduce(gn_sum, o_d.rearrange("p h (m w) -> p (h m) w", w=32), AX_X, ALU.add)\
                        .then_inc(a.sums, 1)

            def by_head(x):
                return x.unsqueeze(1).unsqueeze(3).to_broadcast([P, HALVES, 16, 32])

            o_heads = o_d.rearrange("p h (m w) -> p h m w", w=32)
            squares = o_n.rearrange("p (h m) w -> p h m w", h=HALVES)

            def center(a, b):
                a.pj.wait_full(dve, ("mean", b))
                nc.vector.tensor_tensor(o_heads, o_heads, by_head(a.pj.bank(("mean", b))[:, 0:16]), ALU.subtract)\
                    .then_inc(a.pj.free["dve"], 1)
                dve.wait_ge(*a.pj.emptied(("mean", b)))
                link(nc.vector.tensor_tensor(squares, o_heads, o_heads, ALU.mult))
                nc.vector.tensor_reduce(gn_sum, o_n, AX_X, ALU.add).then_inc(a.sums, 1)

            def scale(a, b):
                a.pj.wait_full(dve, ("variance", b))
                nc.vector.tensor_scalar(gn_ve, a.pj.bank(("variance", b))[:, 0:16], EPS, None, ALU.add)\
                    .then_inc(a.pj.free["dve"], 1)
                dve.wait_ge(*a.pj.emptied(("variance", b)))
                dve.wait_ge(a.gpow, b + 1)
                newton(gn_rs, gn_ve, gn_t)
                gw = o_n.rearrange("p a b -> p (a b)")[:, 0:2 * D]
                link(nc.vector.tensor_tensor(gw.rearrange("p (m w) -> p m w", w=32),
                                             gn[:, 0, :].rearrange("p (m w) -> p m w", w=32),
                                             gn_rs.unsqueeze(2).to_broadcast([P, 16, 32]), ALU.mult))
                link(nc.vector.tensor_tensor(o_d, o_d, gw.unsqueeze(1).to_broadcast([P, HALVES, 2 * D]), ALU.mult))
                nc.vector.tensor_tensor(o_d, o_d, gn[:, 1, :].unsqueeze(1).to_broadcast([P, HALVES, 2 * D]), ALU.add)\
                    .then_inc(a.z, 1)

            def attention(a, dst):
                nc.vector.memset(qkT[STACK:P, :, a.maps:a.groups, :], 1.0).then_inc(a.ones, 1)
                w = a.vw + 1
                v = vaug[:, :, :, 0:a.vheads * w]
                for b in range(2):
                    for half in range(HALVES):
                        nc.vector.memset(vaug_of(a, b)[:, half, :, a.vw:w], 1.0)
                for kind, w in a.steps:
                    if kind == "project":
                        project(a, w)
                    elif kind == "max":
                        row_max(a, *w)
                    elif kind == "divide":
                        divide(a, w)
                    elif kind == "mean":
                        center(a, w)
                    elif kind == "variance":
                        scale(a, w)
                    elif kind == "out":
                        a.pj.wait_full(dve, ("o", w))
                        src = a.pj.bank(("o", w))[:, 0:D]
                        if a.n == 0 and w == 0:
                            dve.wait_ge(sent0, 16 * TOP * TILES)
                        if a.n == 0:
                            nc.vector.tensor_copy(dst[:, w, :], src).then_inc(a.pj.free["dve"], 1)
                        else:
                            nc.vector.tensor_tensor(dst[:, w, :], src, bo, ALU.add).then_inc(a.pj.free["dve"], 1)

            dve.wait_ge(ld["cst"], 32)
            nc.vector.tensor_copy(identb[:, :], ident).then_inc(s_cast, 1)
            for dst, at in ((neg_ts, C_NEG1), (neg_st, C_NEG2), (triu, C_TRIU)):
                nc.vector.tensor_copy(dst[:, :], masks[:, at - C_KEPT:at - C_KEPT + P]).then_inc(s_cast, 1)

            def x_loaded(i):
                if i == 0:
                    dve.wait_ge(ld["x"], 16)

            layer_norm(norms[0], x_in, xn, x_loaded)

            dve.wait_ge(ld["lam"], 16)
            link(nc.vector.tensor_tensor(lamv[:, 0::2, :], lamv[:, 0::2, :], lamv[:, 1::2, :], ALU.mult))
            nc.vector.tensor_reduce(lam2, lamv[:, 0::2, :], AX_X, ALU.add).then_inc(s_lamx, 1)

            v, over = softmax(norms[0], E0, banks[2])
            dve.wait_ge(s_lame, 1)
            link(nc.vector.tensor_tensor(lam, lamx[:, 0:1], lamx[:, 1:2], ALU.subtract))
            link(nc.vector.tensor_scalar(lam, lam, LAMBDA_INIT, None, ALU.add))
            first_largest(v, over, E0, v(1), v(3))
            link(nc.vector.scalar_tensor_tensor(out=v(4), in0=v(3), scalar=-2.0, in1=v(1), op0=ALU.mult, op1=ALU.add))
            first_largest(v, over, E0, v(4), v(0))
            hot = sc[:, 5, :].bitcast(BF16)[:, 0:TILES * E0]
            nc.vector.tensor_tensor(hot, sc[:, 3, :], sc[:, 0, :], ALU.add).then_inc(norms[0].hot, 1)
            for c, one_hot in enumerate((v(3), v(0))):
                link(nc.vector.tensor_tensor(v(4), one_hot, v(1), ALU.mult))
                link(nc.vector.tensor_reduce(weight0[:, :, c], v(4), AX_X, ALU.add))
            dve.wait_ge(norms[0].cum, 1)
            def table(at, n):
                return masks[:, at - C_KEPT:at - C_KEPT + n]
            def cells(a, b):
                return tally[:, 0:a * b].rearrange("p (a b) -> p a b", b=b)
            n_tiles, first, ends = r16[:, 0, :], r16[:, 1, :], r16[:, 2, :]
            total = banks[3][:, TILES * E0:(TILES + 1) * E0]
            link(nc.vector.tensor_copy(ends, total))
            link(nc.vector.tensor_tensor(cells(E0, TILES), ends.unsqueeze(2).to_broadcast([P, E0, TILES]),
                                         table(C_FILLED, TILES).unsqueeze(1).to_broadcast([P, E0, TILES]), ALU.is_gt))
            link(nc.vector.tensor_reduce(n_tiles, cells(E0, TILES), AX_X, ALU.add))
            link(nc.vector.tensor_tensor(cells(E0, E0), table(C_BEFORE, E0 * E0).rearrange("p (a b) -> p a b", b=E0),
                                         n_tiles.unsqueeze(1).to_broadcast([P, E0, E0]), ALU.mult))
            link(nc.vector.tensor_reduce(first, cells(E0, E0), AX_X, ALU.add))
            link(nc.vector.tensor_tensor(ends, first, n_tiles, ALU.add))
            link(nc.vector.tensor_scalar(first, first, float(P), -1.0, ALU.mult, ALU.add))
            link(nc.vector.tensor_tensor(cells(SLOT_TILES0, E0),
                                         table(C_TILE, SLOT_TILES0).unsqueeze(2).to_broadcast([P, SLOT_TILES0, E0]),
                                         ends.unsqueeze(1).to_broadcast([P, SLOT_TILES0, E0]), ALU.is_ge))
            link(nc.vector.tensor_reduce(r32[:, 0:SLOT_TILES0], cells(SLOT_TILES0, E0), AX_X, ALU.add))
            link(nc.vector.tensor_scalar(tile_expert[:, :], r32[:, 0:SLOT_TILES0], E0 - 1.0, None, ALU.min))
            rank = banks[3][:, 0:TILES * E0].rearrange("p (t e) -> p t e", e=E0)
            link(nc.vector.tensor_tensor(v(2), rank, first.unsqueeze(1).to_broadcast([P, TILES, E0]), ALU.add))
            for c, one_hot in enumerate((v(3), v(0))):
                link(nc.vector.tensor_tensor(v(4), one_hot, v(2), ALU.mult))
                link(nc.vector.tensor_reduce(r8a, v(4), AX_X, ALU.add))
                last = nc.vector.tensor_copy(slot0[:, :, c], r8a)
                if c == 0:
                    link(last)
            last.then_inc(norms[0].routed, 1)
            dve.wait_ge(filled, 16 * (SLOT_TILES0 + SLOT_TILES1))
            dve.wait_ge(ld["gn"], 16)
            dve.wait_ge(norms[0].routed, 1)
            attention(attns[0], xres)

            def combine(t):
                dve.wait_ge(back0, 16 * TOP * TILES)
                dve.wait_ge(*m0.dn.emptied(SLOT_TILES0 + SHARED * t + 1))
                for c in range(TOP):
                    out = nc.vector.scalar_tensor_tensor(out=acc[:, t, :], in0=y_back[:, t, c, :], scalar=weight0[:, t, c:c + 1],
                                                         in1=acc[:, t, :], op0=ALU.mult, op1=ALU.add)
                    if c == 0:
                        link(out)
                out.then_inc(m0.sum, 1)

            for n in range(N0 + 2):
                if n < N0:
                    if n >= 2:
                        m0.ht.wait_full(dve, n - 2)
                    dve.wait_ge(m0.silu, n + 1)
                    nc.vector.tensor_tensor(hid[:, n % 2, :], silu_a[:, n % 2, :], m0.up.bank(n)[:, F0:2 * F0], ALU.mult)\
                        .then_inc(m0.up.free["dve"], 1)
                if n >= 2:
                    j = n - 2
                    m0.dn.wait_full(dve, j)
                    src = m0.dn.bank(j)[:, 0:D]
                    if j < SLOT_TILES0:
                        if j >= 4:
                            dve.wait_ge(ys_stored[j % 4], 16 * (j // 4))
                        nc.vector.tensor_copy(ys[:, j % 4, :], src).then_inc(m0.dn.free["dve"], 1)
                    else:
                        t, part = divmod(j - SLOT_TILES0, SHARED)
                        if part == 0:
                            nc.vector.tensor_copy(acc[:, t, :], src).then_inc(m0.dn.free["dve"], 1)
                        else:
                            dve.wait_ge(*m0.dn.emptied(j - 1))
                            nc.vector.tensor_tensor(acc[:, t, :], src, acc[:, t, :], ALU.add).then_inc(m0.dn.free["dve"], 1)
            for t in range(TILES):
                combine(t)

            def gated(m, scale, base):
                def one(i):
                    dve.wait_ge(m.g, i + 1)
                    src, add = base(i)
                    link(nc.vector.scalar_tensor_tensor(out=gval[:, i, :], in0=src, scalar=scale, in1=gval[:, i, :],
                                                        op0=ALU.mult, op1=ALU.mult))
                    nc.vector.tensor_tensor(xres[:, i, :], gval[:, i, :], add, ALU.add).then_inc(m.x, 1)
                    dve.wait_ge(m.x, i + 1)
                return one

            dve.wait_ge(ld["x2"], 16)
            layer_norm(norms[1], xres, xn1,
                       gated(m0, 1.0 - LAMBDA_INIT, lambda i: (xres[:, i, :], x_again[:, i, :])))
            v, over = softmax(norms[1], E1, banks[2])
            first_largest(v, over, E1, v(2), v(3))
            n = TILES * E1
            hot = sc[:, 5, :].bitcast(BF16)[:, 0:n]
            nc.vector.tensor_copy(hot, sc[:, 3, 0:n]).then_inc(norms[1].hot, 1)
            dve.wait_ge(norms[1].cum, 1)
            kept = r8b
            link(nc.vector.tensor_scalar(sc[:, 4, 0:n], banks[3][:, 0:n], CAPACITY + 0.5, None, ALU.is_lt))
            link(nc.vector.tensor_tensor(v(4), v(3), v(4), ALU.mult))
            link(nc.vector.tensor_reduce(kept, v(4), AX_X, ALU.add))
            link(nc.vector.tensor_tensor(v(1), v(4), v(1), ALU.mult))
            link(nc.vector.tensor_reduce(weight1[:, :], v(1), AX_X, ALU.add))
            rank = banks[3][:, 0:n].rearrange("p (t e) -> p t e", e=E1)
            link(nc.vector.tensor_tensor(v(2), rank, cst[:, C_SLOT1:C_SLOT1 + E1].unsqueeze(1).to_broadcast([P, TILES, E1]),
                                         ALU.add))
            link(nc.vector.tensor_tensor(v(2), v(2), v(4), ALU.mult))
            link(nc.vector.tensor_reduce(r8a, v(2), AX_X, ALU.add))
            link(nc.vector.tensor_copy(slot1_out[:, :], r8a))
            link(nc.vector.tensor_scalar(kept, kept, -1.0, 1.0, ALU.mult, ALU.add))
            link(nc.vector.tensor_tensor(kept, kept, cst[:, C_SPARE:C_SPARE + TILES], ALU.mult))
            nc.vector.tensor_tensor(slot1_in[:, :], r8a, kept, ALU.add).then_inc(norms[1].routed, 1)
            dve.wait_ge(norms[1].routed, 1)
            dve.wait_ge(sent1, 16 * TILES)
            dve.wait_ge(ld["bias"], 32)
            attention(attns[1], s1)
            for e in range(E1):
                for c, (at, n) in enumerate(DN1):
                    m1.dn.wait_full(dve, (e, c))
                    if e >= 2:
                        dve.wait_ge(ys1_stored[e % 2], 32 * (e // 2))
                    nc.vector.tensor_copy(ys1[0:n, e % 2, c, :], m1.dn.bank((e, c))[0:n, 0:D]).then_inc(m1.dn.free["dve"], 1)
            one = gated(m1, 1.0, lambda i: (s1[:, i, :], xres[:, i, :]))
            for i in range(TILES):
                one(i)


def kernel(**inputs):
    import concourse.bacc as bacc
    from concourse.bass_utils import run_bass_kernel_spmd as run

    def f(name):
        return np.asarray(inputs[name])

    def kt(a, parts=P):
        return a.reshape(a.shape[0] // parts, parts, a.shape[1]).transpose(1, 0, 2)

    H, KV = 16, 4
    rep = H // KV
    even_odd = np.concatenate([np.arange(0, DH, 2), np.arange(1, DH, 2)])
    wq = f("L0_attn_Wq").reshape(D, KV, rep, 2, DH)[..., even_odd].transpose(0, 1, 3, 2, 4).reshape(D, 2 * D)
    wk = f("L0_attn_Wk").reshape(D, KV, 2, DH)[..., even_odd].reshape(D, D // 2)
    w1, w3, w2 = f("L0_ffn_w1"), f("L0_ffn_w3"), f("L0_ffn_w2")
    up = np.concatenate([w1, w3], axis=1)
    down = w2.transpose(0, 2, 1)
    sw1, sw3, sw2 = (f("L0_ffn_" + n) for n in ("sw1", "sw3", "sw2"))
    sup = np.concatenate([sw1.reshape(SHARED, F0, D), sw3.reshape(SHARED, F0, D)], axis=1)
    sdown = sw2.T.reshape(SHARED, F0, D)
    up = np.concatenate([up, sup]).transpose(0, 2, 1).reshape(EXPERTS0, KD, P, 2 * F0).transpose(2, 0, 1, 3)
    down = np.concatenate([down, sdown]).reshape(EXPERTS0, 2, FH, D).transpose(2, 0, 1, 3)
    arrays = {
        "x": f("L0_attn_x").reshape(-1, D),
        "consts": constants(),
        "wqkv0": kt(np.concatenate([wq, wk, f("L0_attn_Wv")], axis=1)),
        "wo0": kt(f("L0_attn_Wo")),
        "lam": np.stack([f("L0_attn_lambda_" + n) for n in ("q1", "k1", "q2", "k2")]),
        "gn": np.stack([f("L0_attn_gn_w"), f("L0_attn_gn_b")]),
        "gate0": kt(f("L0_ffn_gate_w").T),
        "w13": up,
        "w2": down,
        "wqkv1": kt(f("L1_attn_Wqkv").T),
        "bqkv": f("L1_attn_bqkv"),
        "wo1": kt(f("L1_attn_Wo").T),
        "bo": f("L1_attn_bo"),
        "gate1": kt(f("L1_ffn_gate_weight").T),
        "f1a": f("L1_ffn_w1").reshape(E1, KD, P, F1).transpose(2, 0, 1, 3),
        "f1b": f("L1_ffn_w2").reshape(E1, F1 // P, P, D).transpose(2, 0, 1, 3),
    }
    arrays = {n + "_in": np.ascontiguousarray(a) for n, a in arrays.items()}
    nc = bacc.Bacc("TRN2", target_bir_lowering=False, num_devices=1)
    args = [nc.dram_tensor(n, a.shape, F32, kind="ExternalInput").ap() for n, a in arrays.items()]
    out = nc.dram_tensor("out", (BATCH * SEQ, D), F32, kind="ExternalOutput").ap()
    slots = [nc.dram_tensor(n, (rows, D), F32, kind="Internal").ap()
             for n, rows in (("x0_slots", SLOT_TILES0 * P), ("y0_slots", SLOT_TILES0 * P),
                             ("x1_slots", SLOTS1 + TOKENS), ("y1_slots", SLOTS1))]
    program(nc, *args, out, *slots)
    r = run(nc, [arrays], core_ids=[0])
    return r.results[0]["out"].reshape(BATCH, SEQ, D)
```

```python
from contextlib import ExitStack

import concourse.bass as bass
from concourse import mybir
import numpy as np

P = 128
ALU = mybir.AluOpType
ACT = mybir.ActivationFunctionType
F32 = mybir.dt.float32
I32 = mybir.dt.int32
U32 = mybir.dt.uint32
BF16 = mybir.dt.bfloat16
AX_X = mybir.AxisListType.X

BATCH, SEQ, D = 4, 256, 256
TILES = BATCH * SEQ // P
HALVES = SEQ // P
KD = D // P
DH = 16
EPS = 1e-5
LAMBDA_INIT = 0.2
MASKED = -1e30
PARTS = 3
STACK = 6 * DH
DEEP = STACK + PARTS
SCALE = DH ** -0.5

E0, SHARED, F0 = 16, 2, 176
EXPERTS0 = E0 + SHARED
FH = F0 // 2
TOP = 2
TOKENS = BATCH * SEQ
SLOT_TILES0 = (TOP * TOKENS + E0 * (P - 1)) // P
E1, F1 = 8, 256
CAPACITY = 160
SCHEDULE = (
    dict(maxima=(2, 1, 1, 3, 4, 4, 4, 5), project1=0, project1_at=2, rotate1=0, rotate1_at=2,
         parts1=(2, 2, 2, 3, 3), rows0=0, rows1=(8, 0), mean=2, variance=3, out0=6, out1=7, divide=0,
         divide_at=0, project0=4, rotate0=4, parts0=(8, 8, 8, 8, 8), turn0=5, turn1=7, squares=2, scale=5,
         choose=(0, 4), ranks=(0, 5), send=(1, 0, 1)),
    dict(maxima=(2, 1, 6, 3), project1=0, project1_at=0, rotate1=0, rotate1_at=0, parts1=(1, 1, 1, 1), rows0=0,
         rows1=(4, 2), mean=0, variance=0, out0=1, out1=3, divide=0, divide_at=0, project0=2, rotate0=2,
         parts0=(4, 4, 4, 4), turn0=1, turn1=2, choose=(1, 0), ranks=(1, 3), send=(2, 0, 2)),
)
SLOTS1 = E1 * CAPACITY
SLOT_TILES1 = SLOTS1 // P

HEADS_TALL = P // (2 * DH)

ROPE_COLS = HALVES * 2 * DH
C_IDENT, C_ROPE = 0, P
C_IOTA = C_ROPE + 2 * ROPE_COLS
C_SLOT1 = C_IOTA + E0
C_SPARE = C_SLOT1 + E1
C_HEAD = C_SPARE + TILES
C_NEG1 = C_KEPT = C_HEAD + HEADS_TALL
C_TRIU = C_NEG1 + P
C_FILLED = C_TABLES = C_TRIU + P
C_BEFORE = C_FILLED + TILES
C_TILE = C_BEFORE + E0 * E0
C_COLS = C_TILE + SLOT_TILES0


def constants():
    c = np.zeros((P, C_COLS), np.float32)
    r = np.arange(P)
    c[:, C_IDENT:C_IDENT + P] = np.eye(P)
    c[:, C_NEG1:C_NEG1 + P] = np.where(r[None, :] > r[:, None], MASKED, 0.0)
    c[:, C_TRIU:C_TRIU + P] = r[:, None] <= r[None, :]
    pos = np.arange(SEQ, dtype=np.float32)
    inv = (np.float32(1.0) / np.power(np.float32(10000.0), np.arange(0, DH, 2, dtype=np.float32) / np.float32(DH))).astype(np.float32)
    theta = np.power(np.float32(10000.0), (-np.power(np.float32(2.0), np.arange(DH // 2, dtype=np.float32)) / np.float32(DH)).astype(np.float32)).astype(np.float32)
    for layer, ang in enumerate((pos[:, None] * inv, (pos + 1)[:, None] * theta)):
        cos, sin = np.cos(ang.astype(np.float32)), np.sin(ang.astype(np.float32))
        t = np.concatenate([cos, cos, -sin, sin], axis=1).reshape(HALVES, P, 2 * DH)
        at = C_ROPE + layer * ROPE_COLS
        c[:, at:at + ROPE_COLS] = t.transpose(1, 0, 2).reshape(P, ROPE_COLS)
    c[:, C_IOTA:C_IOTA + E0] = E0 - np.arange(E0)
    c[:, C_SLOT1:C_SLOT1 + E1] = CAPACITY * np.arange(E1) - 1
    c[:, C_SPARE:C_SPARE + TILES] = SLOTS1 + P * np.arange(TILES) + r[:, None]
    c[:, C_HEAD:C_HEAD + HEADS_TALL] = r[:, None] // (2 * DH) == np.arange(HEADS_TALL)
    c[:, C_FILLED:C_FILLED + TILES] = P * np.arange(TILES)
    c[:, C_BEFORE:C_BEFORE + E0 * E0] = np.tril(np.ones((E0, E0)), -1).reshape(-1)
    c[:, C_TILE:C_TILE + SLOT_TILES0] = np.arange(SLOT_TILES0)
    return c


class Stage:
    pass


class Ring:

    def __init__(self, banks, full, **free):
        self.banks, self.full, self.free, self.order, self.at = banks, full, free, [], {}

    def plan(self, key, engine):
        ordinal = 1 + sum(e == engine for e, _ in self.order)
        self.at[key] = len(self.order)
        self.order.append((engine, ordinal))

    def bank(self, key):
        return self.banks[self.at[key] % len(self.banks)]

    def wait_free(self, pe, key):
        before = self.at[key] - len(self.banks)
        if before >= 0:
            engine, ordinal = self.order[before]
            pe.wait_ge(self.free[engine], ordinal)

    def wait_full(self, eng, key):
        eng.wait_ge(self.full, self.at[key] + 1)

    def emptied(self, key):
        engine, ordinal = self.order[self.at[key]]
        return self.free[engine], ordinal

    def wait_drained(self, pe, keys=None):
        for name, s in self.free.items():
            n = sum(self.order[at][0] == name for key, at in self.at.items() if keys is None or key in keys)
            if n:
                pe.wait_ge(s, n)


def program(nc, x_d, consts_d, wqkv0_d, wo0_d, lam_d, gn_d, gate0_d, w13_d, w2_d,
            wqkv1_d, bqkv_d, wo1_d, bo_d, gate1_d, f1a_d, f1b_d, out_d, x0_slots_d, y0_slots_d, x1_slots_d, y1_slots_d):
    with ExitStack() as ctx:
        def sb(name, shape, dt=F32):
            return ctx.enter_context(nc.sbuf_tensor(name, shape, dt))

        def sem(name):
            return ctx.enter_context(nc.semaphore(name))

        banks = [ctx.enter_context(nc.psum_tensor(f"bank{i}", [P, 512], F32)) for i in range(8)]

        class Arena:

            def __init__(self, name, words):
                self.t, self.words, self.at = sb(name, [P, words]), words, 0

            def piece(self, shape, dt=F32):
                n = int(np.prod(shape))
                words = n if dt == F32 else (n + 1) // 2
                assert self.at + words <= self.words, (self.at, words, self.words)
                v = self.t[:, self.at:self.at + words]
                self.at += words
                if dt != F32:
                    v = v.bitcast(dt)
                if len(shape) > 1:
                    names = "abcdef"[:len(shape)]
                    v = v.rearrange(f"p ({' '.join(names)}) -> p {' '.join(names)}", **dict(zip(names, shape)))
                return v

            def restart(self):
                self.at = 0

        cst = sb("cst", [P, C_KEPT])
        ident = cst[:, C_IDENT:C_IDENT + P]
        iota = cst[:, C_IOTA:C_IOTA + E0]
        identb = sb("identb", [P, P], BF16)
        neg_ts = sb("neg_ts", [P, P], BF16)
        triu = sb("triu", [P, P], BF16)
        ones = sb("ones", [P, P], BF16)
        head_mean = sb("head_mean", [P, P])
        xnT = sb("xnT", [P, KD, TILES, P])
        xres = sb("xres", [P, TILES, D])
        wqkv = sb("wqkv", [P, KD, 3 * D])
        wo = sb("wo", [P, 4, D])
        gate = sb("gate", [P, KD, E0])
        gate1 = sb("gate1", [P, KD, E1])
        lamv = sb("lamv", [P, 4, DH])
        gn = sb("gn", [P, 2, 4])
        shared = sb("shared", [P, 4 * D])
        squares = shared[:, :]
        bqkv, bo = shared[:, 0:3 * D], shared[:, 3 * D:4 * D]
        small = sb("small", [P, 256])
        slot0 = sb("slot0", [P, TILES, TOP], U32)
        weight0 = sb("weight0", [P, TILES, TOP])
        tile_expert = sb("tile_expert", [P, SLOT_TILES0], I32)
        slot1_in = sb("slot1_in", [P, TILES], U32)
        slot1_out = sb("slot1_out", [P, TILES], U32)
        weight1 = sb("weight1", [P, TILES])

        moe = Arena("moe", EXPERTS0 * KD * (2 * F0 + D))
        w13 = moe.piece([EXPERTS0, KD, 2 * F0])
        w2 = moe.piece([EXPERTS0, 2, D])
        moe.restart()
        f1a = moe.piece([E1, KD, F1])
        f1b = moe.piece([E1, F1 // P, D])
        s1 = moe.piece([TILES, D])
        xs1 = moe.piece([SLOT_TILES1, D])
        xs1T = moe.piece([KD, SLOTS1])
        gelT = xs1.rearrange("p t d -> p (t d)").rearrange("p (e m t) -> p e m t", e=E1, m=F1 // P)
        ys1 = moe.piece([2, 2, D])
        xn1 = moe.piece([TILES, D])
        sc1 = moe.piece([6, TILES * E1])
        y_back1 = moe.piece([TILES, D])

        work = Arena("work", 22144)
        work.at = 40 * SEQ + 40 * 6 * DH // 2 + 2 * 40 * DH
        x_in = work.piece([TILES, D])
        xn = xres[:, :, :]
        masks = work.piece([C_TABLES - C_KEPT])
        sc0 = wo[:, 0:3, :].rearrange("p c d -> p (c d)").rearrange("p (k n) -> p k n", k=6)
        zeros = wo[:, 3, :]
        tables = shared[:, 0:C_COLS - C_TABLES]
        tally = shared[:, 2 * D:2 * D + SLOT_TILES0 * E0]
        work.restart()
        qkT = work.piece([2, 40, SEQ], BF16)
        stack = work.piece([40, 6, DH], BF16)
        rotary = work.piece([2 * 40 * DH])
        rot_a, rot_b = (rotary[:, k * 40 * DH:(k + 1) * 40 * DH].rearrange("p (g d) -> p g d", d=DH) for k in range(2))
        o_n = rotary[:, 0:32 * 32].rearrange("p (m w) -> p m w", w=32)
        pT = [work.piece([512]) for _ in range(6)]
        vaug = work.piece([3, HALVES, 16 * 17])
        o_raw = work.piece([HALVES * 32 * 33])
        rot_x = o_raw[:, 32 * 33:32 * 33 + 32 * DH].rearrange("p (g d) -> p g d", d=DH)
        o_d = work.piece([HALVES, 2 * D])
        zT = work.piece([4, P])
        nmax = work.piece([32])
        nmax_r = work.piece([32])
        nparts = work.piece([2, PARTS * 32], BF16)
        nT = work.piece([2, P], BF16)
        rsum = work.piece([32])
        work.restart()
        xs = work.piece([4, D])
        xsT = work.piece([2, KD, P])
        ys = work.piece([4, D])
        silu_a = work.piece([2, F0])
        hid = work.piece([2, F0])
        hidT = work.piece([2, 2, P])
        x_again = work.piece([TILES, D])
        acc = work.piece([TILES, D])
        assert work.at <= 40 * SEQ
        y_back = work.piece([TILES, TOP, D])
        gval = work.piece([TILES, D])

        ld = {n: sem("ld_" + n) for n in ("tables", "cst", "wqkv", "wo", "gate", "lam", "gn", "bias", "w13", "w2",
                                          "x2", "wqkv1", "wo1", "f1")}
        out_sem = sem("out_sem")
        x_here = [sem(f"x_here{g}") for g in range(2)]
        filled = sem("filled")
        zeroed = sem("zeroed")
        sent0, sent1 = sem("sent0"), sem("sent1")
        xs_loaded = [sem(f"xs_loaded{k}") for k in range(4)]
        ys_stored = [sem(f"ys_stored{k}") for k in range(4)]
        xs1_loaded = sem("xs1_loaded")
        ys1_stored = [sem(f"ys1_stored{k}") for k in range(2)]
        back0, back1 = ([sem(f"back{n}_{i}") for i in range(TILES)] for n in range(2))
        dve_c, act_c, pool_c = sem("dve_chain"), sem("act_chain"), sem("pool_chain")
        s_cast = sem("s_cast")
        s_ones = sem("s_ones")
        s_lamx, s_lame = sem("s_lamx"), sem("s_lame")

        def norm_state(n):
            q = Stage()
            q.n = n
            q.tp = Ring(banks[0:2], sem(f"ln{n}_tp_full"), act=sem(f"ln{n}_tp_free"))
            for g in range(TILES // 2):
                q.tp.plan(g, "act")
            q.veps, q.pow = sem(f"ln{n}_veps"), sem(f"ln{n}_pow")
            q.xn = sem(f"ln{n}_xn")
            q.routed, q.expin, q.expd = sem(f"ln{n}_routed"), sem(f"ln{n}_expin"), sem(f"ln{n}_expd")
            q.hot = sem(f"ln{n}_hot")
            return q

        norms = [norm_state(0), norm_state(1)]
        stats = small[:, 0:TILES * 6].rearrange("p (t s) -> p t s", s=6)
        mv = small[:, 48:64].rearrange("p (t s) -> p t s", s=2)
        veps, rstd, tmp8 = small[:, 64:72], small[:, 72:80], small[:, 80:88]
        r16, r32 = small[:, 120:168].rearrange("p (k e) -> p k e", e=16), small[:, 168:200]
        r8a, r8b = small[:, 96:104], small[:, 104:112]
        lam2, lamx, lam = small[:, 112:114], small[:, 114:116], small[:, 116:117]
        gn_scale = small[:, 216:220]
        gn_sum, gn_ve, gn_rs, gn_t = small[:, 120:152], small[:, 152:168], small[:, 168:184], small[:, 184:200]
        minus_half16 = small[:, 200:216]

        def attention_state(n, maps, kgroups, vheads, vwidth, kof, vof):
            a = Stage()
            a.n, a.maps, a.units, a.groups = n, maps, maps // 4, maps + kgroups
            a.vheads, a.vw, a.kof, a.vof = vheads, vwidth, kof, vof
            a.tgroups = a.groups // 8
            a.zchunks = vheads * vwidth * (4 if n == 0 else 1) // P
            p = f"a{n}_"
            a.pj = Ring(banks[0:2], sem(p + "pj_full"), act=sem(p + "pj_free_act"), dve=sem(p + "pj_free_dve"))
            a.s = Ring([banks[2], banks[3], banks[6]], sem(p + "s_full"), dve=sem(p + "s_free"))
            a.st = Ring(banks[4:6], sem(p + "st_full"), act=sem(p + "st_free"))
            a.po = Ring(banks[7:8], sem(p + "po_full"), act=sem(p + "po_free_act"))
            a.stacked = sem(p + "stacked")
            a.nmax = sem(p + "nmax")
            a.rows = [sem(p + "rows0"), sem(p + "rows1")]
            a.ones = sem(p + "ones")
            a.cut = sem(p + "cut")
            a.sums = sem(p + "sums")
            a.gpow, a.z = sem(p + "gpow"), sem(p + "z")
            a.scaled = sem(p + "scaled")
            a.squared = sem(p + "squared")
            a.onorm = sem(p + "onorm") if n == 0 else a.z
            u = a.units
            queries, keys = list(range(maps // 8)), list(range(maps // 8, a.tgroups))
            a.order, a.order0 = keys + queries, queries + keys
            begins = []
            steps = [("project", 0), ("rotate", 0), ("logits", n)] + [("part", (0, g)) for g in a.order0]
            for b in range(BATCH + 2):
                slots = [[[], [], []] for _ in range(u + 1)]
                c = SCHEDULE[n]
                if b < BATCH:
                    slots[c["project1"]][c["project1_at"]] += [("project", 2 * b + 1)]
                    slots[c["rotate1"]][c["rotate1_at"]] += [("rotate", 2 * b + 1)]
                    for k, g in enumerate(a.order):
                        slots[c["parts1"][k]][1] += [("part", (2 * b + 1, g))]
                    q = 0
                    for j, count in enumerate(c["maxima"]):
                        slots[j][1] += [("max", (b, q + k)) for k in range(count)]
                        if q < u <= q + count:
                            slots[j + c["rows0"]][2] += [("rows", 2 * b)]
                        q += count
                    slots[c["rows1"][0]][c["rows1"][1]] += [("rows", 2 * b + 1)]
                if b >= 2:
                    i0, i1 = 2 * b - 4, 2 * b - 3
                    slots[c["divide"]][c["divide_at"]] += [("divide", i0), ("divide", i1)]
                    if n == 0:
                        slots[c["mean"]][2] += [("mean", b - 2)]
                        slots[c["squares"]][2] += [("squares", b - 2)]
                        slots[c["variance"]][2] += [("variance", b - 2)]
                        slots[c["scale"]][2] += [("scale", b - 2)]
                    slots[c["turn0"]][2] += [("turn", i0)]
                    slots[c["out0"]][2] += [("out", i0)]
                    slots[c["turn1"]][2] += [("turn", i1)]
                    slots[c["out1"]][2] += [("out", i1)]
                if b == c["choose"][0]:
                    slots[c["choose"][1]][2] += [("choose", n)]
                if b == c["ranks"][0]:
                    slots[c["ranks"][1]][2] += [("ranks", n)]
                if b + 1 < BATCH:
                    slots[c["project0"]][2] += [("project", 2 * b + 2)]
                    slots[c["rotate0"]][2] += [("rotate", 2 * b + 2)]
                    for k, g in enumerate(a.order0):
                        slots[c["parts0"][k]][2 if c["parts0"][k] < u else 0] += [("part", (2 * b + 2, g))]
                if b == c["send"][0]:
                    for i in range(TILES):
                        slots[c["send"][1] + i // c["send"][2]][2] += [("send", i)]
                begins.append(len(steps))
                for j, (before, maxima, after) in enumerate(slots):
                    if 0 < b <= BATCH and j > 0:
                        steps += [("value begins", (b - 1, j - 1))]
                    steps += before
                    if 0 < b <= BATCH and j < u:
                        steps += [("exp", (b - 1, j))]
                    if n == 1 and b == BATCH:
                        steps += [("down", e) for e in range(3 * j, min(3 * j + 3, E1))]
                    steps += maxima
                    if 0 < b <= BATCH and j > 0:
                        steps += [("value", (b - 1, j - 1))]
                    steps += after
            rest = steps.index(("value", (BATCH - 1, a.units - 1))) + 1
            start = rest if n == 0 else begins[BATCH]
            a.started = {"s": [w for kind, w in steps[:start] if kind == "max"],
                         "st": [(*w, c) for kind, w in steps[:start] if kind == "exp" for c in range(3)],
                         "po": [("rows", w) if kind == "rows" else w for kind, w in steps[:start] if kind in ("rows", "value")]}
            a.steps, a.last, a.tail = steps[:start], steps[start:rest], steps[rest:]
            for kind, w in steps:
                if kind == "project":
                    a.pj.plan(("q", w), "dve")
                    a.pj.plan(("kv", w), "dve")
                elif kind == "part":
                    a.pj.plan(("t", *w), "act")
                elif kind in ("mean", "variance", "logits", "ranks"):
                    a.pj.plan((kind, w), "dve")
                elif kind == "turn":
                    a.pj.plan(("z", w), "act")
                elif kind == "out":
                    a.pj.plan(("o", w), "act" if n == 0 else "dve")
                elif kind == "max":
                    a.s.plan(w, "dve")
                elif kind == "exp":
                    for u in range(3):
                        a.st.plan((*w, u), "act")
                elif kind == "rows":
                    a.po.plan(("rows", w), "act")
                elif kind == "value":
                    a.po.plan(w, "act")
            return a

        attns = [attention_state(0, 32, 8, 4, 32, lambda m: m // 4, lambda m: m // 8),
                 attention_state(1, 16, 16, 16, 16, lambda m: m, lambda m: m)]

        def rope_tables(a, half):
            at = C_ROPE + a.n * ROPE_COLS + half * 2 * DH
            return cst[:, at:at + DH], cst[:, at + DH:at + 2 * DH]

        def max_use(a, q):
            return (0, range(4 * q, 4 * q + 4)) if q < a.units else (1, range(2 * (q - a.units), 2 * (q - a.units) + 2))

        def beside_experts(a, n):
            at = n - 1
            return a.tail[at:at + 1] if at >= 0 else []

        def back_at(n, lag):
            return [t for t in range(TILES) if max(SLOT_TILES0 + 7 + t, SLOT_TILES0 + 4 + 2 * t) + lag == n]

        def hot_of(n):
            return ((sc0, E0), (sc1, E1))[n][0][:, 5, :].bitcast(BF16)[:, 0:TILES * (E0, E1)[n]]

        def vaug_of(a, b):
            w = a.vw + 1
            return vaug[:, b % 3, :, 0:a.vheads * w].rearrange("p h (v w) -> p h v w", w=w)

        def raw_of(a):
            w = a.vw + 1
            return o_raw[:, 0:HALVES * a.maps * w].rearrange("p (h m w) -> p h m w", h=HALVES, w=w)

        def bfv(bank):
            return bank[:, :].bitcast(BF16).rearrange("p (m t) -> p m t", t=P)

        m0 = Stage()
        m0.xt = Ring(banks[4:5], sem("m0_xt_full"), act=sem("m0_xsT"))
        m0.up = Ring(banks[2:4], sem("m0_up_full"), dve=sem("m0_hid"))
        m0.ht = Ring(banks[5:6], sem("m0_ht_full"), act=sem("m0_hidT"))
        m0.dn = Ring(banks[6:8], sem("m0_dn_full"), dve=sem("m0_dn_free"))
        m0.silu, m0.g, m0.x = sem("m0_silu"), sem("m0_g"), sem("m0_x")
        m0.sum = sem("m0_sum")
        N0 = SLOT_TILES0 + SHARED * TILES
        for n in range(N0):
            if n < SLOT_TILES0:
                m0.xt.plan(n, "act")
            m0.up.plan(n, "dve")
            m0.ht.plan(n, "act")
            m0.dn.plan(n, "dve")

        m1 = Stage()
        m1.xt = Ring(banks[2:4], sem("m1_xt_full"), act=sem("m1_xt_free"))
        m1.up = Ring(banks[4:6], sem("m1_up_full"), act=sem("m1_up_free"))
        m1.dn = Ring([banks[2], banks[3], banks[6]], sem("m1_dn_full"), dve=sem("m1_dn_free"))
        m1.g, m1.x = sem("m1_g"), sem("m1_x")
        DN1 = ((0, P), (P, CAPACITY - P))
        for g in range(SLOT_TILES1 // 2):
            m1.xt.plan(g, "act")
        for e in range(E1):
            m1.up.plan(e, "act")
            for c in range(2):
                m1.dn.plan((e, c), "dve")

        block = ctx.enter_context(nc.Block())

        @block.sync
        def _(sp):
            x_tiles = x_d.rearrange("(t p) d -> p t d", p=P)
            for g in range(2):
                sp.dma_start(x_in[:, 4 * g:4 * g + 4], x_tiles[:, 4 * g:4 * g + 4]).then_inc(x_here[g], 16)
            sp.dma_start(cst[:, :], consts_d[:, 0:C_KEPT]).then_inc(ld["cst"], 16)
            sp.dma_start(masks, consts_d[:, C_KEPT:C_TABLES]).then_inc(ld["cst"], 16)
            sp.dma_start(gate[:, :, :], gate0_d).then_inc(ld["gate"], 16)
            sp.dma_start(gate1[:, :, :], gate1_d).then_inc(ld["gate"], 16)
            sp.dma_start(wqkv[:, :, :], wqkv0_d).then_inc(ld["wqkv"], 16)
            sp.dma_start(lamv[:, :, :], lam_d.partition_broadcast(P)).then_inc(ld["lam"], 16)
            sp.dma_start(gn[:, :, :], gn_d).then_inc(ld["gn"], 16)
            sp.dma_start(tables, consts_d[:, C_TABLES:]).then_inc(ld["tables"], 16)
            sp.wait_ge(zeroed, 1)
            for j in range(SLOT_TILES0):
                sp.dma_start(x0_slots_d[j * P:j * P + P, :], zeros).then_inc(filled, 16)
            for j in range(SLOT_TILES1):
                sp.dma_start(x1_slots_d[j * P:j * P + P, :], zeros).then_inc(filled, 16)
            for e in range(0, EXPERTS0, 3):
                sp.dma_start(w13[:, e:e + 3], w13_d[:, e:e + 3]).then_inc(ld["w13"], 16)
            for e in range(0, EXPERTS0, 6):
                sp.dma_start(w2[0:FH, e:e + 6], w2_d[:, e:e + 6]).then_inc(ld["w2"], 16)

            sp.wait_ge(norms[0].routed, 1)
            sp.wait_ge(filled, 16 * (SLOT_TILES0 + SLOT_TILES1))
            sp.dma_start(wo[:, :, :], wo0_d).then_inc(ld["wo"], 16)

            def maximum_rows(a, tiles):
                for i in tiles:
                    b, half = divmod(i, HALVES)
                    sp.wait_ge(*a.po.emptied(("rows", i)))
                    if b >= 2:
                        sp.wait_ge(a.st.full, a.st.at[(b - 2, a.units - 1, 2)] + 1)
                    for k in range(PARTS):
                        sp.dma_start(qkT[STACK + k:STACK + k + 1, b % 2, 0:a.maps, half * P:half * P + P],
                                     nT[k * a.maps:(k + 1) * a.maps, i % 2, :]).then_inc(a.rows[b % 2], 16)

            maximum_rows(attns[0], range(TILES))
            a0 = attns[0]
            a0.st.wait_full(sp, (BATCH - 1, a0.units - 1, 2))
            sp.dma_start(x_again, x_d.rearrange("(t p) d -> p t d", p=P)).then_inc(ld["x2"], 16)
            sp.wait_ge(sent0, 16 * TOP * TILES)
            for n in range(SLOT_TILES0 + 5):
                if n < SLOT_TILES0:
                    if n >= 4:
                        m0.xt.wait_full(sp, n - 4)
                    sp.dma_start(xs[:, n % 4, :], x0_slots_d[n * P:n * P + P, :]).then_inc(xs_loaded[n % 4], 16)
                if n >= 5:
                    j = n - 5
                    sp.wait_ge(*m0.dn.emptied(j))
                    sp.dma_start(y0_slots_d[j * P:j * P + P, :], ys[:, j % 4, :]).then_inc(ys_stored[j % 4], 16)
            sp.wait_ge(*a0.pj.emptied(("o", TILES - 1)))
            sp.dma_start(wqkv[:, :, :], wqkv1_d).then_inc(ld["wqkv1"], 16)
            sp.dma_start(wo[:, 0:2, :], wo1_d).then_inc(ld["wo1"], 16)
            sp.dma_start(bqkv, bqkv_d.partition_broadcast(P)).then_inc(ld["bias"], 16)
            sp.dma_start(bo, bo_d.partition_broadcast(P)).then_inc(ld["bias"], 16)
            m0.dn.wait_full(sp, N0 - 1)
            sp.dma_start(f1a, f1a_d).then_inc(ld["f1"], 16)
            sp.dma_start(f1b, f1b_d).then_inc(ld["f1"], 16)
            maximum_rows(attns[1], range(TILES - 2))
            sp.wait_ge(sent1, 16 * TILES)
            sp.dma_start(xs1, x1_slots_d[0:SLOTS1, :].rearrange("(t p) d -> p t d", p=P)).then_inc(xs1_loaded, 16)
            maximum_rows(attns[1], range(TILES - 2, TILES))
            for e in range(E1):
                for c, (at, n) in enumerate(DN1):
                    sp.wait_ge(*m1.dn.emptied((e, c)))
                    row = e * CAPACITY + at
                    sp.dma_start(y1_slots_d[row:row + n, :], ys1[0:n, e % 2, c, :]).then_inc(ys1_stored[e % 2], 16)
            for i in range(TILES):
                sp.wait_ge(m1.x, i + 1)
                sp.dma_start(out_d[i * P:i * P + P, :], xres[:, i, :]).then_inc(out_sem, 16)
            sp.wait_ge(out_sem, 16 * TILES)

        @block.tensor
        def _(pe):
            def layer_norm(q, xn_t):
                for g in range(TILES // 2):
                    q.tp.wait_free(pe, g)
                    bank = q.tp.bank(g)
                    for u in range(2):
                        i = 2 * g + u
                        pe.wait_ge(q.xn, i + 1)
                        for k in range(KD):
                            mm = nc.tensor.transpose(bank[:, (2 * u + k) * P:(2 * u + k + 1) * P],
                                                     xn_t[:, i, k * P:(k + 1) * P], ident)
                    mm.then_inc(q.tp.full, 1)

            def logits(a):
                pe.wait_ge(ld["gate"], 32)
                norms[a.n].tp.wait_drained(pe)
                key = ("logits", a.n)
                a.pj.wait_free(pe, key)
                experts, weights = ((E0, gate), (E1, gate1))[a.n]
                for i in range(TILES):
                    for k in range(KD):
                        mm = nc.tensor.matmul(a.pj.bank(key)[:, i * experts:(i + 1) * experts], xnT[:, k, i, :],
                                              weights[:, k, :], start=(k == 0), stop=(k == KD - 1))
                mm.then_inc(a.pj.full, 1)

            def project(a, i, beside):
                cols = {"q": slice(0, 512), "kv": slice(512, 768)}
                for use, n in (("q", 512), ("kv", 256)):
                    key = (use, i)
                    a.pj.wait_free(pe, key)
                    for k in range(KD):
                        mm = nc.tensor.matmul(a.pj.bank(key)[:, 0:n], xnT[:, k, i, :], wqkv[:, k, cols[use]],
                                              start=(k == 0), stop=(k == KD - 1))
                        if k == KD - 1:
                            mm.then_inc(a.pj.full, 1)
                        next(beside, None)

            def part(a, i, g, beside):
                pe.wait_ge(a.stacked, i + 1)
                key = ("t", i, g)
                a.pj.wait_free(pe, key)
                for u in range(8):
                    mm = nc.tensor.transpose(bfv(a.pj.bank(key))[0:STACK, u, :],
                                             stack[:, 8 * g + u].rearrange("p s d -> p (s d)"), identb[:, :])
                mm.then_inc(a.pj.full, 1)
                for _ in range(3):
                    next(beside, None)

            def transposed(a, i, m):
                order = a.order if i % 2 else a.order0
                last = max(order.index(m // 8), max(order.index(g) for g in range(a.maps // 8, a.tgroups)))
                pe.wait_ge(*a.pj.emptied(("t", i, order[last])))

            def scores(a, b, q, beside):
                half, ms = max_use(a, q)
                transposed(a, 2 * b + half, ms[-1])
                if half:
                    transposed(a, 2 * b, ms[-1])
                a.s.wait_free(pe, (b, q))
                bank = a.s.bank((b, q))
                n = P * (half + 1)
                view = bank[:, :].rearrange("p (m s) -> p m s", s=n)
                nc.tensor.matmul(view[:, :, half * P:half * P + P], identb[:, :],
                                 neg_ts[:, :].unsqueeze(1).to_broadcast([P, len(ms), P]),
                                 start=True, stop=False, skip_group_check=True)
                for u, m in enumerate(ms):
                    mm = nc.tensor.matmul(view[:, u, :], qkT[0:STACK, b % 2, m, half * P:half * P + P],
                                          qkT[0:STACK, b % 2, a.maps + a.kof(m), 0:n],
                                          start=False, stop=True, skip_group_check=True)
                    if m == ms[-1]:
                        mm.then_inc(a.s.full, 1)
                    next(beside, None)

            def exp_scores(a, b, j, beside):
                pe.wait_ge(a.rows[b % 2], 16 * PARTS * HALVES * (b // 2 + 1))
                pe.wait_ge(a.ones, 1 + 3 * HALVES)
                for u in range(3):
                    key = (b, j, u)
                    a.st.wait_free(pe, key)
                    bank = a.st.bank(key)
                    if u < 2:
                        keys, ms, t0, n = 0, (4 * j + 2 * u, 4 * j + 2 * u + 1), 0, SEQ
                    else:
                        keys, ms, t0, n = 1, range(4 * j, 4 * j + 4), P, P
                    view = bank[:, :].rearrange("p (m t) -> p m t", t=n)
                    for v, m in enumerate(ms):
                        mm = nc.tensor.matmul(view[:, v, :],
                                              qkT[0:DEEP, b % 2, a.maps + a.kof(m), keys * P:keys * P + P],
                                              qkT[0:DEEP, b % 2, m, t0:t0 + n],
                                              start=True, stop=True)
                        if m == ms[-1]:
                            mm.then_inc(a.st.full, 1)
                        next(beside, None)

            def rows(a, i):
                pe.wait_ge(a.nmax, i + 1)
                key = ("rows", i)
                a.po.wait_free(pe, key)
                n = PARTS * a.maps
                nc.tensor.transpose(bfv(a.po.bank(key))[0:n, 0, :], nparts[:, i % 2, 0:n], identb[:, :])\
                    .then_inc(a.po.full, 1)

            def value(a, b, j):
                key = (b, j)
                a.po.wait_free(pe, key)
                w = a.vw + 1
                out = a.po.bank(key)[:, 0:HALVES * 4 * w].rearrange("p (h m w) -> p h m w", h=HALVES, w=w)
                v = vaug_of(a, b)
                pe.wait_ge(a.cut, a.st.at[(b, j, 2)] + 1)
                probs = [pT[a.st.at[(b, j, u)] % 6] for u in range(3)]
                for r in range(4):
                    vh = a.vof(4 * j + r)
                    p0 = probs[r // 2][:, (r % 2) * SEQ:(r % 2) * SEQ + SEQ]
                    nc.tensor.matmul(out[:, 0, r, :], p0[:, 0:P], v[:, 0, vh, :], start=True, stop=True)
                    yield
                    nc.tensor.matmul(out[:, 1, r, :], p0[:, P:SEQ], v[:, 0, vh, :], start=True, stop=False)
                    yield
                    mm = nc.tensor.matmul(out[:, 1, r, :], probs[2][:, r * P:r * P + P], v[:, 1, vh, :],
                                          start=False, stop=True)
                    if r < 3:
                        yield
                mm.then_inc(a.po.full, 1)
                yield

            def head_statistic(a, kind, b):
                key = (kind, b)
                pe.wait_ge(a.sums, 2 * b + (1 if kind == "mean" else 2))
                a.pj.wait_free(pe, key)
                for half in range(HALVES):
                    mm = nc.tensor.matmul(a.pj.bank(key)[:, 0:16], head_mean[:, :], gn_sum[:, 16 * half:16 * half + 16],
                                          start=(half == 0), stop=(half == HALVES - 1))
                mm.then_inc(a.pj.full, 1)

            def turn(a, i):
                pe.wait_ge(*(a.pj.emptied(("mean", i // HALVES)) if a.n == 0 else (a.z, i + 1)))
                key = ("z", i)
                a.pj.wait_free(pe, key)
                for c in range(a.zchunks):
                    mm = nc.tensor.transpose(a.pj.bank(key)[:, c * P:(c + 1) * P], o_d[:, i % 2, c * P:(c + 1) * P], ident)
                mm.then_inc(a.pj.full, 1)

            def out(a, i):
                pe.wait_ge(*a.pj.emptied(("z", i)))
                pe.wait_ge(ld["wo" if a.n == 0 else "wo1"], 16)
                key = ("o", i)
                a.pj.wait_free(pe, key)
                for c in range(a.zchunks):
                    mm = nc.tensor.matmul(a.pj.bank(key)[:, 0:D], zT[:, c, :], wo[:, c, :],
                                          start=(c == 0), stop=(c == a.zchunks - 1))
                mm.then_inc(a.pj.full, 1)

            def ranks(a):
                q, experts, hot = norms[a.n], (E0, E1)[a.n], hot_of(a.n)
                pe.wait_ge(q.hot, 1)
                key = ("ranks", a.n)
                a.pj.wait_free(pe, key)
                for i in range(TILES + 1):
                    for j in range(min(i + 1, TILES)):
                        mm = nc.tensor.matmul(a.pj.bank(key)[:, i * experts:(i + 1) * experts],
                                              (triu if j == i else ones)[:, :], hot[:, j * experts:(j + 1) * experts],
                                              start=(j == 0), stop=(j == min(i, TILES - 1)))
                mm.then_inc(a.pj.full, 1)

            def down(e, beside):
                for c, (at, n) in enumerate(DN1):
                    m1.dn.wait_free(pe, (e, c))
                    for f in range(2):
                        mm = nc.tensor.matmul(m1.dn.bank((e, c))[0:n, 0:D], gelT[:, e, f, at:at + n],
                                              f1b[:, e, f, :], start=(f == 0), stop=(f == 1))
                        if f == 1:
                            mm.then_inc(m1.dn.full, 1)
                        next(beside, None)

            def attention(a, steps):
                beside = iter(())
                for kind, w in steps:
                    if kind == "project":
                        project(a, w, beside)
                    elif kind == "part":
                        part(a, *w, beside)
                    elif kind == "max":
                        scores(a, *w, beside)
                    elif kind == "exp":
                        exp_scores(a, *w, beside)
                    elif kind == "rows":
                        rows(a, w)
                    elif kind == "down":
                        down(w, beside)
                    elif kind == "value begins":
                        beside = value(a, *w)
                    elif kind == "value":
                        for _ in beside:
                            pass
                    elif kind in ("mean", "variance"):
                        head_statistic(a, kind, w)
                    elif kind == "turn":
                        turn(a, w)
                    elif kind == "out":
                        out(a, w)
                    elif kind == "logits":
                        logits(a)
                    elif kind == "ranks":
                        ranks(a)

            def experts0():
                chosen = {}

                def turn_rows(n):
                    m0.xt.wait_free(pe, n)
                    pe.wait_ge(xs_loaded[n % 4], 16 * (n // 4 + 1))
                    for k in range(KD):
                        mm = nc.tensor.transpose(m0.xt.bank(n)[:, k * P:(k + 1) * P], xs[:, n % 4, k * P:(k + 1) * P], ident)
                    mm.then_inc(m0.xt.full, 1)

                def up(n):
                    m0.up.wait_free(pe, n)
                    if n < SLOT_TILES0:
                        e = pe.value_load(tile_expert[0:1, n:n + 1], min_val=0, max_val=E0 - 1)
                        chosen[n] = e
                        pe.wait_ge(*m0.xt.emptied(n))
                    for k in range(KD):
                        if n < SLOT_TILES0:
                            x_t, w = xsT[:, n % 2, k, :], w13[:, bass.ds(e, 1), k, :]
                        else:
                            t, part = divmod(n - SLOT_TILES0, SHARED)
                            x_t, w = xnT[:, k, t, :], w13[:, E0 + part, k, :]
                        mm = nc.tensor.matmul(m0.up.bank(n)[:, 0:2 * F0], x_t, w, start=(k == 0), stop=(k == KD - 1))
                    mm.then_inc(m0.up.full, 1)

                def turn_hidden(n):
                    pe.wait_ge(*m0.up.emptied(n))
                    m0.ht.wait_free(pe, n)
                    for f in range(2):
                        mm = nc.tensor.transpose(m0.ht.bank(n)[0:FH, f * P:(f + 1) * P],
                                                 hid[:, n % 2, f * FH:(f + 1) * FH], ident)
                    mm.then_inc(m0.ht.full, 1)

                def down(n):
                    pe.wait_ge(*m0.ht.emptied(n))
                    m0.dn.wait_free(pe, n)
                    for f in range(2):
                        if n < SLOT_TILES0:
                            w = w2[0:FH, bass.ds(chosen[n], 1), f, :]
                        else:
                            w = w2[0:FH, E0 + (n - SLOT_TILES0) % SHARED, f, :]
                        mm = nc.tensor.matmul(m0.dn.bank(n)[:, 0:D], hidT[0:FH, n % 2, f, :], w,
                                              start=(f == 0), stop=(f == 1))
                    mm.then_inc(m0.dn.full, 1)

                pe.wait_ge(ld["w13"], 16 * 6)
                pe.wait_ge(ld["w2"], 16 * 3)
                turn_rows(0)
                for n in range(N0 + 2):
                    attention(attns[0], beside_experts(attns[0], n))
                    if n + 1 < SLOT_TILES0:
                        turn_rows(n + 1)
                    if n < N0:
                        up(n)
                    if 1 <= n <= N0:
                        turn_hidden(n - 1)
                    if n >= 2:
                        down(n - 2)
                for ring in (attns[0].pj, m0.up, m0.ht, m0.dn):
                    ring.wait_drained(pe)

            def experts1():
                pe.wait_ge(xs1_loaded, 16)
                for g in range(SLOT_TILES1 // 2):
                    m1.xt.wait_free(pe, g)
                    for u in range(2):
                        for k in range(KD):
                            mm = nc.tensor.transpose(m1.xt.bank(g)[:, (2 * k + u) * P:(2 * k + u + 1) * P],
                                                     xs1[:, 2 * g + u, k * P:(k + 1) * P], ident)
                    mm.then_inc(m1.xt.full, 1)

                def up(e):
                    m1.up.wait_free(pe, e)
                    pe.wait_ge(*m1.xt.emptied(((e + 1) * CAPACITY - 1) // (2 * P)))
                    for m in range(F1 // P):
                        for k in range(KD):
                            mm = nc.tensor.matmul(m1.up.bank(e)[:, m * CAPACITY:(m + 1) * CAPACITY],
                                                  f1a[:, e, k, m * P:(m + 1) * P],
                                                  xs1T[:, k, e * CAPACITY:(e + 1) * CAPACITY],
                                                  start=(k == 0), stop=(k == KD - 1))
                    mm.then_inc(m1.up.full, 1)

                pe.wait_ge(ld["f1"], 32)
                for e in range(E1):
                    up(e)
                for ring in (m1.xt, m1.up):
                    ring.wait_drained(pe)

            pe.wait_ge(ld["cst"], 32)
            pe.wait_ge(s_cast, 3)
            for a, load, xn_t, experts in ((attns[0], "wqkv", xn, experts0), (attns[1], "wqkv1", xn1, experts1)):
                layer_norm(norms[a.n], xn_t)
                norms[a.n].tp.wait_drained(pe)
                pe.wait_ge(ld[load], 16)
                attention(a, a.steps)
                for ring, keys in ((a.s, "s"), (a.st, "st"), (a.po, "po")):
                    ring.wait_drained(pe, a.started[keys])
                experts()
            attention(attns[1], attns[1].last + attns[1].tail)

        @block.scalar
        def _(act):
            def copy(dst, src):
                return nc.scalar.activation(dst, src, ACT.Copy)

            def layer_norm(q):
                for g in range(TILES // 2):
                    q.tp.wait_full(act, g)
                    copy(xnT[:, :, 2 * g:2 * g + 2, :].rearrange("p k u t -> p u k t"),
                         q.tp.bank(g)[:, :].rearrange("p (u k t) -> p u k t", u=2, k=KD)).then_inc(q.tp.free["act"], 1)

            def attention(a, steps):
                for kind, w in steps:
                    if kind == "choose":
                        act.wait_ge(norms[a.n].expin, 1)
                        sc = (sc0, sc1)[a.n]
                        nc.scalar.activation(sc[:, 1, :], sc[:, 0, :], ACT.Exp).then_inc(norms[a.n].expd, 1)
                    elif kind == "part":
                        i, g = w
                        b, half = divmod(i, HALVES)
                        if b >= 2:
                            unit = 2 * g + 1 if g < a.maps // 8 else a.units - 1
                            act.wait_ge(a.st.full, a.st.at[(b - 2, unit, 2)] + 1)
                        key = ("t", i, g)
                        a.pj.wait_full(act, key)
                        copy(qkT[0:STACK, b % 2, 8 * g:8 * g + 8, half * P:half * P + P],
                             bfv(a.pj.bank(key))[0:STACK, :, :]).then_inc(a.pj.free["act"], 1)
                    elif kind == "rows":
                        b = w // HALVES
                        if w >= 2:
                            for p in range(2):
                                done = [i for i in range(w - 1) if (i // HALVES) % 2 == p]
                                if done:
                                    act.wait_ge(a.rows[p], 16 * PARTS * len(done))
                        a.po.wait_full(act, ("rows", w))
                        n = PARTS * a.maps
                        copy(nT[0:n, w % 2, :], bfv(a.po.bank(("rows", w)))[0:n, 0, :]).then_inc(a.po.free["act"], 1)
                    elif kind == "exp":
                        for u in range(3):
                            key = (*w, u)
                            at = a.st.at[key]
                            if at >= 6:
                                a.po.wait_full(act, divmod(at // 3 - 2, a.units))
                            a.st.wait_full(act, key)
                            nc.scalar.activation(pT[at % 6], a.st.bank(key)[:, :], ACT.Exp, scale=SCALE)\
                                .then_inc(a.st.free["act"], 1)
                    elif kind == "value":
                        b, j = w
                        if b >= 1:
                            act.wait_ge(a.onorm, HALVES * b)
                        a.po.wait_full(act, w)
                        n = a.vw + 1
                        copy(raw_of(a)[:, :, 4 * j:4 * j + 4, :],
                             a.po.bank(w)[:, 0:HALVES * 4 * n].rearrange("p (h m w) -> p h m w", h=HALVES, w=n))\
                            .then_inc(a.po.free["act"], 1)
                    elif kind == "mean":
                        act.wait_ge(norms[0].routed, 1)
                        act.wait_ge(*a.pj.emptied(("mean", w)))
                        nc.scalar.activation(squares, o_d.rearrange("p h n -> p (h n)"), ACT.Square)\
                            .then_inc(a.squared, 1)
                    elif kind == "out" and a.n == 0:
                        a.pj.wait_full(act, ("o", w))
                        if w == 0:
                            act.wait_ge(sent0, 16 * TOP * TILES)
                        copy(xres[:, w, :], a.pj.bank(("o", w))[:, 0:D]).then_inc(a.pj.free["act"], 1)
                    elif kind == "turn":
                        if w:
                            a.pj.wait_full(act, ("o", w - 1))
                        a.pj.wait_full(act, ("z", w))
                        turned = a.pj.bank(("z", w))[:, 0:a.zchunks * P].rearrange("p (c t) -> p c t", t=P)
                        if a.n == 1:
                            copy(zT[:, 0:a.zchunks, :], turned).then_inc(a.pj.free["act"], 1)
                            continue
                        act.wait_ge(a.scaled, w // HALVES + 1)
                        for c in range(a.zchunks):
                            last = nc.scalar.activation(zT[:, c, :], turned[:, c, :], ACT.Identity,
                                                        scale=gn_scale[:, c:c + 1], bias=gn[:, 1, c:c + 1])
                        last.then_inc(a.pj.free["act"], 1)

            layer_norm(norms[0])
            act.wait_ge(s_lamx, 1)
            nc.scalar.activation(lamx, lam2, ACT.Exp).then_inc(s_lame, 1)
            attention(attns[0], attns[0].steps)

            def rows_turned(n):
                m0.xt.wait_full(act, n)
                if n >= 2:
                    m0.up.wait_full(act, n - 2)
                copy(xsT[:, n % 2, :, :], m0.xt.bank(n)[:, 0:KD * P].rearrange("p (k t) -> p k t", t=P))\
                    .then_inc(m0.xt.free["act"], 1)

            rows_turned(0)
            for n in range(N0 + 4):
                for i in back_at(n, 1):
                    act.wait_ge(m0.sum, i + 1)
                    nc.scalar.activation(gval[:, i, :], acc[:, i, :], ACT.Silu).then_inc(m0.g, 1)
                if n > N0:
                    continue
                attention(attns[0], beside_experts(attns[0], n))
                if n + 1 < SLOT_TILES0:
                    rows_turned(n + 1)
                if n < N0:
                    m0.up.wait_full(act, n)
                    if n >= 2:
                        act.wait_ge(*m0.up.emptied(n - 2))
                    nc.scalar.activation(silu_a[:, n % 2, :], m0.up.bank(n)[:, 0:F0], ACT.Silu).then_inc(m0.silu, 1)
                if n:
                    m0.ht.wait_full(act, n - 1)
                    if n >= 3:
                        m0.dn.wait_full(act, n - 3)
                    copy(hidT[0:FH, (n - 1) % 2, :, :], m0.ht.bank(n - 1)[0:FH, 0:2 * P]
                         .rearrange("p (f t) -> p f t", t=P)).then_inc(m0.ht.free["act"], 1)
            layer_norm(norms[1])
            attention(attns[1], attns[1].steps)
            for g in range(SLOT_TILES1 // 2):
                m1.xt.wait_full(act, g)
                copy(xs1T[:, :, 2 * g * P:2 * (g + 1) * P], m1.xt.bank(g)[:, :].rearrange("p (k t) -> p k t", k=KD))\
                    .then_inc(m1.xt.free["act"], 1)
            for e in range(E1):
                m1.up.wait_full(act, e)
                m1.xt.wait_full(act, SLOT_TILES1 // 2 - 1)
                nc.scalar.activation(gelT[:, e, :, :], m1.up.bank(e)[:, 0:F1 // P * CAPACITY]
                                     .rearrange("p (m t) -> p m t", t=CAPACITY), ACT.Gelu).then_inc(m1.up.free["act"], 1)
            attention(attns[1], attns[1].last)
            for i in range(TILES):
                act.wait_ge(back1[i], 16)
                nc.scalar.activation(y_back1[:, i, :], y_back1[:, i, :], ACT.Silu, scale=weight1[:, i:i + 1])\
                    .then_inc(m1.g, 1)
            attention(attns[1], attns[1].tail)

        @block.gpsimd
        def _(pool):
            nc.gpsimd.memset(zeros, 0.0).then_inc(zeroed, 1)
            nc.gpsimd.memset(ones[:, :], 1.0).then_inc(s_ones, 1)
            nc.gpsimd.memset(minus_half16, -0.5).then_inc(s_ones, 1)
            nc.gpsimd.memset(head_mean[:, :], 1.0 / (SEQ * 2 * DH)).then_inc(s_ones, 1)
            pool.wait_ge(s_ones, 3)
            zero_fill = pool.to_reg(0.0)

            def power(ready, n, done, count, dst, src, width):
                pool.wait_ge(ready, n)
                nc.gpsimd.tensor_tensor(dst, src, minus_half16[:, 0:width], ALU.pow).then_inc(done, 1)
                pool.wait_ge(done, count)

            def ones_beside(a):
                nc.gpsimd.memset(qkT[STACK:P, :, a.maps:a.groups, :], 1.0).then_inc(a.ones, 1)
                pool.wait_ge(a.ones, 1)
                for b in range(3):
                    for half in range(HALVES):
                        nc.gpsimd.memset(vaug_of(a, b)[:, half, :, a.vw:a.vw + 1], 1.0).then_inc(a.ones, 1)
                pool.wait_ge(a.ones, 1 + 3 * HALVES)

            def attention(a, steps):
                for kind, w in steps:
                    if kind == "variance":
                        power(*a.pj.emptied((kind, w)), a.gpow, w + 1, gn_rs, gn_ve, 16)
                    elif kind == "exp":
                        for u in range(3):
                            key = (*w, u)
                            maps, n = (2, SEQ) if u < 2 else (4, P)
                            pool.wait_ge(*a.st.emptied(key))
                            probs = pT[a.st.at[key] % 6].rearrange("p (m t) -> p m t", t=n)[:, :, 0:P]
                            nc.gpsimd.affine_select(probs, probs, [[0, maps], [1, P]], ALU.is_ge, zero_fill, base=0,
                                                    channel_multiplier=-1).then_inc(a.cut, 1)
                        pool.wait_ge(a.cut, a.st.at[key] + 1)
                    elif kind == "send" and a.n == 0:
                        for c in range(TOP):
                            send(x0_slots_d, slot0[:, w, c:c + 1], xn[:, w, :], sent0)
                    elif kind == "send":
                        send(x1_slots_d, slot1_in[:, w:w + 1], xn1[:, w, :], sent1)
                    elif kind == "ranks":
                        pool.wait_ge(filled, 16 * (SLOT_TILES0 + SLOT_TILES1))
                        pool.wait_ge(norms[a.n].routed, 1)

            def send(slots_d, slot, src, done):
                nc.gpsimd.indirect_dma_start(slots_d, bass.IndirectOffsetOnAxis(ap=slot, axis=0), src, None)\
                    .then_inc(done, 16)

            def fetch(slots_d, slot, dst, done):
                nc.gpsimd.indirect_dma_start(dst, None, slots_d, bass.IndirectOffsetOnAxis(ap=slot, axis=0))\
                    .then_inc(done, 16)

            def layer_norm(q):
                for g in range(2):
                    power(q.veps, g + 1, q.pow, g + 1, rstd[:, 4 * g:4 * g + 4], veps[:, 4 * g:4 * g + 4], 4)

            layer_norm(norms[0])
            ones_beside(attns[0])
            attention(attns[0], attns[0].steps + attns[0].tail)
            for k in range(4):
                pool.wait_ge(ys_stored[k], 16 * len(range(k, SLOT_TILES0, 4)))
            for i in range(TILES):
                for c in range(TOP):
                    fetch(y0_slots_d, slot0[:, i, c:c + 1], y_back[:, i, c, :], back0[i])
            layer_norm(norms[1])
            pool.wait_ge(norms[1].xn, TILES)
            ones_beside(attns[1])
            attention(attns[1], attns[1].steps + attns[1].last)
            for k in range(2):
                pool.wait_ge(ys1_stored[k], 16 * E1)
            for i in range(TILES):
                fetch(y1_slots_d, slot1_out[:, i:i + 1], y_back1[:, i, :], back1[i])

        @block.vector
        def _(dve):
            chain = [0]

            def link(ins):
                chain[0] += 1
                ins.then_inc(dve_c, 1)
                dve.wait_ge(dve_c, chain[0])

            def newton(y, v, t):
                link(nc.vector.tensor_tensor(t, y, y, ALU.mult))
                link(nc.vector.tensor_tensor(t, t, v, ALU.mult))
                link(nc.vector.tensor_scalar(t, t, -0.5, 1.5, ALU.mult, ALU.add))
                link(nc.vector.tensor_tensor(y, y, t, ALU.mult))

            def statistics(q, x_t, i):
                link(nc.vector.bn_stats(stats[:, i, :], x_t[:, i, :]))
                link(nc.vector.bn_aggr(mv[:, i, :], stats[:, i, :]))
                if i % 4 == 3:
                    nc.vector.tensor_scalar(veps[:, i - 3:i + 1], mv[:, i - 3:i + 1, 1], EPS, None, ALU.add)\
                        .then_inc(q.veps, 1)

            def normalize(q, x_t, xn_t, halves=(0, 1)):
                for g in halves:
                    group = slice(4 * g, 4 * g + 4)
                    dve.wait_ge(q.pow, g + 1)
                    newton(rstd[:, group], veps[:, group], tmp8[:, group])
                    for i in range(4 * g, 4 * g + 4):
                        nc.vector.tensor_scalar(xn_t[:, i, :], x_t[:, i, :], mv[:, i, 0:1], rstd[:, i:i + 1],
                                                ALU.subtract, ALU.mult).then_inc(q.xn, 1)

            def router_views(n):
                experts, sc = ((E0, sc0), (E1, sc1))[n]

                def v(k):
                    return sc[:, k, :].rearrange("p (t e) -> p t e", e=experts)

                def over(x):
                    return x.unsqueeze(2).to_broadcast([P, TILES, experts])

                return v, over

            def logits(a):
                v, over = router_views(a.n)
                key, sc = ("logits", a.n), (sc0, sc1)[a.n]
                a.pj.wait_full(dve, key)
                nc.vector.tensor_copy(sc[:, 2, :], a.pj.bank(key)[:, 0:sc.shape[2]]).then_inc(a.pj.free["dve"], 1)
                dve.wait_ge(*a.pj.emptied(key))
                link(nc.vector.tensor_reduce(r8a, v(2), AX_X, ALU.max))
                nc.vector.tensor_tensor(v(0), v(2), over(r8a), ALU.subtract).then_inc(norms[a.n].expin, 1)

            def softmax(q, v, over):
                dve.wait_ge(q.expd, 1)
                link(nc.vector.tensor_reduce(r8b, v(1), AX_X, ALU.add))
                link(nc.vector.reciprocal(r8b, r8b))
                link(nc.vector.tensor_tensor(v(1), v(1), over(r8b), ALU.mult))

            def first_largest(v, over, experts, src, dst):
                link(nc.vector.tensor_reduce(r8a, src, AX_X, ALU.max))
                link(nc.vector.tensor_tensor(dst, src, over(r8a), ALU.is_ge))
                count = iota[:, 0:experts].unsqueeze(1).to_broadcast([P, TILES, experts])
                link(nc.vector.tensor_tensor(dst, dst, count, ALU.mult))
                link(nc.vector.tensor_reduce(r8a, dst, AX_X, ALU.max))
                link(nc.vector.tensor_tensor(dst, dst, over(r8a), ALU.is_ge))

            def rotated(a, i):
                b, half = divmod(i, HALVES)
                cos, sin = rope_tables(a, half)
                nq = 32 if a.n == 0 else 32

                def rotate(src, g0, g1):
                    n = g1 - g0
                    nc.vector.tensor_tensor(rot_a[:, g0:g1, :], src, cos.unsqueeze(1).to_broadcast([P, n, DH]), ALU.mult)
                    h = DH // 2
                    nc.vector.tensor_tensor(rot_b[:, g0:g1, 0:h], src[:, :, h:DH],
                                            sin[:, 0:h].unsqueeze(1).to_broadcast([P, n, h]), ALU.mult)
                    return nc.vector.tensor_tensor(rot_b[:, g0:g1, h:DH], src[:, :, 0:h],
                                                   sin[:, h:DH].unsqueeze(1).to_broadcast([P, n, h]), ALU.mult)

                a.pj.wait_full(dve, ("q", i))
                first = a.pj.bank(("q", i))[:, :].rearrange("p (g d) -> p g d", d=DH)
                if a.n == 0:
                    rotate(first, 0, nq).then_inc(a.pj.free["dve"], 1)
                else:
                    nc.vector.tensor_tensor(rot_x, first, bqkv[:, 0:512].rearrange("p (g d) -> p g d", d=DH), ALU.add)\
                        .then_inc(a.pj.free["dve"], 1)
                    dve.wait_ge(*a.pj.emptied(("q", i)))
                    link(rotate(rot_x, 0, nq))
                a.pj.wait_full(dve, ("kv", i))
                second = a.pj.bank(("kv", i))
                v0 = 2 * D // 4 if a.n == 0 else 0
                if a.n == 0:
                    rotate(second[:, 0:v0].rearrange("p (g d) -> p g d", d=DH), nq, a.groups)
                vals = second[:, v0:v0 + a.vheads * a.vw].rearrange("p (v w) -> p v w", w=a.vw)
                if b >= 3:
                    a.po.wait_full(dve, (b - 3, a.units - 1))
                dst = vaug_of(a, b)[:, half, :, 0:a.vw]
                if a.n == 0:
                    nc.vector.tensor_copy(dst, vals).then_inc(a.pj.free["dve"], 1)
                else:
                    nc.vector.tensor_tensor(dst, vals, bqkv[:, 512:768].rearrange("p (v w) -> p v w", w=a.vw), ALU.add)\
                        .then_inc(a.pj.free["dve"], 1)
                dve.wait_ge(*a.pj.emptied(("kv", i)))
                ng, m = a.groups, a.maps
                link(nc.vector.tensor_tensor(rot_a[:, 0:ng, :], rot_a[:, 0:ng, :], rot_b[:, 0:ng, :], ALU.add))
                if i:
                    a.pj.wait_full(dve, ("t", i - 1, (a.order if i % 2 == 0 else a.order0)[-1]))
                link(nc.vector.tensor_copy(stack[:, 0:ng, 0, :], rot_a[:, 0:ng, :]))
                link(nc.vector.tensor_tensor(rot_a[:, 0:ng, :], rot_a[:, 0:ng, :], stack[:, 0:ng, 0, :], ALU.subtract))
                nc.vector.tensor_copy(stack[:, 0:m, 1:3, :], stack[:, 0:m, 0:1, :].to_broadcast([P, m, 2, DH]))
                link(nc.vector.tensor_copy(stack[:, 0:ng, 4, :], rot_a[:, 0:ng, :]))
                nc.vector.tensor_copy(stack[:, m:ng, 3, :], stack[:, m:ng, 0, :])
                nc.vector.tensor_copy(stack[:, m:ng, 5, :], stack[:, m:ng, 0, :])
                nc.vector.tensor_copy(stack[:, 0:m, 3, :], stack[:, 0:m, 4, :])
                nc.vector.tensor_copy(stack[:, m:ng, 1, :], stack[:, m:ng, 4, :])
                nc.vector.tensor_tensor(stack[:, 0:m, 5, :], rot_a[:, 0:m, :], stack[:, 0:m, 4, :], ALU.subtract)
                nc.vector.tensor_tensor(stack[:, m:ng, 2, :], rot_a[:, m:ng, :], stack[:, m:ng, 4, :], ALU.subtract)\
                    .then_inc(a.stacked, 1)

            def row_max(a, b, q):
                half, ms = max_use(a, q)
                a.s.wait_full(dve, (b, q))
                n = P * (half + 1)
                nc.vector.tensor_reduce(nmax[:, ms[0]:ms[-1] + 1], a.s.bank((b, q))[:, :].rearrange("p (m s) -> p m s", s=n),
                                        AX_X, ALU.max, negate=True).then_inc(a.s.free["dve"], 1)
                last = a.units - 1 if half == 0 else 3 * a.units - 1
                if q != last:
                    return
                i = 2 * b + half
                m = a.maps
                dve.wait_ge(*a.s.emptied((b, q)))
                if i >= 2:
                    a.po.wait_full(dve, ("rows", i - 2))
                parts = nparts[:, i % 2, 0:PARTS * m].rearrange("p (k m) -> p k m", m=m)
                link(nc.vector.tensor_copy(parts[:, 0, :], nmax[:, 0:m]))
                link(nc.vector.tensor_tensor(nmax_r[:, 0:m], nmax[:, 0:m], parts[:, 0, :], ALU.subtract))
                link(nc.vector.tensor_copy(parts[:, 1, :], nmax_r[:, 0:m]))
                nc.vector.tensor_tensor(parts[:, 2, :], nmax_r[:, 0:m], parts[:, 1, :], ALU.subtract)\
                    .then_inc(a.nmax, 1)

            def divide(a, i):
                b, half = divmod(i, HALVES)
                raw = raw_of(a)[:, half]
                m = a.maps
                dve.wait_ge(*a.po.emptied((b, a.units - 1)))
                link(nc.vector.reciprocal(rsum[:, 0:m].unsqueeze(2), raw[:, :, a.vw:a.vw + 1]))
                bc = rsum[:, 0:m].unsqueeze(2).to_broadcast([P, m, a.vw])
                if i >= 2:
                    a.pj.wait_full(dve, ("z", i - 2))
                if a.n == 1:
                    nc.vector.tensor_tensor(o_d[:, half, 0:D].rearrange("p (m w) -> p m w", w=a.vw), raw[:, :, 0:a.vw],
                                            bc, ALU.mult).then_inc(a.z, 1)
                    dve.wait_ge(a.z, i + 1)
                    return
                second = rsum[:, :].rearrange("p (v c r) -> p v c r", c=2, r=4)[:, :, 1, :]
                link(nc.vector.tensor_scalar(second, second, lam, None, ALU.mult))
                nc.vector.tensor_tensor(o_n, raw[:, :, 0:a.vw], bc, ALU.mult).then_inc(a.onorm, 1)
                dve.wait_ge(a.onorm, i + 1)
                maps = o_n.rearrange("p (v c r) w -> p v c (r w)", c=2, r=4)
                link(nc.vector.tensor_tensor(o_d[:, half, :].rearrange("p (v n) -> p v n", v=4), maps[:, :, 0],
                                             maps[:, :, 1], ALU.subtract))
                if half == HALVES - 1:
                    nc.vector.tensor_reduce(gn_sum, o_d.rearrange("p h (m w) -> p (h m) w", w=32), AX_X, ALU.add)\
                        .then_inc(a.sums, 1)

            def by_head(x):
                return x.unsqueeze(1).unsqueeze(3).to_broadcast([P, HALVES, 16, 32])

            o_heads = o_d.rearrange("p h (m w) -> p h m w", w=32)

            def center(a, b):
                a.pj.wait_full(dve, ("mean", b))
                nc.vector.tensor_tensor(o_heads, o_heads, by_head(a.pj.bank(("mean", b))[:, 0:16]), ALU.subtract)\
                    .then_inc(a.pj.free["dve"], 1)

            def sum_squares(a, b):
                dve.wait_ge(a.squared, b + 1)
                a.pj.wait_full(dve, ("mean", b))
                nc.vector.tensor_reduce(gn_sum, squares.rearrange("p (m w) -> p m w", w=32), AX_X, ALU.add)\
                    .then_inc(a.sums, 1)

            def variance(a, b):
                a.pj.wait_full(dve, ("variance", b))
                nc.vector.tensor_scalar(gn_ve, a.pj.bank(("variance", b))[:, 0:16], EPS, None, ALU.add)\
                    .then_inc(a.pj.free["dve"], 1)

            def scale(a, b):
                dve.wait_ge(*a.pj.emptied(("variance", b)))
                dve.wait_ge(a.gpow, b + 1)
                newton(gn_rs, gn_ve, gn_t)
                mine = cst[:, C_HEAD:C_HEAD + HEADS_TALL].unsqueeze(1).to_broadcast([P, 4, HEADS_TALL])
                by_chunk = gn_t.rearrange("p (c k) -> p c k", k=HEADS_TALL)
                link(nc.vector.tensor_tensor(by_chunk, gn_rs.rearrange("p (c k) -> p c k", k=HEADS_TALL), mine, ALU.mult))
                if b == 0:
                    dve.wait_ge(ld["gn"], 16)
                if b:
                    dve.wait_ge(*a.pj.emptied(("z", 2 * b - 1)))
                link(nc.vector.tensor_reduce(gn_scale, by_chunk, AX_X, ALU.add))
                nc.vector.tensor_tensor(gn_scale, gn_scale, gn[:, 0, :], ALU.mult).then_inc(a.scaled, 1)
                dve.wait_ge(a.scaled, b + 1)

            def choose0():
                v, over = router_views(0)
                softmax(norms[0], v, over)
                first_largest(v, over, E0, v(1), v(3))
                link(nc.vector.scalar_tensor_tensor(out=v(4), in0=v(3), scalar=-2.0, in1=v(1), op0=ALU.mult, op1=ALU.add))
                first_largest(v, over, E0, v(4), v(0))
                nc.vector.tensor_tensor(hot_of(0), sc0[:, 3, :], sc0[:, 0, :], ALU.add).then_inc(norms[0].hot, 1)
                for c, one_hot in enumerate((v(3), v(0))):
                    link(nc.vector.tensor_tensor(v(4), one_hot, v(1), ALU.mult))
                    link(nc.vector.tensor_reduce(weight0[:, :, c], v(4), AX_X, ALU.add))

            def slots0(a):
                v, over = router_views(0)
                key = ("ranks", 0)
                a.pj.wait_full(dve, key)
                counts = a.pj.bank(key)
                dve.wait_ge(ld["tables"], 16)
                def table(at, n):
                    return tables[:, at - C_TABLES:at - C_TABLES + n]
                def cells(a, b):
                    return tally[:, 0:a * b].rearrange("p (a b) -> p a b", b=b)
                n_tiles, first, ends = r16[:, 0, :], r16[:, 1, :], r16[:, 2, :]
                total = counts[:, TILES * E0:(TILES + 1) * E0]
                link(nc.vector.tensor_copy(ends, total))
                link(nc.vector.tensor_tensor(cells(E0, TILES), ends.unsqueeze(2).to_broadcast([P, E0, TILES]),
                                             table(C_FILLED, TILES).unsqueeze(1).to_broadcast([P, E0, TILES]), ALU.is_gt))
                link(nc.vector.tensor_reduce(n_tiles, cells(E0, TILES), AX_X, ALU.add))
                link(nc.vector.tensor_tensor(cells(E0, E0), table(C_BEFORE, E0 * E0).rearrange("p (a b) -> p a b", b=E0),
                                             n_tiles.unsqueeze(1).to_broadcast([P, E0, E0]), ALU.mult))
                link(nc.vector.tensor_reduce(first, cells(E0, E0), AX_X, ALU.add))
                link(nc.vector.tensor_tensor(ends, first, n_tiles, ALU.add))
                link(nc.vector.tensor_scalar(first, first, float(P), -1.0, ALU.mult, ALU.add))
                link(nc.vector.tensor_tensor(cells(SLOT_TILES0, E0),
                                             table(C_TILE, SLOT_TILES0).unsqueeze(2).to_broadcast([P, SLOT_TILES0, E0]),
                                             ends.unsqueeze(1).to_broadcast([P, SLOT_TILES0, E0]), ALU.is_ge))
                link(nc.vector.tensor_reduce(r32[:, 0:SLOT_TILES0], cells(SLOT_TILES0, E0), AX_X, ALU.add))
                link(nc.vector.tensor_scalar(tile_expert[:, :], r32[:, 0:SLOT_TILES0], E0 - 1.0, None, ALU.min))
                rank = counts[:, 0:TILES * E0].rearrange("p (t e) -> p t e", e=E0)
                nc.vector.tensor_tensor(v(2), rank, first.unsqueeze(1).to_broadcast([P, TILES, E0]), ALU.add)\
                    .then_inc(a.pj.free["dve"], 1)
                dve.wait_ge(*a.pj.emptied(key))
                for c, one_hot in enumerate((v(3), v(0))):
                    link(nc.vector.tensor_tensor(v(4), one_hot, v(2), ALU.mult))
                    link(nc.vector.tensor_reduce(r8a, v(4), AX_X, ALU.add))
                    last = nc.vector.tensor_copy(slot0[:, :, c], r8a)
                    if c == 0:
                        link(last)
                last.then_inc(norms[0].routed, 1)

            def choose1():
                v, over = router_views(1)
                softmax(norms[1], v, over)
                first_largest(v, over, E1, v(2), v(3))
                nc.vector.tensor_copy(hot_of(1), sc1[:, 3, :]).then_inc(norms[1].hot, 1)

            def slots1(a):
                v, over = router_views(1)
                key = ("ranks", 1)
                a.pj.wait_full(dve, key)
                counts = a.pj.bank(key)
                kept = r8b
                link(nc.vector.tensor_scalar(sc1[:, 4, :], counts[:, 0:TILES * E1], CAPACITY + 0.5, None, ALU.is_lt))
                link(nc.vector.tensor_tensor(v(4), v(3), v(4), ALU.mult))
                link(nc.vector.tensor_reduce(kept, v(4), AX_X, ALU.add))
                link(nc.vector.tensor_tensor(v(1), v(4), v(1), ALU.mult))
                link(nc.vector.tensor_reduce(weight1[:, :], v(1), AX_X, ALU.add))
                rank = counts[:, 0:TILES * E1].rearrange("p (t e) -> p t e", e=E1)
                nc.vector.tensor_tensor(v(2), rank, cst[:, C_SLOT1:C_SLOT1 + E1].unsqueeze(1).to_broadcast([P, TILES, E1]),
                                        ALU.add).then_inc(a.pj.free["dve"], 1)
                dve.wait_ge(*a.pj.emptied(key))
                link(nc.vector.tensor_tensor(v(2), v(2), v(4), ALU.mult))
                link(nc.vector.tensor_reduce(r8a, v(2), AX_X, ALU.add))
                link(nc.vector.tensor_copy(slot1_out[:, :], r8a))
                link(nc.vector.tensor_scalar(kept, kept, -1.0, 1.0, ALU.mult, ALU.add))
                link(nc.vector.tensor_tensor(kept, kept, cst[:, C_SPARE:C_SPARE + TILES], ALU.mult))
                nc.vector.tensor_tensor(slot1_in[:, :], r8a, kept, ALU.add).then_inc(norms[1].routed, 1)

            def rows_out(e):
                for c, (at, n) in enumerate(DN1):
                    m1.dn.wait_full(dve, (e, c))
                    if e >= 2:
                        dve.wait_ge(ys1_stored[e % 2], 32 * (e // 2))
                    nc.vector.tensor_copy(ys1[0:n, e % 2, c, :], m1.dn.bank((e, c))[0:n, 0:D]).then_inc(m1.dn.free["dve"], 1)

            def attention(a, steps):
                for kind, w in steps:
                    if kind == "down":
                        rows_out(w)
                    elif kind == "rotate":
                        rotated(a, w)
                    elif kind == "max":
                        row_max(a, *w)
                    elif kind == "divide":
                        divide(a, w)
                    elif kind == "logits":
                        logits(a)
                    elif kind == "choose":
                        (choose0, choose1)[w]()
                    elif kind == "ranks":
                        (slots0, slots1)[w](a)
                    elif kind == "mean":
                        center(a, w)
                    elif kind == "squares":
                        sum_squares(a, w)
                    elif kind == "variance":
                        variance(a, w)
                    elif kind == "scale":
                        scale(a, w)
                    elif kind == "out" and a.n == 1:
                        a.pj.wait_full(dve, ("o", w))
                        nc.vector.tensor_tensor(s1[:, w, :], a.pj.bank(("o", w))[:, 0:D], bo, ALU.add)\
                            .then_inc(a.pj.free["dve"], 1)

            for i in range(TILES):
                if i % 4 == 0:
                    dve.wait_ge(x_here[i // 4], 16)
                statistics(norms[0], x_in, i)
            dve.wait_ge(ld["cst"], 32)
            nc.vector.tensor_copy(identb[:, :], ident).then_inc(s_cast, 1)
            for dst, at in ((neg_ts, C_NEG1), (triu, C_TRIU)):
                nc.vector.tensor_copy(dst[:, :], masks[:, at - C_KEPT:at - C_KEPT + P]).then_inc(s_cast, 1)
            normalize(norms[0], x_in, xn)

            dve.wait_ge(ld["lam"], 16)
            link(nc.vector.tensor_tensor(lamv[:, 0::2, :], lamv[:, 0::2, :], lamv[:, 1::2, :], ALU.mult))
            nc.vector.tensor_reduce(lam2, lamv[:, 0::2, :], AX_X, ALU.add).then_inc(s_lamx, 1)

            dve.wait_ge(s_lame, 1)
            link(nc.vector.tensor_tensor(lam, lamx[:, 0:1], lamx[:, 1:2], ALU.subtract))
            link(nc.vector.tensor_scalar(lam, lam, LAMBDA_INIT, None, ALU.add))
            attention(attns[0], attns[0].steps)

            def gated(m, scale, gval, base):
                def one(i):
                    dve.wait_ge(m.g, i + 1)
                    src, add = base(i)
                    link(nc.vector.scalar_tensor_tensor(out=gval[:, i, :], in0=src, scalar=scale, in1=gval[:, i, :],
                                                        op0=ALU.mult, op1=ALU.mult))
                    nc.vector.tensor_tensor(xres[:, i, :], gval[:, i, :], add, ALU.add).then_inc(m.x, 1)
                    dve.wait_ge(m.x, i + 1)
                return one

            def combine(t):
                dve.wait_ge(back0[t], 16 * TOP)
                dve.wait_ge(*m0.dn.emptied(SLOT_TILES0 + SHARED * t + 1))
                for c in range(TOP):
                    out = nc.vector.scalar_tensor_tensor(out=acc[:, t, :], in0=y_back[:, t, c, :], scalar=weight0[:, t, c:c + 1],
                                                         in1=acc[:, t, :], op0=ALU.mult, op1=ALU.add)
                    if c == 0:
                        link(out)
                out.then_inc(m0.sum, 1)

            one = gated(m0, 1.0 - LAMBDA_INIT, gval, lambda i: (xres[:, i, :], x_again[:, i, :]))
            for n in range(N0 + 5):
                attention(attns[0], beside_experts(attns[0], n))
                for t in back_at(n, 0):
                    combine(t)
                for i in back_at(n, 2):
                    if i == 0:
                        dve.wait_ge(ld["x2"], 16)
                    one(i)
                    statistics(norms[1], xres, i)
                    if i == TILES - 3:
                        normalize(norms[1], xres, xn1, (0,))
                if n < N0:
                    if n >= 2:
                        m0.ht.wait_full(dve, n - 2)
                    dve.wait_ge(m0.silu, n + 1)
                    nc.vector.tensor_tensor(hid[:, n % 2, :], silu_a[:, n % 2, :], m0.up.bank(n)[:, F0:2 * F0], ALU.mult)\
                        .then_inc(m0.up.free["dve"], 1)
                if 2 <= n < N0 + 2:
                    j = n - 2
                    m0.dn.wait_full(dve, j)
                    src = m0.dn.bank(j)[:, 0:D]
                    if j < SLOT_TILES0:
                        if j >= 4:
                            dve.wait_ge(ys_stored[j % 4], 16 * (j // 4))
                        nc.vector.tensor_copy(ys[:, j % 4, :], src).then_inc(m0.dn.free["dve"], 1)
                    else:
                        t, part = divmod(j - SLOT_TILES0, SHARED)
                        if part == 0:
                            nc.vector.tensor_copy(acc[:, t, :], src).then_inc(m0.dn.free["dve"], 1)
                        else:
                            dve.wait_ge(*m0.dn.emptied(j - 1))
                            nc.vector.tensor_tensor(acc[:, t, :], src, acc[:, t, :], ALU.add).then_inc(m0.dn.free["dve"], 1)
            normalize(norms[1], xres, xn1, (1,))
            dve.wait_ge(ld["bias"], 32)
            attention(attns[1], attns[1].steps)
            attention(attns[1], attns[1].last + attns[1].tail[:HALVES])
            one = gated(m1, 1.0, y_back1, lambda i: (s1[:, i, :], xres[:, i, :]))
            for i in range(TILES - HALVES):
                one(i)
            attention(attns[1], attns[1].tail[HALVES:])
            for i in range(TILES - HALVES, TILES):
                one(i)


def kernel(**inputs):
    import concourse.bacc as bacc
    from concourse.bass_utils import run_bass_kernel_spmd as run

    def f(name):
        return np.asarray(inputs[name])

    def kt(a, parts=P):
        return a.reshape(a.shape[0] // parts, parts, a.shape[1]).transpose(1, 0, 2)

    H, KV = 16, 4
    rep = H // KV
    even_odd = np.concatenate([np.arange(0, DH, 2), np.arange(1, DH, 2)])
    wq = f("L0_attn_Wq").reshape(D, KV, rep, 2, DH)[..., even_odd].transpose(0, 1, 3, 2, 4).reshape(D, 2 * D)
    wk = f("L0_attn_Wk").reshape(D, KV, 2, DH)[..., even_odd].reshape(D, D // 2)
    w1, w3, w2 = f("L0_ffn_w1"), f("L0_ffn_w3"), f("L0_ffn_w2")
    up = np.concatenate([w1, w3], axis=1)
    down = w2.transpose(0, 2, 1)
    sw1, sw3, sw2 = (f("L0_ffn_" + n) for n in ("sw1", "sw3", "sw2"))
    sup = np.concatenate([sw1.reshape(SHARED, F0, D), sw3.reshape(SHARED, F0, D)], axis=1)
    sdown = sw2.T.reshape(SHARED, F0, D)
    up = np.concatenate([up, sup]).transpose(0, 2, 1).reshape(EXPERTS0, KD, P, 2 * F0).transpose(2, 0, 1, 3)
    down = np.concatenate([down, sdown]).reshape(EXPERTS0, 2, FH, D).transpose(2, 0, 1, 3)
    arrays = {
        "x": f("L0_attn_x").reshape(-1, D),
        "consts": constants(),
        "wqkv0": kt(np.concatenate([wq, wk, f("L0_attn_Wv")], axis=1)),
        "wo0": kt(f("L0_attn_Wo")),
        "lam": np.stack([f("L0_attn_lambda_" + n) for n in ("q1", "k1", "q2", "k2")]),
        "gn": np.stack([f("L0_attn_gn_w"), f("L0_attn_gn_b")]).reshape(2, 4, P).transpose(2, 0, 1),
        "gate0": kt(f("L0_ffn_gate_w").T),
        "w13": up,
        "w2": down,
        "wqkv1": kt(f("L1_attn_Wqkv").T),
        "bqkv": f("L1_attn_bqkv"),
        "wo1": kt(f("L1_attn_Wo").T),
        "bo": f("L1_attn_bo"),
        "gate1": kt(f("L1_ffn_gate_weight").T),
        "f1a": f("L1_ffn_w1").reshape(E1, KD, P, F1).transpose(2, 0, 1, 3),
        "f1b": f("L1_ffn_w2").reshape(E1, F1 // P, P, D).transpose(2, 0, 1, 3),
    }
    arrays = {n + "_in": np.ascontiguousarray(a) for n, a in arrays.items()}
    nc = bacc.Bacc("TRN2", target_bir_lowering=False, num_devices=1)
    args = [nc.dram_tensor(n, a.shape, F32, kind="ExternalInput").ap() for n, a in arrays.items()]
    out = nc.dram_tensor("out", (BATCH * SEQ, D), F32, kind="ExternalOutput").ap()
    slots = [nc.dram_tensor(n, (rows, D), F32, kind="Internal").ap()
             for n, rows in (("x0_slots", SLOT_TILES0 * P), ("y0_slots", SLOT_TILES0 * P),
                             ("x1_slots", SLOTS1 + TOKENS), ("y1_slots", SLOTS1))]
    program(nc, *args, out, *slots)
    r = run(nc, [arrays], core_ids=[0])
    return r.results[0]["out"].reshape(BATCH, SEQ, D)
```
